# Optimizing a Trainium2 kernel written in Bass

```python
import numpy as np
import jax
import jax.numpy as jnp

def _softmax(x, axis=-1):
    return jax.nn.softmax(x, axis=axis)

def _gelu(x):
    return jax.nn.gelu(x, approximate=True)

def _silu(x):
    return jax.nn.silu(x)

def _sigmoid(x):
    return jax.nn.sigmoid(x)

def _layernorm(x, axis=-1, eps=1e-05):
    m = jnp.mean(x, axis=axis, keepdims=True)
    v = jnp.var(x, axis=axis, keepdims=True)
    return (x - m) / jnp.sqrt(v + eps)

def _scatter_add(tgt, idx, src, axis=0):
    return tgt.at[idx].add(src)

def _segment_sum(src, seg, n):
    return jax.ops.segment_sum(src, seg, n)
kernel_name = 'mk_prb_d2_jaxref_r8_f38002'

def setup_inputs(seed: int=0):
    np.random.seed(seed)
    _w = jnp.asarray

    def _L0_attn_setup():
        import jax, jax.numpy as jnp
        import numpy as np
        from jax import lax
        LN_EPS = 1e-05
        B, T, C = (4, 512, 128)

        def _layernorm(x, w, b):
            mu = jnp.mean(x, axis=-1, keepdims=True)
            var = jnp.mean((x - mu) ** 2, axis=-1, keepdims=True)
            return (x - mu) * lax.rsqrt(var + LN_EPS) * w + b
        key = jax.random.key(seed)
        ks = jax.random.split(key, 12)
        s = 1.0 / np.sqrt(C)
        return {'x': jax.random.normal(ks[0], (B, T, C), dtype=jnp.float32), 'time_mix_k': jax.random.uniform(ks[1], (C,), dtype=jnp.float32), 'time_mix_v': jax.random.uniform(ks[2], (C,), dtype=jnp.float32), 'time_mix_r': jax.random.uniform(ks[3], (C,), dtype=jnp.float32), 'time_decay': jnp.zeros((C,), dtype=jnp.float32), 'time_first': jnp.zeros((C,), dtype=jnp.float32), 'Wk': jax.random.uniform(ks[4], (C, C), jnp.float32, -s, s), 'Wv': jax.random.uniform(ks[5], (C, C), jnp.float32, -s, s), 'Wr': jax.random.uniform(ks[6], (C, C), jnp.float32, -s, s), 'Wo': jax.random.uniform(ks[7], (C, C), jnp.float32, -s, s), 'ln_w': jnp.ones((C,), dtype=jnp.float32), 'ln_b': jnp.zeros((C,), dtype=jnp.float32)}
    _L0_attn_in = _L0_attn_setup()

    def _L0_ffn_setup():
        import jax, jax.numpy as jnp
        import numpy as np
        B, T, D = (8, 512, 128)
        NUM_SLOTS = 64
        TOP_K = 8
        DQ = D // 4
        DH = D // 2

        def _forward(x, slot_init, w1, b1, w2, b2, tau, Wih, Whh, bih, bhh, wq, bq, wk, bk, wv, bv, ln_g, ln_b, wvp, bvp, wo, bo):
            Bx, Tx, Dx = x.shape
            S = jnp.broadcast_to(slot_init[None], (Bx, NUM_SLOTS, Dx)).astype(x.dtype)
            slot_mean = jnp.broadcast_to(S.mean(axis=1, keepdims=True), (Bx, Tx, Dx))
            ctx = jnp.concatenate([x, slot_mean], axis=-1)
            h = jax.nn.gelu(ctx @ w1 + b1, approximate=False)
            route_logits = (h @ w2 + b2) / (jnp.abs(tau) + 0.1)
            topk_vals, topk_idx = jax.lax.top_k(route_logits, TOP_K)
            topk_w = jax.nn.softmax(topk_vals, axis=-1)
            alpha = (jax.nn.one_hot(topk_idx, NUM_SLOTS, dtype=x.dtype) * topk_w[..., None]).sum(axis=-2)
            slot_input = jnp.einsum('bts,btd->bsd', alpha, x)
            denom = alpha.sum(axis=1) + 1e-08
            si = slot_input / denom[..., None]
            gi = si @ Wih.T + bih
            gh = S @ Whh.T + bhh
            i_r, i_z, i_n = jnp.split(gi, 3, axis=-1)
            h_r, h_z, h_n = jnp.split(gh, 3, axis=-1)
            r = jax.nn.sigmoid(i_r + h_r)
            z = jax.nn.sigmoid(i_z + h_z)
            n = jnp.tanh(i_n + r * h_n)
            S_new = (1.0 - z) * n + z * S
            q = S_new @ wq + bq
            k = S_new @ wk + bk
            v = S_new @ wv + bv
            scale = DQ ** (-0.5)
            attn = jax.nn.softmax(jnp.einsum('bsq,btq->bst', q, k) * scale, axis=-1)
            S_comm = jnp.einsum('bst,btd->bsd', attn, v)
            y = S_new + S_comm
            mu = y.mean(axis=-1, keepdims=True)
            var = y.var(axis=-1, keepdims=True)
            y = (y - mu) * jax.lax.rsqrt(var + 1e-05) * ln_g + ln_b
            slot_values = y @ wvp + bvp
            out = jnp.einsum('bts,bsd->btd', alpha, slot_values)
            return out @ wo + bo
        key = jax.random.key(seed)
        ks = jax.random.split(key, 24)
        n = lambda k, shp, s=0.02: jax.random.normal(k, shp, dtype=jnp.float32) * s
        return {'x': jax.random.normal(ks[0], (B, T, D), dtype=jnp.float32), 'slot_init': n(ks[1], (NUM_SLOTS, D)), 'w1': n(ks[2], (2 * D, DH)), 'b1': jnp.zeros((DH,)), 'w2': n(ks[3], (DH, NUM_SLOTS)), 'b2': jnp.zeros((NUM_SLOTS,)), 'tau': jnp.ones((1,)), 'Wih': n(ks[4], (3 * D, D)), 'Whh': n(ks[5], (3 * D, D)), 'bih': jnp.zeros((3 * D,)), 'bhh': jnp.zeros((3 * D,)), 'wq': n(ks[6], (D, DQ)), 'bq': jnp.zeros((DQ,)), 'wk': n(ks[7], (D, DQ)), 'bk': jnp.zeros((DQ,)), 'wv': n(ks[8], (D, D)), 'bv': jnp.zeros((D,)), 'ln_g': jnp.ones((D,)), 'ln_b': jnp.zeros((D,)), 'wvp': n(ks[9], (D, D)), 'bvp': jnp.zeros((D,)), 'wo': n(ks[10], (D, D)), 'bo': jnp.zeros((D,))}
    _L0_ffn_in = _L0_ffn_setup()

    def _L1_attn_setup():
        import jax, jax.numpy as jnp
        import numpy as np
        N_HEADS = 16
        WINDOW = 128
        EPS = 1e-06

        def rmsnorm(x, w):
            return x * jax.lax.rsqrt(jnp.mean(x * x, axis=-1, keepdims=True) + EPS) * w

        def linear(x, W, b=None):
            y = jnp.einsum('bsd,od->bso', x, W)
            return y + b if b is not None else y

        def min_gru(x, Wg, bg, Wv, bv, Wd, bd):
            g = linear(x, Wg, bg)
            v = linear(x, Wv, bv)
            d = linear(x, Wd, bd)
            x_scan = jax.nn.sigmoid(g) * jnp.tanh(v)
            a = 0.001 + 0.998 * jax.nn.sigmoid(d)

            def comb(e1, e2):
                a1, x1 = e1
                a2, x2 = e2
                return (a1 * a2, a2 * x1 + x2)
            _, h = jax.lax.associative_scan(comb, (a, x_scan), axis=1)
            return h

        def sliding_attn(x, Wqkv, Wo):
            B, S, D = x.shape
            Hh, Wd_ = (N_HEADS, D // N_HEADS)
            W = WINDOW
            qkv = linear(x, Wqkv).reshape(B, S, 3, Hh, Wd_)
            q = qkv[:, :, 0].transpose(0, 2, 1, 3)
            k = qkv[:, :, 1].transpose(0, 2, 1, 3)
            v = qkv[:, :, 2].transpose(0, 2, 1, 3)
            nC = S // W
            qc = q.reshape(B, Hh, nC, W, Wd_)
            kc = k.reshape(B, Hh, nC, W, Wd_)
            vc = v.reshape(B, Hh, nC, W, Wd_)
            kp = jnp.concatenate([jnp.zeros_like(kc[:, :, :1]), kc[:, :, :-1]], axis=2)
            vp = jnp.concatenate([jnp.zeros_like(vc[:, :, :1]), vc[:, :, :-1]], axis=2)
            kk = jnp.concatenate([kp, kc], axis=3)
            vv = jnp.concatenate([vp, vc], axis=3)
            scores = jnp.einsum('bhcqd,bhckd->bhcqk', qc, kk) / np.sqrt(Wd_)
            j = jnp.arange(W)[:, None]
            kidx = jnp.arange(2 * W)[None, :]
            cidx = jnp.arange(nC)[:, None, None]
            mask = (kidx <= W + j) & (kidx >= j + 1) & ((kidx >= W) | (cidx > 0))
            scores = jnp.where(mask[None, None], scores, jnp.finfo(scores.dtype).min)
            attn = jax.nn.softmax(scores, axis=-1)
            out = jnp.einsum('bhcqk,bhckd->bhcqd', attn, vv)
            out = out.reshape(B, Hh, S, Wd_).transpose(0, 2, 1, 3).reshape(B, S, D)
            return linear(out, Wo)

        def glu_ffn(x, Wgate, Wup, Wout):
            return linear(jax.nn.silu(linear(x, Wgate)) * linear(x, Wup), Wout)
        key = jax.random.key(seed)
        B, S, D, DFF = (4, 256, 128, 512)
        ks = jax.random.split(key, 10)
        w = lambda k, shp: jax.random.normal(k, shp, dtype=jnp.float32) * 0.02
        return {'x': jax.random.normal(ks[0], (B, S, D), dtype=jnp.float32), 'w_rms_mix': jnp.ones((D,), jnp.float32), 'Wg': w(ks[1], (D, D)), 'bg': jnp.zeros((D,), jnp.float32), 'Wv': w(ks[2], (D, D)), 'bv': jnp.zeros((D,), jnp.float32), 'Wd': w(ks[3], (D, D)), 'bd': jnp.ones((D,), jnp.float32), 'w_rms_attn': jnp.ones((D,), jnp.float32), 'Wqkv': w(ks[4], (3 * D, D)), 'Wo': w(ks[5], (D, D)), 'w_rms_ffn': jnp.ones((D,), jnp.float32), 'Wgate': w(ks[6], (DFF, D)), 'Wup': w(ks[7], (DFF, D)), 'Wout': w(ks[8], (D, DFF))}
    _L1_attn_in = _L1_attn_setup()

    def _L1_ffn_setup():
        import jax, jax.numpy as jnp
        import numpy as np
        B, S, D, E, H, K = (4, 256, 128, 8, 512, 2)
        EPS = 1e-06

        def _ln(x, scale, bias):
            m = jnp.mean(x, axis=-1, keepdims=True)
            v = jnp.mean(jnp.square(x - m), axis=-1, keepdims=True)
            return (x - m) * jax.lax.rsqrt(v + EPS) * scale + bias
        key = jax.random.key(seed)
        ks = jax.random.split(key, 4)
        s1 = 1.0 / np.sqrt(D)
        s2 = 1.0 / np.sqrt(H)
        return {'x': jax.random.normal(ks[0], (B, S, D), jnp.float32), 'router_ln_scale': jnp.ones((D,), jnp.float32), 'router_ln_bias': jnp.zeros((D,), jnp.float32), 'router_w': jax.random.normal(ks[1], (E, D), jnp.float32) * s1, 'router_b': jnp.zeros((E,), jnp.float32), 'expert_ln_scale': jnp.ones((E, D), jnp.float32), 'expert_ln_bias': jnp.zeros((E, D), jnp.float32), 'w1': jax.random.normal(ks[2], (E, H, D), jnp.float32) * s1, 'b1': jnp.zeros((E, H), jnp.float32), 'w2': jax.random.normal(ks[3], (E, D, H), jnp.float32) * s2, 'b2': jnp.zeros((E, D), jnp.float32)}
    _L1_ffn_in = _L1_ffn_setup()
    _d = {'L0_attn_x': _L0_attn_in['x'], 'L0_attn_time_mix_k': _L0_attn_in['time_mix_k'], 'L0_attn_time_mix_v': _L0_attn_in['time_mix_v'], 'L0_attn_time_mix_r': _L0_attn_in['time_mix_r'], 'L0_attn_time_decay': _L0_attn_in['time_decay'], 'L0_attn_time_first': _L0_attn_in['time_first'], 'L0_attn_Wk': _L0_attn_in['Wk'], 'L0_attn_Wv': _L0_attn_in['Wv'], 'L0_attn_Wr': _L0_attn_in['Wr'], 'L0_attn_Wo': _L0_attn_in['Wo'], 'L0_attn_ln_w': _L0_attn_in['ln_w'], 'L0_attn_ln_b': _L0_attn_in['ln_b'], 'L0_ffn_slot_init': _L0_ffn_in['slot_init'], 'L0_ffn_w1': _L0_ffn_in['w1'], 'L0_ffn_b1': _L0_ffn_in['b1'], 'L0_ffn_w2': _L0_ffn_in['w2'], 'L0_ffn_b2': _L0_ffn_in['b2'], 'L0_ffn_tau': _L0_ffn_in['tau'], 'L0_ffn_Wih': _L0_ffn_in['Wih'], 'L0_ffn_Whh': _L0_ffn_in['Whh'], 'L0_ffn_bih': _L0_ffn_in['bih'], 'L0_ffn_bhh': _L0_ffn_in['bhh'], 'L0_ffn_wq': _L0_ffn_in['wq'], 'L0_ffn_bq': _L0_ffn_in['bq'], 'L0_ffn_wk': _L0_ffn_in['wk'], 'L0_ffn_bk': _L0_ffn_in['bk'], 'L0_ffn_wv': _L0_ffn_in['wv'], 'L0_ffn_bv': _L0_ffn_in['bv'], 'L0_ffn_ln_g': _L0_ffn_in['ln_g'], 'L0_ffn_ln_b': _L0_ffn_in['ln_b'], 'L0_ffn_wvp': _L0_ffn_in['wvp'], 'L0_ffn_bvp': _L0_ffn_in['bvp'], 'L0_ffn_wo': _L0_ffn_in['wo'], 'L0_ffn_bo': _L0_ffn_in['bo'], 'L1_attn_w_rms_mix': _L1_attn_in['w_rms_mix'], 'L1_attn_Wg': _L1_attn_in['Wg'], 'L1_attn_bg': _L1_attn_in['bg'], 'L1_attn_Wv': _L1_attn_in['Wv'], 'L1_attn_bv': _L1_attn_in['bv'], 'L1_attn_Wd': _L1_attn_in['Wd'], 'L1_attn_bd': _L1_attn_in['bd'], 'L1_attn_w_rms_attn': _L1_attn_in['w_rms_attn'], 'L1_attn_Wqkv': _L1_attn_in['Wqkv'], 'L1_attn_Wo': _L1_attn_in['Wo'], 'L1_attn_w_rms_ffn': _L1_attn_in['w_rms_ffn'], 'L1_attn_Wgate': _L1_attn_in['Wgate'], 'L1_attn_Wup': _L1_attn_in['Wup'], 'L1_attn_Wout': _L1_attn_in['Wout'], 'L1_ffn_router_ln_scale': _L1_ffn_in['router_ln_scale'], 'L1_ffn_router_ln_bias': _L1_ffn_in['router_ln_bias'], 'L1_ffn_router_w': _L1_ffn_in['router_w'], 'L1_ffn_router_b': _L1_ffn_in['router_b'], 'L1_ffn_expert_ln_scale': _L1_ffn_in['expert_ln_scale'], 'L1_ffn_expert_ln_bias': _L1_ffn_in['expert_ln_bias'], 'L1_ffn_w1': _L1_ffn_in['w1'], 'L1_ffn_b1': _L1_ffn_in['b1'], 'L1_ffn_w2': _L1_ffn_in['w2'], 'L1_ffn_b2': _L1_ffn_in['b2']}
    _x0 = _d['L0_attn_x']
    _d['L0_attn_x'] = jax.random.normal(jax.random.fold_in(jax.random.key(seed), 1), (2, 2048, 128), dtype=_x0.dtype)
    del _x0
    return _d

def reference(L0_attn_x, L0_attn_time_mix_k, L0_attn_time_mix_v, L0_attn_time_mix_r, L0_attn_time_decay, L0_attn_time_first, L0_attn_Wk, L0_attn_Wv, L0_attn_Wr, L0_attn_Wo, L0_attn_ln_w, L0_attn_ln_b, L0_ffn_slot_init, L0_ffn_w1, L0_ffn_b1, L0_ffn_w2, L0_ffn_b2, L0_ffn_tau, L0_ffn_Wih, L0_ffn_Whh, L0_ffn_bih, L0_ffn_bhh, L0_ffn_wq, L0_ffn_bq, L0_ffn_wk, L0_ffn_bk, L0_ffn_wv, L0_ffn_bv, L0_ffn_ln_g, L0_ffn_ln_b, L0_ffn_wvp, L0_ffn_bvp, L0_ffn_wo, L0_ffn_bo, L1_attn_w_rms_mix, L1_attn_Wg, L1_attn_bg, L1_attn_Wv, L1_attn_bv, L1_attn_Wd, L1_attn_bd, L1_attn_w_rms_attn, L1_attn_Wqkv, L1_attn_Wo, L1_attn_w_rms_ffn, L1_attn_Wgate, L1_attn_Wup, L1_attn_Wout, L1_ffn_router_ln_scale, L1_ffn_router_ln_bias, L1_ffn_router_w, L1_ffn_router_b, L1_ffn_expert_ln_scale, L1_ffn_expert_ln_bias, L1_ffn_w1, L1_ffn_b1, L1_ffn_w2, L1_ffn_b2):

    def _L0_attn_ref(x, time_mix_k, time_mix_v, time_mix_r, time_decay, time_first, Wk, Wv, Wr, Wo, ln_w, ln_b):
        import jax, jax.numpy as jnp
        import numpy as np
        from jax import lax
        LN_EPS = 1e-05
        B, T, C = (4, 512, 128)

        def _layernorm(x, w, b):
            mu = jnp.mean(x, axis=-1, keepdims=True)
            var = jnp.mean((x - mu) ** 2, axis=-1, keepdims=True)
            return (x - mu) * lax.rsqrt(var + LN_EPS) * w + b
        xt = _layernorm(x, ln_w, ln_b)
        x_prev = jnp.pad(xt[:, :-1], ((0, 0), (1, 0), (0, 0)))
        decay = jax.nn.sigmoid(time_decay)
        first = jnp.exp(time_first)
        mk, mv, mr = (time_mix_k, time_mix_v, time_mix_r)
        K = jnp.einsum('btc,dc->btd', xt * mk + x_prev * (1.0 - mk), Wk)
        V = jnp.einsum('btc,dc->btd', xt * mv + x_prev * (1.0 - mv), Wv)
        R = jax.nn.sigmoid(jnp.einsum('btc,dc->btd', xt * mr + x_prev * (1.0 - mr), Wr))

        def step(state, k_t):
            state = state * decay + k_t
            return (state, state)
        _, S = lax.scan(step, jnp.zeros((x.shape[0], K.shape[-1]), x.dtype), jnp.swapaxes(K, 0, 1))
        S = jnp.swapaxes(S, 0, 1)
        rwkv = (S * first + K) * V
        y = jnp.einsum('btc,dc->btd', R * rwkv, Wo)
        return x + y

    def _L0_ffn_ref(x, slot_init, w1, b1, w2, b2, tau, Wih, Whh, bih, bhh, wq, bq, wk, bk, wv, bv, ln_g, ln_b, wvp, bvp, wo, bo):
        import jax, jax.numpy as jnp
        import numpy as np
        B, T, D = (8, 512, 128)
        NUM_SLOTS = 64
        TOP_K = 8
        DQ = D // 4
        DH = D // 2

        def _forward(x, slot_init, w1, b1, w2, b2, tau, Wih, Whh, bih, bhh, wq, bq, wk, bk, wv, bv, ln_g, ln_b, wvp, bvp, wo, bo):
            Bx, Tx, Dx = x.shape
            S = jnp.broadcast_to(slot_init[None], (Bx, NUM_SLOTS, Dx)).astype(x.dtype)
            slot_mean = jnp.broadcast_to(S.mean(axis=1, keepdims=True), (Bx, Tx, Dx))
            ctx = jnp.concatenate([x, slot_mean], axis=-1)
            h = jax.nn.gelu(ctx @ w1 + b1, approximate=False)
            route_logits = (h @ w2 + b2) / (jnp.abs(tau) + 0.1)
            topk_vals, topk_idx = jax.lax.top_k(route_logits, TOP_K)
            topk_w = jax.nn.softmax(topk_vals, axis=-1)
            alpha = (jax.nn.one_hot(topk_idx, NUM_SLOTS, dtype=x.dtype) * topk_w[..., None]).sum(axis=-2)
            slot_input = jnp.einsum('bts,btd->bsd', alpha, x)
            denom = alpha.sum(axis=1) + 1e-08
            si = slot_input / denom[..., None]
            gi = si @ Wih.T + bih
            gh = S @ Whh.T + bhh
            i_r, i_z, i_n = jnp.split(gi, 3, axis=-1)
            h_r, h_z, h_n = jnp.split(gh, 3, axis=-1)
            r = jax.nn.sigmoid(i_r + h_r)
            z = jax.nn.sigmoid(i_z + h_z)
            n = jnp.tanh(i_n + r * h_n)
            S_new = (1.0 - z) * n + z * S
            q = S_new @ wq + bq
            k = S_new @ wk + bk
            v = S_new @ wv + bv
            scale = DQ ** (-0.5)
            attn = jax.nn.softmax(jnp.einsum('bsq,btq->bst', q, k) * scale, axis=-1)
            S_comm = jnp.einsum('bst,btd->bsd', attn, v)
            y = S_new + S_comm
            mu = y.mean(axis=-1, keepdims=True)
            var = y.var(axis=-1, keepdims=True)
            y = (y - mu) * jax.lax.rsqrt(var + 1e-05) * ln_g + ln_b
            slot_values = y @ wvp + bvp
            out = jnp.einsum('bts,bsd->btd', alpha, slot_values)
            return out @ wo + bo
        return _forward(x, slot_init, w1, b1, w2, b2, tau, Wih, Whh, bih, bhh, wq, bq, wk, bk, wv, bv, ln_g, ln_b, wvp, bvp, wo, bo)

    def _L1_attn_ref(x, w_rms_mix, Wg, bg, Wv, bv, Wd, bd, w_rms_attn, Wqkv, Wo, w_rms_ffn, Wgate, Wup, Wout):
        import jax, jax.numpy as jnp
        import numpy as np
        N_HEADS = 16
        WINDOW = 128
        EPS = 1e-06

        def rmsnorm(x, w):
            return x * jax.lax.rsqrt(jnp.mean(x * x, axis=-1, keepdims=True) + EPS) * w

        def linear(x, W, b=None):
            y = jnp.einsum('bsd,od->bso', x, W)
            return y + b if b is not None else y

        def min_gru(x, Wg, bg, Wv, bv, Wd, bd):
            g = linear(x, Wg, bg)
            v = linear(x, Wv, bv)
            d = linear(x, Wd, bd)
            x_scan = jax.nn.sigmoid(g) * jnp.tanh(v)
            a = 0.001 + 0.998 * jax.nn.sigmoid(d)

            def comb(e1, e2):
                a1, x1 = e1
                a2, x2 = e2
                return (a1 * a2, a2 * x1 + x2)
            _, h = jax.lax.associative_scan(comb, (a, x_scan), axis=1)
            return h

        def sliding_attn(x, Wqkv, Wo):
            B, S, D = x.shape
            Hh, Wd_ = (N_HEADS, D // N_HEADS)
            W = WINDOW
            qkv = linear(x, Wqkv).reshape(B, S, 3, Hh, Wd_)
            q = qkv[:, :, 0].transpose(0, 2, 1, 3)
            k = qkv[:, :, 1].transpose(0, 2, 1, 3)
            v = qkv[:, :, 2].transpose(0, 2, 1, 3)
            nC = S // W
            qc = q.reshape(B, Hh, nC, W, Wd_)
            kc = k.reshape(B, Hh, nC, W, Wd_)
            vc = v.reshape(B, Hh, nC, W, Wd_)
            kp = jnp.concatenate([jnp.zeros_like(kc[:, :, :1]), kc[:, :, :-1]], axis=2)
            vp = jnp.concatenate([jnp.zeros_like(vc[:, :, :1]), vc[:, :, :-1]], axis=2)
            kk = jnp.concatenate([kp, kc], axis=3)
            vv = jnp.concatenate([vp, vc], axis=3)
            scores = jnp.einsum('bhcqd,bhckd->bhcqk', qc, kk) / np.sqrt(Wd_)
            j = jnp.arange(W)[:, None]
            kidx = jnp.arange(2 * W)[None, :]
            cidx = jnp.arange(nC)[:, None, None]
            mask = (kidx <= W + j) & (kidx >= j + 1) & ((kidx >= W) | (cidx > 0))
            scores = jnp.where(mask[None, None], scores, jnp.finfo(scores.dtype).min)
            attn = jax.nn.softmax(scores, axis=-1)
            out = jnp.einsum('bhcqk,bhckd->bhcqd', attn, vv)
            out = out.reshape(B, Hh, S, Wd_).transpose(0, 2, 1, 3).reshape(B, S, D)
            return linear(out, Wo)

        def glu_ffn(x, Wgate, Wup, Wout):
            return linear(jax.nn.silu(linear(x, Wgate)) * linear(x, Wup), Wout)
        x = x + min_gru(rmsnorm(x, w_rms_mix), Wg, bg, Wv, bv, Wd, bd)
        x = x + sliding_attn(rmsnorm(x, w_rms_attn), Wqkv, Wo)
        x = x + glu_ffn(rmsnorm(x, w_rms_ffn), Wgate, Wup, Wout)
        return x

    def _L1_ffn_ref(x, router_ln_scale, router_ln_bias, router_w, router_b, expert_ln_scale, expert_ln_bias, w1, b1, w2, b2):
        import jax, jax.numpy as jnp
        import numpy as np
        B, S, D, E, H, K = (4, 256, 128, 8, 512, 2)
        EPS = 1e-06

        def _ln(x, scale, bias):
            m = jnp.mean(x, axis=-1, keepdims=True)
            v = jnp.mean(jnp.square(x - m), axis=-1, keepdims=True)
            return (x - m) * jax.lax.rsqrt(v + EPS) * scale + bias
        orig_shape = x.shape
        xf = x.reshape(-1, D)
        T = xf.shape[0]
        logits = _ln(xf, router_ln_scale, router_ln_bias) @ router_w.T + router_b
        probs = jax.nn.softmax(logits, axis=-1)
        topw, topi = jax.lax.top_k(probs, K)
        topw = topw / jnp.sum(topw, axis=-1, keepdims=True)
        gates = jnp.zeros((T, E), xf.dtype).at[jnp.arange(T)[:, None], topi].set(topw)

        def expert(ls, lb, W1, B1, W2, B2):
            h = jax.nn.gelu(_ln(xf, ls, lb) @ W1.T + B1, approximate=False)
            return h @ W2.T + B2
        ys = jax.vmap(expert)(expert_ln_scale, expert_ln_bias, w1, b1, w2, b2)
        out = jnp.einsum('te,etd->td', gates, ys)
        return out.reshape(orig_shape)
    x = L0_attn_x
    xn = _layernorm(x, axis=-1)
    x = x + _L0_attn_ref(xn, L0_attn_time_mix_k, L0_attn_time_mix_v, L0_attn_time_mix_r, L0_attn_time_decay, L0_attn_time_first, L0_attn_Wk, L0_attn_Wv, L0_attn_Wr, L0_attn_Wo, L0_attn_ln_w, L0_attn_ln_b) + _L0_ffn_ref(xn, L0_ffn_slot_init, L0_ffn_w1, L0_ffn_b1, L0_ffn_w2, L0_ffn_b2, L0_ffn_tau, L0_ffn_Wih, L0_ffn_Whh, L0_ffn_bih, L0_ffn_bhh, L0_ffn_wq, L0_ffn_bq, L0_ffn_wk, L0_ffn_bk, L0_ffn_wv, L0_ffn_bv, L0_ffn_ln_g, L0_ffn_ln_b, L0_ffn_wvp, L0_ffn_bvp, L0_ffn_wo, L0_ffn_bo)
    xn = _layernorm(x, axis=-1)
    x = x + _L1_attn_ref(xn, L1_attn_w_rms_mix, L1_attn_Wg, L1_attn_bg, L1_attn_Wv, L1_attn_bv, L1_attn_Wd, L1_attn_bd, L1_attn_w_rms_attn, L1_attn_Wqkv, L1_attn_Wo, L1_attn_w_rms_ffn, L1_attn_Wgate, L1_attn_Wup, L1_attn_Wout) + _L1_ffn_ref(xn, L1_ffn_router_ln_scale, L1_ffn_router_ln_bias, L1_ffn_router_w, L1_ffn_router_b, L1_ffn_expert_ln_scale, L1_ffn_expert_ln_bias, L1_ffn_w1, L1_ffn_b1, L1_ffn_w2, L1_ffn_b2)
    return x

_drawn_inputs = setup_inputs


def setup_inputs(seed=0):
    import zlib

    import numpy as np

    out = dict(_drawn_inputs(seed))
    spreads = {'L0_attn_time_decay': (0.0, 0.8),
     'L0_attn_time_first': (0.0, 0.769),
     'L0_attn_ln_w': (1.0, 0.2),
     'L0_attn_ln_b': (0.0, 0.325),
     'L0_ffn_b1': (0.0, 2.0),
     'L0_ffn_b2': (0.0, 2.0),
     'L0_ffn_bih': (0.0, 0.516),
     'L0_ffn_bhh': (0.0, 0.595),
     'L0_ffn_bq': (0.0, 2.0),
     'L0_ffn_bk': (0.0, 2.0),
     'L0_ffn_bv': (0.0, 0.283),
     'L0_ffn_ln_g': (1.0, 0.6),
     'L0_ffn_ln_b': (0.0, 0.8),
     'L0_ffn_bvp': (0.0, 0.483),
     'L0_ffn_bo': (0.0, 0.1),
     'L1_attn_w_rms_mix': (1.0, 0.6),
     'L1_attn_bg': (0.0, 0.8),
     'L1_attn_bv': (0.0, 0.1),
     'L1_attn_bd': (1.0, 0.6),
     'L1_attn_w_rms_attn': (1.0, 0.6),
     'L1_attn_w_rms_ffn': (1.0, 0.6),
     'L1_ffn_router_ln_scale': (1.0, 0.6),
     'L1_ffn_router_ln_bias': (0.0, 0.584),
     'L1_ffn_router_b': (0.0, 0.738),
     'L1_ffn_expert_ln_scale': (1.0, 0.6),
     'L1_ffn_expert_ln_bias': (0.0, 2.0),
     'L1_ffn_b1': (0.0, 2.0),
     'L1_ffn_b2': (0.0, 1.502)}
    factors = {'L0_attn_time_mix_r': 4.219,
     'L0_ffn_slot_init': 8.0,
     'L0_ffn_w1': 8.0,
     'L0_ffn_w2': 8.0,
     'L0_ffn_Wih': 8.0,
     'L0_ffn_Whh': 38.625,
     'L0_ffn_wq': 32.287,
     'L0_ffn_wk': 25.236,
     'L0_ffn_wv': 8.0,
     'L1_attn_Wg': 7.621,
     'L1_attn_Wd': 8.0,
     'L1_attn_Wqkv': 8.0,
     'L1_attn_Wo': 8.0,
     'L1_attn_Wgate': 8.0,
     'L1_attn_Wup': 8.0,
     'L1_attn_Wout': 8.0}
    for name, (base, spread) in spreads.items():
        noise = np.random.default_rng([zlib.crc32(name.encode()), seed]).standard_normal(out[name].shape)
        drawn = base * np.exp(spread * noise) if base else spread * noise
        out[name] = jnp.asarray(drawn.astype(out[name].dtype))
    for name, factor in factors.items():
        out[name] = (out[name] * factor).astype(out[name].dtype)
    return out
```

```python
from contextlib import ExitStack

import concourse.bass as bass
from concourse import mybir

P = 128
F32 = mybir.dt.float32
BF16 = mybir.dt.bfloat16
U32 = mybir.dt.uint32
ALU = mybir.AluOpType
ACT = mybir.ActivationFunctionType
AX_X = mybir.AxisListType.X

B, T, C = 2, 2048, 128
NTOK = B * T
NT = NTOK // P
TG = 4
GW = TG * P
NG = NT // TG
GB = NG // B
SLOTS = 64
NH, DH, DHP = 16, 8, 9
NPART = 6
QP = (0, 0, 1, 1, 0, 2)
KP = (0, 1, 0, 1, 2, 0)
DFF, NF = 512, 4
E = 8
NEG = -1.0e30
LN_EPS, RMS_EPS, MOE_EPS = 1e-5, 1e-6, 1e-6
HQ = 4
NQ = NH // HQ
R3 = 3

MAT0 = [("Wk", 128), ("Wv", 128), ("Wr", 128), ("Wo", 128), ("w1a", 64), ("w1b", 64),
        ("slotT", 64), ("slotT2", 128), ("slot2", 128), ("ident", 128)]
MAT1 = [("Wih", 384), ("Whh", 384), ("wq", 32), ("wk", 32), ("wv", 128), ("wvp", 128), ("wo", 128), ("blockneg", 128)]
MAT2 = [("Wg", 128), ("Wv", 128), ("Wd", 128), ("Wqkv", 384), ("Wo", 128), ("Wgate", 512), ("Wup", 512),
        ("Wout", 512), ("maskprev", 128), ("maskcur", 128), ("router", 8)]
COLS = [("mk", 1), ("mv", 1), ("mr", 1), ("decay", 1), ("first", 1), ("ln_w", 1), ("ln_b", 1), ("bvp", 1),
        ("w_mix", 1), ("bg", 1), ("bv", 1), ("bd", 1), ("w_attn", 1), ("w_ffn", 1), ("rln_s", 1), ("rln_b", 1),
        ("els", 8), ("elb", 8), ("b1", 32)]
ROWS = [("b2", 64), ("tau", 1), ("bih", 384), ("bhh", 384), ("bv", 128), ("ln_g", 128), ("ln_b", 128),
        ("bo", 128), ("router_b", 8), ("iota8", 8)]


def places(pack):
    at, out = 0, {}
    for name, n in pack:
        out[name] = (at, at + n)
        at += n
    return out, at


def build(nc, x, mat0, mat1, mat2, cols, rows, w2s, bqk, b1s, moe_w1, moe_w2, moe_b2, out):
    p0, n0 = places(MAT0)
    p1, n1 = places(MAT1)
    p2, n2 = places(MAT2)
    pc, ncol = places(COLS)
    pr, nrow = places(ROWS)
    x_v = x.rearrange("(t p) c -> p t c", p=P)
    out_v = out.rearrange("(t p) c -> p t c", p=P)
    q_dram = nc.dram_tensor("q_parts", [3, NH, DH, NTOK], BF16, kind="Internal").ap()
    k_dram = nc.dram_tensor("k_parts", [3, NH, DH, NTOK], BF16, kind="Internal").ap()

    with ExitStack() as ctx:
        def sb(name, shape, dt=F32):
            return ctx.enter_context(nc.sbuf_tensor(name, shape, dt))

        def sem(name):
            return ctx.enter_context(nc.semaphore(name))

        M0, M1, M2 = sb("M0", [P, n0]), sb("M1", [P, n1]), sb("M2", [P, n2])
        CO, RO = sb("CO", [P, ncol]), sb("RO", [P, nrow])
        W2S, BQK, B1S = sb("W2S", [64, 64]), sb("BQK", [32, 2]), sb("B1S", [64, 1])
        B2E = sb("B2E", [E, P])
        ACC = sb("ACC", [P, NT, C])
        XN = sb("XN", [P, NT, C + 1])
        BIG = sb("BIG", [P, 4 * NTOK])
        SM = sb("SM", [P, 4096])

        m0 = {k: M0[:, a:b] for k, (a, b) in p0.items()}
        m1 = {k: M1[:, a:b] for k, (a, b) in p1.items()}
        m2 = {k: M2[:, a:b] for k, (a, b) in p2.items()}
        co = {k: CO[:, a:b] for k, (a, b) in pc.items()}
        ro = {k: RO[:, a:b] for k, (a, b) in pr.items()}
        ident = m0["ident"]

        ST = sb("ST", [P, NT, 6])
        MV = sb("MV", [P, NT, 2])
        VE = sb("VE", [P, NT])
        RS = sb("RS", [P, NT])
        MH = sb("MH", [P, NT])
        cst = sb("cst", [P, 16])
        DEC = sb("DEC", [P, GW])

        PS = ctx.enter_context(nc.psum_tensor("PS", [P, 8, 512], F32))
        bank = [PS[:, i, :] for i in range(8)]
        bank4 = [b.rearrange("p (t c) -> p t c", t=TG) for b in bank]

        XH = BIG[:, 0:NTOK].rearrange("p (t c) -> p t c", t=NT)
        XT = BIG[:, NTOK:NTOK + B * (T + 1)].rearrange("p (b t) -> p b t", b=B)
        o = NTOK + B * (T + 1) + 2
        LG = BIG[:, o:o + NT * SLOTS].rearrange("p (t s) -> p t s", t=NT)
        o += NT * SLOTS
        LR = BIG[:, o:o + NT * SLOTS].rearrange("p (t s) -> p t s", t=NT)
        o += NT * SLOTS
        xnT = [BIG[:, o + 512 * i:o + 512 * i + 512] for i in range(2)]
        o += 1024
        R2 = sb("R2", [P, 2048])
        mixed = [[BIG[:, o + 512 * j:o + 512 * j + 512] for j in range(3)], [R2[:, 512 * j:512 * j + 512] for j in range(3)]]
        assert o + 1536 <= 4 * NTOK
        V8 = sb("V8", [P, NT, 8])
        I8 = sb("I8", [P, NT, 8], U32)
        hT = [SM[0:64, 512 * i:512 * i + 512] for i in range(2)]
        rT = [SM[:, 1024 + 512 * i:1024 + 512 * i + 512] for i in range(2)]
        rw = [SM[:, 2048 + 512 * i:2048 + 512 * i + 512] for i in range(2)]
        SS = [SM[:, 3072 + 512 * i:3072 + 512 * i + 512] for i in range(2)]
        dif = sb("dif", [P, GW])

        ld_m0, ld_x, ld_m1, ld_m2 = sem("ld_m0"), [sem(f"ld_x{i}") for i in range(4)], sem("ld_m1"), sem("ld_m2")
        ld_small = sem("ld_small")
        ld_moe = sem("ld_moe")
        dve_step, act_step, pool_step = sem("dve_step"), sem("act_step"), sem("pool_step")
        var_ready, rstd_ready = sem("var_ready"), sem("rstd_ready")
        xh_ready, xn_ready = sem("xh_ready"), sem("xn_ready")
        xhT_ready, xt_ready, xnT_ready, xnTs_ready = sem("xhT_ready"), sem("xt_ready"), sem("xnT_ready"), sem("xnTs_ready")
        pre_ready = sem("pre_ready")
        h1_ready, h_ready, logit_ready, logit_used = sem("h1_ready"), sem("h_ready"), sem("logit_ready"), sem("logit_used")
        mix_ready, kvr_ready, kv_used, r_ready, rw_ready = sem("mix_ready"), sem("kvr_ready"), sem("kv_used"), sem("r_ready"), sem("rw_ready")
        y_ready, y_used = sem("y_ready"), sem("y_used")
        pre_mm, col_ready = sem("pre_mm"), sem("col_ready")
        slot_pe, slot_act, slot_dve, slot_pool = sem("slot_pe"), sem("slot_act"), sem("slot_dve"), sem("slot_pool")
        fills = sem("fills")
        phase_done = sem("phase_done")
        act_pre, q_hi, v8_ready, k_hi = sem("act_pre"), sem("q_hi"), sem("v8_ready"), sem("k_hi")

        def meet(eng, k):
            eng.wait_ge(phase_done, k)

        class Steps:
            def __init__(self, eng, s):
                self.eng, self.s, self.n = eng, s, 0

            def __call__(self, ins):
                self.n += 1
                ins.then_inc(self.s, 1)

            def wait(self):
                self.eng.wait_ge(self.s, self.n)

        block = ctx.enter_context(nc.Block())

        def slot_tile(i, n=P):
            return BIG[:, i:i + n]

        s1 = NTOK + B * (T + 1) + 2 + 2 * NT * SLOTS
        rden_t = sb("rden_t", [P, NT])
        si_t, siT_t = BIG[:, s1:s1 + 128], BIG[:, s1 + 128:s1 + 256]
        rz_t, hn_t = BIG[:, s1 + 256:s1 + 512], BIG[:, s1 + 512:s1 + 640]
        n_t, z_t = BIG[:, s1 + 640:s1 + 768], BIG[:, s1 + 768:s1 + 896]
        sn_t, snT_t = BIG[:, s1 + 896:s1 + 1024], BIG[:, s1 + 1024:s1 + 1152]
        qk_t = BIG[0:32, s1 + 1152:s1 + 1408].rearrange("p (a s) -> p a s", a=2)
        vv_t = BIG[:, s1 + 1408:s1 + 1536]
        sc_t, pe_t, pT_t = BIG[:, s1 + 1536:s1 + 1664], BIG[:, s1 + 1664:s1 + 1792], BIG[:, s1 + 1792:s1 + 1920]
        yy_t, yT_t, svT_t = BIG[:, s1 + 1920:s1 + 2048], BIG[:, s1 + 2048:s1 + 2176], BIG[:, s1 + 2176:s1 + 2304]
        col_t = sb("col_t", [P, 8])
        SVO = sb("SVO", [SLOTS, B, P])

        XLT = BIG[:, 0:NTOK]
        o = NTOK + B * (T + 1) + 2 + NT * SLOTS
        XR = BIG[:, o:o + NT * P].rearrange("p (t c) -> p t c", t=NT)
        XL = BIG[:, NTOK:2 * NTOK].rearrange("p (t c) -> p t c", t=NT)
        assert o + NT * P <= 4 * NTOK
        aT = [SM[0:64, 512 * i:512 * i + 512] for i in range(2)]
        o += NT * P

        xrT = [SM[:, 1024 + 512 * i:1536 + 512 * i] for i in range(2)]
        tg_t = [SM[:, 2048 + 512 * i:2560 + 512 * i] for i in range(2)]
        tv_t = [SM[:, 3072 + 512 * i:3584 + 512 * i] for i in range(2)]
        ta_t = [R2[:, 512 * i:512 * i + 512] for i in range(2)]
        hh_t = [R2[:, 1024 + 512 * i:1536 + 512 * i] for i in range(2)]
        alphaT_ready, alphaTs_ready, o_ready, x1_ready = sem("alphaT_ready"), sem("alphaTs_ready"), sem("o_ready"), sem("x1_ready")
        xr2_ready, tr_ready, trs_ready = sem("xr2_ready"), sem("tr_ready"), sem("trs_ready")
        gvd_ready, gate_ready, gvd_used = sem("gvd_ready"), sem("gate_ready"), sem("gvd_used")
        scan_ready, hT_ready, hT_used = sem("scan_ready"), sem("hT_ready"), sem("hT_used")
        xl_ready, xlT_ready, xlTs_ready = sem("xl_ready"), sem("xlT_ready"), sem("xlTs_ready")
        rl_ready, gates_ready = sem("rl_ready"), sem("gates_ready")

        x3T = [SM[:, 512 * i:512 * i + 512] for i in range(2)]
        part = [[SM[:, 1024 + 768 * i + 256 * j:1280 + 768 * i + 256 * j].bitcast(BF16) for j in range(3)] for i in range(2)]
        part2 = [[R2[:, 768 * i + 256 * j:768 * i + 256 * j + 256].bitcast(BF16) for j in range(3)] for i in range(2)]
        rest = [SM[:, 2560 + 512 * i:3072 + 512 * i] for i in range(2)]
        VN = sb("VN", [P, NT, NH, DHP])
        VD = sb("VD", [P, 2, NH, DHP])
        x2_ready = sem("x2_ready")
        x3_ready, x3T_ready, x3Ts_ready = sem("x3_ready"), sem("x3T_ready"), sem("x3Ts_ready")
        qkv_ready, q_split, k_split, v_copied = sem("qkv_ready"), sem("q_split"), sem("k_split"), sem("v_copied")
        q_out, k_out = [sem("q_out0"), sem("q_out1")], [sem("k_out0"), sem("k_out1")]

        o = NTOK
        CW = 2 * P
        QS = [BIG[0:48, o + 2048 * i:o + 2048 * i + 2048].bitcast(BF16).rearrange("p (h t) -> p h t", h=NH) for i in range(2)]
        o += 4096
        KS = [BIG[0:48, o + 3072 * i:o + 3072 * i + 3072].bitcast(BF16).rearrange("p (h t) -> p h t", h=NH) for i in range(2)]
        o += 6144
        assert o <= 4 * NTOK
        SM2 = sb("SM2", [P, (2 + 3 * R3 - 8) * 512])
        tiles4 = [a[:, 512 * i:512 * i + 512].rearrange("p (h k) -> p h k", h=HQ)
                  for a, n in ((SM, 8), (SM2, 3 * R3 - 6)) for i in range(n)]
        D4, P4, PT4, PC4 = tiles4[0:2], tiles4[2:2 + R3], tiles4[2 + R3:2 + 2 * R3], tiles4[2 + 2 * R3:2 + 3 * R3]
        AO = [R2[:, 512 * i:512 * i + 512].rearrange("p (t c) -> p t c", t=TG) for i in range(2)]
        aoT = R2[:, 1024:1536].rearrange("p (t c) -> p t c", t=TG)
        OT = [R2[:, 1536 + 128 * i:1664 + 128 * i] for i in range(2)]
        ot_copied, o_turned, zero_bank = sem("ot_copied"), sem("o_turned"), sem("zero_bank")
        NGT_t = sb("NGT", [P, HQ * P])
        NGT = NGT_t[:, :].rearrange("p (h k) -> p h k", h=HQ)
        zero_col = cst[:, 4:5]
        BLT, G2 = sb("BLT", [P, E]), sb("G2", [P, NT, E])
        NM = sb("NM", [P, 2, HQ])
        RC = sb("RC", [P, NH])
        q_in, k_in = [sem("q_in0"), sem("q_in1")], [sem("k_in0"), sem("k_in1")]
        s_ready, s_used, d_ready, p_ready = sem("s_ready"), sem("s_used"), sem("d_ready"), sem("p_ready")
        pt_ready, pts_ready, pc_ready, pv_ready = sem("pt_ready"), sem("pts_ready"), sem("pc_ready"), sem("pv_ready")
        vd_ready, ao_ready, aoT_ready, aoTs_ready, at_ready, x3_done = sem("vd_ready"), sem("ao_ready"), sem("aoT_ready"), sem("aoTs_ready"), sem("at_ready"), sem("x3_done")

        XF = BIG[:, NTOK:2 * NTOK].rearrange("p (t c) -> p t c", t=NT)
        xfT = [SM[:, 512 * i:512 * i + 512] for i in range(2)]
        th_t = [SM[:, 1024 + 512 * i:1536 + 512 * i] for i in range(2)]
        t1_t = [SM[:, 2048 + 512 * i:2560 + 512 * i] for i in range(2)]
        hf_t = [BIG[:, 2 * NTOK + 2048 * i:2 * NTOK + 2048 * i + 2048] for i in range(2)]
        xf_ready, xfT_ready, xfTs_ready, gu_ready, th_ready, gu_used, ff_ready, ff_used = (
            sem("xf_ready"), sem("xfT_ready"), sem("xfTs_ready"), sem("gu_ready"), sem("th_ready"), sem("gu_used"),
            sem("ff_ready"), sem("ff_used"))

        MW1 = BIG[:, NTOK:2 * NTOK].rearrange("p (e h) -> p e h", e=E)
        MW2 = BIG[:, 2 * NTOK:3 * NTOK].rearrange("p (e f d) -> p e f d", e=E, f=NF)
        HE = [BIG[:, 3 * NTOK + 2048 * i:3 * NTOK + 2048 * i + 2048].rearrange("p (f t) -> p f t", f=NF) for i in range(2)]
        GT = sb("GT", [P, NT, E])
        LE = sb("LE", [P, NT, E])
        B1C = sb("B1C", [P, E * NF])
        BLR = sb("BLR", [P, E])
        gTt = [SM[0:E, 512 * i:512 * i + 512] for i in range(2)]
        b1_mm, b1_done, w1_scaled = sem("b1_mm"), sem("b1_done"), sem("w1_scaled")
        gT_ready, gTs_ready, gb_ready, gb_used = sem("gT_ready"), sem("gTs_ready"), sem("gb_ready"), sem("gb_used")
        up_ready, act_ready, dn_ready, dn_used = sem("up_ready"), sem("act_ready"), sem("dn_ready"), sem("dn_used")
        st_out = sem("st_out")

        @block.sync
        def _(sp):
            sp.dma_start(M0[:, :], mat0).then_inc(ld_m0, 16)
            for i in range(4):
                sp.dma_start(ACC[:, 8 * i:8 * i + 8, :], x_v[:, 8 * i:8 * i + 8, :]).then_inc(ld_x[i], 16)
            for dst, src in ((CO, cols), (W2S, w2s), (BQK, bqk), (B1S, b1s), (B2E, moe_b2)):
                sp.dma_start(dst[:, :], src).then_inc(ld_small, 16)
            sp.dma_start(RO[:, :], rows.partition_broadcast(P)).then_inc(ld_small, 16)
            sp.dma_start(M1[:, :], mat1).then_inc(ld_m1, 16)
            sp.dma_start(M2[:, :], mat2).then_inc(ld_m2, 16)
            for g in range(NG):
                for (split, parts, dram, went) in ((q_split, part, q_dram, q_out), (k_split, part2, k_dram, k_out)):
                    sp.wait_ge(split, g + 1)
                    for j in range(3):
                        sp.dma_start(dram[j].rearrange("h d t -> (h d) t")[:, g * GW:(g + 1) * GW],
                                     parts[g % 2][j]).then_inc(went[g % 2], 16)
            for r in range(2):
                sp.wait_ge(q_out[r], 16 * 3 * NG // 2)
                sp.wait_ge(k_out[r], 16 * 3 * NG // 2)
            meet(sp, 4)
            for i in range(NT // 2):
                if i >= 2:
                    sp.wait_ge(s_ready, 2 * NQ * (i - 1))
                first = i % (NT // 2 // B) == 0
                for p in range(NPART):
                    sp.dma_start(QS[i % 2][8 * p:8 * p + 8, :, :],
                                 q_dram[QP[p]].rearrange("h d t -> d h t")[:, :, i * CW:(i + 1) * CW]).then_inc(q_in[i % 2], 16)
                    lo = P if first else 0
                    sp.dma_start(KS[i % 2][8 * p:8 * p + 8, :, lo:3 * P],
                                 k_dram[KP[p]].rearrange("h d t -> d h t")[:, :, i * CW - P + lo:(i + 1) * CW]).then_inc(k_in[i % 2], 16)
            meet(sp, 6)
            sp.dma_start(MW1, moe_w1).then_inc(ld_moe, 16)
            sp.dma_start(MW2, moe_w2).then_inc(ld_moe, 16)
            for g in range(NG):
                sp.wait_ge(dn_used, TG * E * (g + 1))
                sp.dma_start(out_v[:, g * TG:(g + 1) * TG, :], ACC[:, g * TG:(g + 1) * TG, :]).then_inc(st_out, 16)
            sp.wait_ge(st_out, 16 * NG)

        @block.gpsimd
        def _(pool):
            nc.gpsimd.memset(MH[:, :], -0.5).then_inc(pool_step, 1)
            pool.wait_ge(pool_step, 1)

            def rstd(n):
                pool.wait_ge(var_ready, n)
                nc.gpsimd.tensor_tensor(RS[:, :], VE[:, :], MH[:, :], ALU.pow).then_inc(rstd_ready, 1)

            nc.gpsimd.memset(XT[:, :, 0:1], 0.0).then_inc(fills, 1)
            nc.gpsimd.memset(XN[:, :, C:C + 1], 1.0).then_inc(fills, 1)
            nc.gpsimd.memset(VN[:, :, :, DH:DHP], 1.0).then_inc(fills, 1)
            for n in range(1, 8):
                rstd(n)
            meet(pool, 4)
            for i in range(NT * NQ):
                pool.wait_ge(pts_ready, i + 1)
                if i >= R3:
                    pool.wait_ge(pv_ready, i - R3 + 1)
                nc.gpsimd.tensor_tensor(PC4[i % R3], PT4[i % R3], m2["maskcur"].unsqueeze(1).broadcast_to([P, HQ, P]),
                                        ALU.mult).then_inc(pc_ready, 1)
            rstd(8)

        @block.tensor
        def _(pe):
            mm, tr = nc.tensor.matmul, nc.tensor.transpose

            def transposes(dst, src4, n=P):
                for t in range(TG):
                    last = tr(dst[0:n, t * P:(t + 1) * P], src4[:, t, 0:n], ident)
                return last

            pe.wait_ge(ld_m0, 16)
            pe.wait_ge(col_ready, 2)
            mm(bank[2][0:64, 0:1], m0["w1b"], col_t[:, 3:4], start=True, stop=True).then_inc(pre_mm, 1)
            for g in range(NG + 2):
                if g < NG:
                    pe.wait_ge(xh_ready, g + 1)
                    if g >= 1:
                        pe.wait_ge(xt_ready, g)
                    transposes(bank[0], XH[:, g * TG:(g + 1) * TG, :]).then_inc(xhT_ready, 1)
                    if g >= 1:
                        pe.wait_ge(xnTs_ready, g)
                    transposes(bank[1], XN[:, g * TG:(g + 1) * TG, :]).then_inc(xnT_ready, 1)
                if 1 <= g <= NG:
                    i = g - 1
                    pe.wait_ge(xnTs_ready, i + 1)
                    if i == 0:
                        pe.wait_ge(pre_ready, 1)
                    if i >= 1:
                        pe.wait_ge(h_ready, i)
                    mm(bank[2][0:64, :], m0["w1a"], xnT[i % 2], start=True, stop=True).then_inc(h1_ready, 1)
                    pe.wait_ge(mix_ready, i + 1)
                    if i >= 1:
                        pe.wait_ge(kv_used, i)
                        pe.wait_ge(r_ready, i)
                    for j, w in enumerate(("Wk", "Wv", "Wr")):
                        last = mm(bank[4 + j], m0[w], mixed[i % 2][j], start=True, stop=True)
                    last.then_inc(kvr_ready, 1)
                if g >= 2:
                    i = g - 2
                    pe.wait_ge(h_ready, i + 1)
                    if i == 0:
                        pe.wait_ge(col_ready, 3)
                    if i >= 1:
                        pe.wait_ge(logit_used, i)
                    for t in range(TG):
                        last = mm(bank[3][:, t * 64:(t + 1) * 64], hT[i % 2][:, t * P:(t + 1) * P], W2S[:, :],
                                  start=True, stop=True)
                    last.then_inc(logit_ready, 1)
                    pe.wait_ge(rw_ready, i + 1)
                    if i >= 1:
                        pe.wait_ge(y_used, i)
                    for t in range(TG):
                        last = mm(bank4[7][:, t, :], rw[i % 2][:, t * P:(t + 1) * P], m0["Wo"], start=True, stop=True)
                    last.then_inc(y_ready, 1)
            meet(pe, 1)
            pe.wait_ge(slot_dve, 1)
            for b in range(B):
                for t in range(NT // B):
                    n = b * (NT // B) + t
                    last = mm(bank[b][64 * b:64 * b + 64, 0:C + 1], LG[:, n, :], XN[:, n, :],
                              start=(t == 0), stop=(t == NT // B - 1))
            last.then_inc(slot_pe, 1)
            pe.wait_ge(ld_m1, 16)
            for j in range(2):
                mm(bank[2][:, j * P:(j + 1) * P], m0["slotT2"], m1["Whh"][:, j * P:(j + 1) * P], start=(j == 0), stop=False,
                   skip_group_check=True)
            mm(bank[3][:, 0:P], m0["slotT2"], m1["Whh"][:, 256:384], start=True, stop=True)
            pe.wait_ge(slot_dve, 2)
            tr(bank[4][:, 0:P], si_t, ident).then_inc(slot_pe, 1)
            pe.wait_ge(slot_act, 1)
            for j in range(2):
                mm(bank[2][:, j * P:(j + 1) * P], siT_t, m1["Wih"][:, j * P:(j + 1) * P], start=False, stop=(j == 1),
                   skip_group_check=True)
            mm(bank[3][:, P:2 * P], siT_t, m1["Wih"][:, 256:384], start=True, stop=True).then_inc(slot_pe, 1)
            pe.wait_ge(slot_dve, 5)
            tr(bank[4][:, 0:P], sn_t, ident).then_inc(slot_pe, 1)
            pe.wait_ge(slot_act, 4)
            mm(bank[5][0:32, 0:P], m1["wq"], snT_t, start=True, stop=True)
            mm(bank[5][0:32, P:2 * P], m1["wk"], snT_t, start=True, stop=True)
            mm(bank[6][:, 0:P], snT_t, m1["wv"], start=True, stop=True).then_inc(slot_pe, 1)
            pe.wait_ge(slot_dve, 6)
            mm(bank[7][:, 0:P], qk_t[:, 0, :], qk_t[:, 1, :], start=True, stop=True).then_inc(slot_pe, 1)
            pe.wait_ge(slot_dve, 8)
            tr(bank[4][:, 0:P], pe_t, ident).then_inc(slot_pe, 1)
            pe.wait_ge(slot_act, 6)
            mm(bank[6][:, P:2 * P], pT_t, vv_t, start=True, stop=True).then_inc(slot_pe, 1)
            pe.wait_ge(slot_dve, 9)
            tr(bank[4][:, 0:P], yy_t, ident).then_inc(slot_pe, 1)
            pe.wait_ge(slot_act, 7)
            mm(bank[5][:, 0:P], m1["wvp"], yT_t, start=True, stop=True).then_inc(slot_pe, 1)
            pe.wait_ge(slot_act, 8)
            for b in range(B):
                last = mm(bank[0][0:64, b * P:(b + 1) * P], svT_t[:, 64 * b:64 * b + 64], m1["wo"], start=True, stop=True)
            last.then_inc(slot_pe, 1)
            meet(pe, 2)
            for g in range(NG + 1):
                if g < NG:
                    if g >= 1:
                        pe.wait_ge(alphaTs_ready, g)
                    transposes(bank[0], LG[:, g * TG:(g + 1) * TG, :], n=SLOTS).then_inc(alphaT_ready, 1)
                if g >= 1:
                    i = g - 1
                    pe.wait_ge(alphaTs_ready, i + 1)
                    if i >= 1:
                        pe.wait_ge(x1_ready, i)
                    for t in range(TG):
                        last = mm(bank4[1][:, t, :], aT[i % 2][:, t * P:(t + 1) * P], SVO[:, i // GB, :], start=True, stop=True)
                    last.then_inc(o_ready, 1)
            pe.wait_ge(ld_m2, 16)
            for g in range(NG + 3):
                if g < NG:
                    pe.wait_ge(xr2_ready, g + 1)
                    if g >= 1:
                        pe.wait_ge(trs_ready, g)
                    transposes(bank[2], XR[:, g * TG:(g + 1) * TG, :]).then_inc(tr_ready, 1)
                if 1 <= g <= NG:
                    i = g - 1
                    pe.wait_ge(trs_ready, i + 1)
                    if i >= 1:
                        pe.wait_ge(gate_ready, i)
                    for j, w in enumerate(("Wg", "Wv", "Wd")):
                        last = mm(bank[3 + j], m2[w], xrT[i % 2], start=True, stop=True)
                    last.then_inc(gvd_ready, 1)
                if 2 <= g <= NG + 1:
                    i = g - 2
                    pe.wait_ge(scan_ready, i + 1)
                    if i >= 1:
                        pe.wait_ge(hT_used, i)
                    for t in range(TG):
                        last = tr(bank4[6][:, t, :], hh_t[i % 2][:, t * P:(t + 1) * P], ident)
                    last.then_inc(hT_ready, 1)
            for g in range(NG):
                pe.wait_ge(xl_ready, g + 1)
                if g >= 1:
                    pe.wait_ge(xlTs_ready, g)
                transposes(bank[7], XL[:, g * TG:(g + 1) * TG, :]).then_inc(xlT_ready, 1)
            mm(bank[1][:, 0:E], co["rln_b"].broadcast_to([P, P]), m2["router"], start=True, stop=True)
            pe.wait_ge(col_ready, 4)
            for t in range(NT):
                if t % TG == 0:
                    pe.wait_ge(xlTs_ready, t // TG + 1)
                last = mm(bank[0][:, t * E:(t + 1) * E], XLT[:, t * P:(t + 1) * P], BLR[:, :], start=True, stop=True)
            last.then_inc(rl_ready, 1)
            meet(pe, 3)
            for g in range(NG + 1):
                if g < NG:
                    pe.wait_ge(x3_ready, g + 1)
                    if g >= 1:
                        pe.wait_ge(x3Ts_ready, g)
                    transposes(bank[0], XR[:, g * TG:(g + 1) * TG, :]).then_inc(x3T_ready, 1)
                if g >= 1:
                    i = g - 1
                    pe.wait_ge(x3Ts_ready, i + 1)
                    if i >= 2:
                        pe.wait_ge(q_split, i - 1)
                        pe.wait_ge(k_split, i - 1)
                        pe.wait_ge(v_copied, i - 1)
                    o = 1 + 3 * (i % 2)
                    mm(bank[o], m2["Wqkv"][:, 0:P], x3T[i % 2], start=True, stop=True)
                    mm(bank[o + 1], m2["Wqkv"][:, P:2 * P], x3T[i % 2], start=True, stop=True)
                    for t in range(TG):
                        last = mm(bank4[o + 2][:, t, :], x3T[i % 2][:, t * P:(t + 1) * P], m2["Wqkv"][:, 2 * P:3 * P],
                                  start=True, stop=True)
                    last.then_inc(qkv_ready, 1)
            meet(pe, 4)

            def scores(i):
                c, hq = i // NQ, i % NQ
                r = (c // 2) % 2
                if i % (2 * NQ) == 0:
                    n = 16 * NPART * (c // 4 + 1)
                    pe.wait_ge(q_in[r], n)
                    pe.wait_ge(k_in[r], n)
                if i >= 2:
                    pe.wait_ge(d_ready, i - 1)
                first = c % (NT // B) == 0
                for h in range(HQ):
                    lo = P if first else 0
                    k0 = (c % 2) * P
                    last = mm(bank[2 * (i % 2) + h // 2][:, (h % 2) * 2 * P + lo:(h % 2 + 1) * 2 * P],
                              QS[r][:, hq * HQ + h, (c % 2) * P:(c % 2 + 1) * P],
                              KS[r][:, hq * HQ + h, k0 + lo:k0 + 2 * P], start=True, stop=True)
                last.then_inc(s_ready, 1)

            def weights_turn(i):
                pe.wait_ge(p_ready, i + 1)
                if i >= 2:
                    pe.wait_ge(pts_ready, i - 1)
                for h in range(HQ):
                    last = tr(bank[4 + i % 2][:, h * P:(h + 1) * P], P4[i % R3][:, h, :], ident)
                last.then_inc(pt_ready, 1)

            def weighted(i):
                c, hq = i // NQ, i % NQ
                first = c % (NT // B) == 0
                pe.wait_ge(pc_ready, i + 1)
                if i >= 1:
                    pe.wait_ge(ot_copied, i)
                if hq == 0 and not first:
                    pe.wait_ge(vd_ready, c + 1)
                for h in range(HQ):
                    hh = hq * HQ + h
                    dst = bank[6][32 * h:32 * h + DHP, 0:P]
                    if first:
                        last = mm(dst, VN[:, c, hh, :], PT4[i % R3][:, h, :], start=True, stop=True)
                    else:
                        mm(dst, VN[:, c - 1, hh, :], PT4[i % R3][:, h, :], start=True, stop=False)
                        last = mm(dst, VD[:, c % 2, hh, :], PC4[i % R3][:, h, :], start=False, stop=True)
                last.then_inc(pv_ready, 1)

            def sums_turn(i):
                c, hq = i // NQ, i % NQ
                pe.wait_ge(ot_copied, i + 1)
                if hq == 0 and c >= 1:
                    pe.wait_ge(ao_ready, c)
                tr(bank[7][:, hq * P:(hq + 1) * P], OT[i % 2], ident).then_inc(o_turned, 1)

            def out_proj(g):
                pe.wait_ge(ao_ready, TG * (g + 1))
                for t in range(TG):
                    last = tr(bank4[6][:, t, :], AO[g % 2][:, t, :], ident)
                last.then_inc(aoT_ready, 1)

            def out_proj2(g):
                pe.wait_ge(aoTs_ready, g + 1)
                for t in range(TG):
                    last = mm(bank4[6][:, t, :], aoT[:, t, :], m2["Wo"], start=True, stop=True)
                last.then_inc(at_ready, 1)

            N = NT * NQ
            NP = TG * NQ
            pe.wait_ge(zero_bank, 1)
            for i in range(N + 8):
                if i < N:
                    scores(i)
                if 2 <= i <= N + 1:
                    weights_turn(i - 2)
                if 5 <= i <= N + 4:
                    sums_turn(i - 5)
                if i >= 7 and (i - 7) % NP == NP - 1:
                    out_proj((i - 7) // NP)
                    out_proj2((i - 7) // NP)
                    pe.wait_ge(x3_done, (i - 7) // NP + 1)
                if 4 <= i <= N + 3:
                    weighted(i - 4)
            meet(pe, 5)

            def gate_up(i):
                for f in range(NF):
                    n = i * NF + f
                    if n >= 2:
                        pe.wait_ge(gu_used, n - 1)
                    mm(bank[1 + 2 * (n % 2)], m2["Wgate"][:, f * P:(f + 1) * P], xfT[i % 2], start=True, stop=True)
                    mm(bank[2 + 2 * (n % 2)], m2["Wup"][:, f * P:(f + 1) * P], xfT[i % 2], start=True,
                       stop=True).then_inc(gu_ready, 1)

            for g in range(NG + 2):
                if g < NG:
                    pe.wait_ge(xf_ready, g + 1)
                    if g >= 1:
                        pe.wait_ge(xfTs_ready, g)
                    transposes(bank[0], XF[:, g * TG:(g + 1) * TG, :]).then_inc(xfT_ready, 1)
                if 1 <= g <= NG:
                    pe.wait_ge(xfTs_ready, g)
                    gate_up(g - 1)
                if g >= 2:
                    i = g - 2
                    pe.wait_ge(gu_used, NF * (i + 1))
                    if i >= 2:
                        pe.wait_ge(ff_used, i - 1)
                    for t in range(TG):
                        for f in range(NF):
                            last = mm(bank4[5 + i % 2][:, t, :], hf_t[i % 2][:, f * GW + t * P:f * GW + (t + 1) * P],
                                      m2["Wout"][:, f * P:(f + 1) * P], start=(f == 0), stop=(f == NF - 1))
                    last.then_inc(ff_ready, 1)
            meet(pe, 6)
            pe.wait_ge(ld_moe, 32)
            for e in range(E):
                for f in range(NF):
                    last = mm(bank[0][:, e * NF + f:e * NF + f + 1], MW1[:, e, f * P:(f + 1) * P], co["elb"][:, e:e + 1],
                              start=True, stop=True)
            last.then_inc(b1_mm, 1)
            for g in range(NG):
                if g >= 1:
                    pe.wait_ge(gTs_ready, g)
                transposes(bank[7], GT[:, g * TG:(g + 1) * TG, :], n=E).then_inc(gT_ready, 1)
                pe.wait_ge(gTs_ready, g + 1)
                if g >= 1:
                    pe.wait_ge(gb_used, g)
                for t in range(TG):
                    last = mm(bank4[6][:, t, :], gTt[g % 2][:, t * P:(t + 1) * P], B2E[:, :], start=True, stop=True)
                last.then_inc(gb_ready, 1)

            def up(k):
                g, e = k // E, k % E
                if k < E:
                    pe.wait_ge(w1_scaled, e + 1)
                for f in range(NF):
                    n = k * NF + f
                    if n < 4:
                        pe.wait_ge(b1_done, 1)
                    if n >= 4:
                        pe.wait_ge(act_ready, n - 3)
                    mm(bank[n % 4], MW1[:, e, f * P:(f + 1) * P], XLT[:, g * GW:(g + 1) * GW], start=True,
                       stop=True).then_inc(up_ready, 1)

            def down(k):
                g, e = k // E, k % E
                pe.wait_ge(act_ready, NF * (k + 1))
                if k >= 2:
                    pe.wait_ge(dn_used, TG * (k - 1))
                for t in range(TG):
                    for f in range(NF):
                        last = mm(bank4[4 + k % 2][:, t, :], HE[k % 2][:, f, t * P:(t + 1) * P], MW2[:, e, f, :],
                                  start=(f == 0), stop=(f == NF - 1))
                last.then_inc(dn_ready, 1)

            for k in range(NG * E + 1):
                if k < NG * E:
                    up(k)
                if k >= 1:
                    down(k - 1)

        @block.scalar
        def _(act):
            A = nc.scalar.activation
            act.wait_ge(ld_small, 16 * 6)
            A(col_t[:, 4:5], co["decay"], ACT.Tanh, scale=0.5).then_inc(act_pre, 1)
            A(col_t[:, 1:2], co["first"], ACT.Exp).then_inc(act_pre, 1)
            A(col_t[:, 2:3], ro["tau"], ACT.Abs).then_inc(act_pre, 1)
            act.wait_ge(pre_ready, 1)
            for g in range(NG + 1):
                if g < NG:
                    b, o = g // GB, 1 + (g % GB) * GW
                    act.wait_ge(xhT_ready, g + 1)
                    A(XT[:, b, o:o + GW], bank[0], ACT.Identity, bias=co["ln_b"], scale=co["ln_w"]).then_inc(xt_ready, 1)
                    act.wait_ge(xnT_ready, g + 1)
                    if g >= 2:
                        act.wait_ge(h1_ready, g - 1)
                    nc.scalar.copy(xnT[g % 2], bank[1]).then_inc(xnTs_ready, 1)
                if g >= 1:
                    i = g - 1
                    act.wait_ge(h1_ready, i + 1)
                    if i >= 2:
                        act.wait_ge(logit_ready, i - 1)
                    A(hT[i % 2], bank[2][0:64, :], ACT.Gelu, bias=B1S[:, :]).then_inc(h_ready, 1)
                    act.wait_ge(kvr_ready, i + 1)
                    if i >= 2:
                        act.wait_ge(rw_ready, i - 1)
                    A(rT[i % 2], bank[6], ACT.Tanh, scale=0.5).then_inc(r_ready, 1)
            act.wait_ge(v8_ready, 1)
            A(LG, LG, ACT.Exp).then_inc(v8_ready, 1)
            act.wait_ge(slot_pe, 2)
            nc.scalar.copy(siT_t, bank[4][:, 0:P]).then_inc(slot_act, 1)
            act.wait_ge(slot_dve, 3)
            A(rz_t, rz_t, ACT.Tanh, scale=0.5).then_inc(slot_act, 1)
            act.wait_ge(slot_dve, 4)
            A(n_t, n_t, ACT.Tanh).then_inc(slot_act, 1)
            act.wait_ge(slot_pe, 4)
            nc.scalar.copy(snT_t, bank[4][:, 0:P]).then_inc(slot_act, 1)
            act.wait_ge(slot_dve, 7)
            A(pe_t, sc_t, ACT.Exp, bias=cst[:, 2:3], accum_out=cst[:, 3:4]).then_inc(slot_act, 1)
            act.wait_ge(slot_pe, 7)
            nc.scalar.copy(pT_t, bank[4][:, 0:P]).then_inc(slot_act, 1)
            act.wait_ge(slot_pe, 9)
            nc.scalar.copy(yT_t, bank[4][:, 0:P]).then_inc(slot_act, 1)
            act.wait_ge(slot_pe, 10)
            A(svT_t, bank[5][:, 0:P], ACT.Identity, bias=co["bvp"]).then_inc(slot_act, 1)
            for g in range(NG):
                act.wait_ge(alphaT_ready, g + 1)
                if g >= 2:
                    act.wait_ge(o_ready, g - 1)
                nc.scalar.copy(aT[g % 2], bank[0][0:64, :]).then_inc(alphaTs_ready, 1)
            for g in range(NG + 1):
                if g < NG:
                    act.wait_ge(tr_ready, g + 1)
                    if g >= 2:
                        act.wait_ge(gvd_ready, g - 1)
                    A(xrT[g % 2], bank[2], ACT.Identity, bias=zero_col, scale=co["w_mix"]).then_inc(trs_ready, 1)
                if g >= 1:
                    i = g - 1
                    act.wait_ge(gvd_ready, i + 1)
                    if i >= 2:
                        act.wait_ge(scan_ready, i - 1)
                    A(tg_t[i % 2], bank[3], ACT.Tanh, scale=0.5, bias=cst[:, 0:1])
                    A(tv_t[i % 2], bank[4], ACT.Tanh, bias=co["bv"])
                    A(ta_t[i % 2], bank[5], ACT.Tanh, scale=0.5, bias=cst[:, 1:2]).then_inc(gate_ready, 1)
            for g in range(NG):
                act.wait_ge(xlT_ready, g + 1)
                nc.scalar.copy(XLT[:, g * GW:(g + 1) * GW], bank[7]).then_inc(xlTs_ready, 1)
            act.wait_ge(gates_ready, 1)
            A(LE[:, :, :], LE[:, :, :], ACT.Exp).then_inc(gates_ready, 1)
            for g in range(NG + 1):
                if g < NG:
                    act.wait_ge(x3T_ready, g + 1)
                    if g >= 2:
                        act.wait_ge(qkv_ready, g - 1)
                    A(x3T[g % 2], bank[0], ACT.Identity, bias=zero_col, scale=co["w_attn"]).then_inc(x3Ts_ready, 1)
                if g >= 1:
                    i = g - 1
                    o = 1 + 3 * (i % 2)
                    act.wait_ge(qkv_ready, i + 1)
                    if i >= 2:
                        act.wait_ge(q_out[i % 2], 48 * (i // 2))
                        act.wait_ge(k_out[i % 2], 48 * (i // 2))
                    nc.scalar.copy(part[i % 2][0], bank[o]).then_inc(q_hi, 1)
                    nc.scalar.copy(part2[i % 2][0], bank[o + 1]).then_inc(k_hi, 1)
                    nc.scalar.copy(VN[:, i * TG:(i + 1) * TG, :, 0:DH],
                                   bank[o + 2].rearrange("p (t h d) -> p t h d", t=TG, h=NH)).then_inc(v_copied, 1)
            SC = DH ** -0.5

            def exps(i):
                act.wait_ge(d_ready, i + 1)
                if i >= R3:
                    act.wait_ge(pt_ready, i - R3 + 1)
                A(P4[i % R3], D4[i % 2], ACT.Exp, scale=SC).then_inc(p_ready, 1)

            def turned(i):
                act.wait_ge(pt_ready, i + 1)
                if i >= R3:
                    act.wait_ge(pv_ready, i - R3 + 1)
                    act.wait_ge(pc_ready, i - R3 + 1)
                nc.scalar.copy(PT4[i % R3], bank4[4 + i % 2]).then_inc(pts_ready, 1)

            N = NT * NQ
            for i in range(N + 8):
                if i >= 7 and (i - 7) % (TG * NQ) == TG * NQ - 1:
                    g = (i - 7) // (TG * NQ)
                    act.wait_ge(aoT_ready, g + 1)
                    nc.scalar.copy(aoT, bank4[6]).then_inc(aoTs_ready, 1)
                if i < N:
                    exps(i)
                if 2 <= i <= N + 1:
                    turned(i - 2)
                if 4 <= i <= N + 3:
                    j = i - 4
                    act.wait_ge(pv_ready, j + 1)
                    if j >= 2:
                        act.wait_ge(o_turned, j - 1)
                    nc.scalar.copy(OT[j % 2], bank[6][:, 0:P]).then_inc(ot_copied, 1)
            for g in range(NG + 1):
                if g < NG:
                    act.wait_ge(xfT_ready, g + 1)
                    if g >= 2:
                        act.wait_ge(gu_ready, NF * (g - 1))
                    A(xfT[g % 2], bank[0], ACT.Identity, bias=zero_col, scale=co["w_ffn"]).then_inc(xfTs_ready, 1)
                if g >= 1:
                    for f in range(NF):
                        n = (g - 1) * NF + f
                        act.wait_ge(gu_ready, n + 1)
                        if n >= 2:
                            act.wait_ge(gu_used, n - 1)
                        A(th_t[n % 2], bank[1 + 2 * (n % 2)], ACT.Tanh, scale=0.5).then_inc(th_ready, 1)
            meet(act, 6)
            for g in range(NG):
                act.wait_ge(gT_ready, g + 1)
                if g >= 2:
                    act.wait_ge(gb_ready, g - 1)
                nc.scalar.copy(gTt[g % 2], bank[7][0:E, :]).then_inc(gTs_ready, 1)
            act.wait_ge(b1_done, 1)
            for k in range(NG * E):
                e = k % E
                if k >= 2:
                    act.wait_ge(dn_ready, k - 1)
                for f in range(NF):
                    n = k * NF + f
                    act.wait_ge(up_ready, n + 1)
                    A(HE[k % 2][:, f, :], bank[n % 4], ACT.Gelu, bias=B1C[:, e * NF + f:e * NF + f + 1]).then_inc(act_ready, 1)

        @block.vector
        def _(dve):
            V = nc.vector
            st = Steps(dve, dve_step)

            def statistics(src, rms, eps, n, first=0, tiles=NT):
                for t in range(tiles):
                    if src is ACC and n == 1 and t % 8 == 0:
                        dve.wait_ge(ld_x[t // 8], 16)
                    st(V.bn_stats(ST[:, t, :], src[:, t, 0:C]))
                st.wait()
                for t in range(tiles):
                    st(V.bn_aggr(MV[:, t, :], ST[:, t, :]))
                st.wait()
                root_input(rms, eps, n, tiles)

            def root_input(rms, eps, n, tiles=NT):
                if n >= 2:
                    dve.wait_ge(rstd_ready, n - 1)
                m, v = MV[:, 0:tiles, 0], MV[:, 0:tiles, 1]
                if rms:
                    st(V.tensor_tensor(VE[:, 0:tiles], m, m, ALU.mult))
                    st.wait()
                    st(V.tensor_tensor(VE[:, 0:tiles], VE[:, 0:tiles], v, ALU.add))
                    st.wait()
                    V.tensor_scalar(VE[:, 0:tiles], VE[:, 0:tiles], eps, None, ALU.add).then_inc(var_ready, 1)
                elif tiles == NT:
                    V.tensor_scalar(VE[:, :], v, eps, None, ALU.add).then_inc(var_ready, 1)
                else:
                    V.tensor_scalar(VE[:, 0:tiles], v, eps, None, ALU.add).then_inc(var_ready, 1)

            def normalise(dst, src, t):
                return V.tensor_scalar(dst[:, t, 0:C], src[:, t, 0:C], MV[:, t, 0:1], RS[:, t:t + 1], ALU.subtract, ALU.mult)

            def scaled(dst, src, t):
                return V.tensor_scalar(dst[:, t, 0:C], src[:, t, 0:C], RS[:, t:t + 1], None, ALU.mult)

            dve.wait_ge(ld_small, 16 * 6)
            dve.wait_ge(act_pre, 3)
            st(V.tensor_scalar(col_t[:, 0:1], col_t[:, 4:5], 0.5, 0.5, ALU.mult, ALU.add))
            st(V.tensor_scalar(cst[:, 0:1], co["bg"], 0.5, None, ALU.mult))
            st(V.tensor_scalar(cst[:, 1:2], co["bd"], 0.5, None, ALU.mult))
            st(V.memset(cst[:, 4:5], 0.0))
            st(V.memset(NGT_t[:, :], NEG))
            dve.wait_ge(ld_m0, 16)
            st(V.tensor_reduce(col_t[:, 5:6], m0["slotT"], AX_X, ALU.add))
            st.wait()
            st(V.tensor_scalar(col_t[:, 6:7], col_t[:, 2:3], 0.1, None, ALU.add))
            st(V.tensor_copy(DEC[:, :], col_t[:, 0:1].broadcast_to([P, GW])))
            V.tensor_scalar(col_t[:, 3:4], col_t[:, 5:6], 1.0 / SLOTS, None, ALU.mult).then_inc(col_ready, 2)
            st.wait()
            st(V.reciprocal(col_t[:, 7:8], col_t[:, 6:7]))
            st.wait()
            st(V.tensor_scalar(ro["b2"], ro["b2"], col_t[:, 7:8], None, ALU.mult))
            V.tensor_scalar(W2S[:, :], W2S[:, :], col_t[0:64, 7:8], None, ALU.mult).then_inc(col_ready, 1)
            dve.wait_ge(pre_mm, 1)
            V.tensor_tensor(B1S[:, :], B1S[:, :], bank[2][0:64, 0:1], ALU.add).then_inc(pre_ready, 1)
            dve.wait_ge(fills, 3)
            statistics(ACC, False, LN_EPS, 1)
            dve.wait_ge(rstd_ready, 1)
            for t in range(NT):
                st(normalise(XN, ACC, t))
            st.wait()
            st(V.tensor_tensor(ACC[:, :, :], ACC[:, :, :], XN[:, :, 0:C], ALU.add))
            statistics(XN, False, LN_EPS, 2)
            dve.wait_ge(rstd_ready, 2)
            for g in range(NG + 3):
                if g < NG:
                    for t in range(TG):
                        last = normalise(XH, XN, g * TG + t)
                    last.then_inc(xh_ready, 1)
                if 1 <= g <= NG:
                    i = g - 1
                    b, o = i // GB, (i % GB) * GW
                    dve.wait_ge(xt_ready, i + 1)
                    if i >= 2:
                        dve.wait_ge(kvr_ready, i - 1)
                    if i >= 1:
                        dve.wait_ge(mix_ready, i)
                    prev, cur = XT[:, b, o:o + GW], XT[:, b, o + 1:o + 1 + GW]
                    st(V.tensor_tensor(dif[:, :], cur, prev, ALU.subtract))
                    st.wait()
                    for j, w in enumerate(("mk", "mv", "mr")):
                        last = V.scalar_tensor_tensor(out=mixed[i % 2][j], in0=dif[:, :], scalar=co[w], in1=prev,
                                                      op0=ALU.mult, op1=ALU.add)
                    last.then_inc(mix_ready, 1)
                if 2 <= g <= NG + 1:
                    i = g - 2
                    dve.wait_ge(kvr_ready, i + 1)
                    dve.wait_ge(r_ready, i + 1)
                    if i >= 2:
                        dve.wait_ge(y_ready, i - 1)
                    if i >= 1:
                        dve.wait_ge(rw_ready, i)
                    init = 0.0 if i % GB == 0 else SS[(i - 1) % 2][:, GW - 1:GW]
                    st(V.tensor_tensor_scan(SS[i % 2], DEC[:, :], bank[4], init, ALU.mult, ALU.add))
                    st.wait()
                    st(V.scalar_tensor_tensor(out=rw[i % 2], in0=SS[i % 2], scalar=col_t[:, 1:2], in1=bank[4],
                                              op0=ALU.mult, op1=ALU.add))
                    st.wait()
                    V.tensor_tensor(rw[i % 2], rw[i % 2], bank[5], ALU.mult).then_inc(kv_used, 1)
                    dve.wait_ge(kv_used, i + 1)
                    V.scalar_tensor_tensor(out=rw[i % 2], in0=rT[i % 2], scalar=1.0, in1=rw[i % 2],
                                           op0=ALU.add, op1=ALU.mult).then_inc(rw_ready, 1)
                    dve.wait_ge(logit_ready, i + 1)
                    sl = slice(i * TG, (i + 1) * TG)
                    V.tensor_tensor(LG[:, sl, :], bank[3][:, 0:TG * SLOTS].rearrange("p (t s) -> p t s", t=TG),
                                    ro["b2"].unsqueeze(1).broadcast_to([P, TG, SLOTS]), ALU.add).then_inc(logit_used, 1)
                    dve.wait_ge(logit_used, i + 1)
                    for t in range(i * TG, (i + 1) * TG):
                        st(V.max(V8[:, t, :], LG[:, t, :]))
                    st.wait()
                    for t in range(i * TG, (i + 1) * TG):
                        st(V.match_replace(LR[:, t, :], V8[:, t, :], LG[:, t, :], NEG))
                if g >= 3:
                    i = g - 3
                    dve.wait_ge(y_ready, i + 1)
                    sl = slice(i * TG, (i + 1) * TG)
                    V.scalar_tensor_tensor(out=ACC[:, sl, :], in0=bank4[7], scalar=0.5, in1=ACC[:, sl, :],
                                           op0=ALU.mult, op1=ALU.add).then_inc(y_used, 1)
            st.wait()
            dve.wait_ge(y_used, NG)
            st(V.tensor_tensor(LR, LR, LG, ALU.not_equal))
            st.wait()
            V.tensor_tensor(LG, LG, V8[:, :, 0:1].broadcast_to([P, NT, SLOTS]), ALU.subtract).then_inc(v8_ready, 1)
            dve.wait_ge(v8_ready, 1)
            V.memset(cst[:, 9:10], 0.0).then_inc(phase_done, 1)
            dve.wait_ge(v8_ready, 2)
            st(V.tensor_tensor(LG, LG, LR, ALU.mult))
            st.wait()
            st(V.tensor_reduce(rden_t[:, :], LG, AX_X, ALU.add))
            st.wait()
            st(V.reciprocal(rden_t[:, :], rden_t[:, :]))
            st.wait()
            V.tensor_tensor(LG, LG, rden_t[:, :].unsqueeze(2).broadcast_to([P, NT, SLOTS]), ALU.mult).then_inc(slot_dve, 1)
            dve.wait_ge(slot_pe, 1)
            for b in range(B):
                s = slice(64 * b, 64 * b + 64)
                st(V.tensor_scalar(cst[s, 5:6], bank[b][s, C:C + 1], 1e-8, None, ALU.add))
            st.wait()
            st(V.reciprocal(cst[:, 6:7], cst[:, 5:6]))
            st.wait()
            for b in range(B):
                s = slice(64 * b, 64 * b + 64)
                last = V.tensor_scalar(si_t[s, :], bank[b][s, 0:C], cst[s, 6:7], None, ALU.mult)
                if b == 0:
                    st(last)
            last.then_inc(slot_dve, 1)
            dve.wait_ge(slot_pe, 3)
            dve.wait_ge(ld_m1, 16)
            st(V.tensor_tensor(rz_t, bank[2][:, 0:256], ro["bih"][:, 0:256], ALU.add))
            st(V.tensor_tensor(hn_t, bank[3][:, 0:P], ro["bhh"][:, 256:384], ALU.add))
            st.wait()
            V.tensor_tensor(rz_t, rz_t, ro["bhh"][:, 0:256], ALU.add).then_inc(slot_dve, 1)
            dve.wait_ge(slot_act, 2)
            st(V.tensor_scalar(rz_t, rz_t, 0.5, 0.5, ALU.mult, ALU.add))
            st.wait()
            st(V.tensor_tensor(n_t, rz_t[:, 0:P], hn_t, ALU.mult))
            st.wait()
            st(V.tensor_tensor(n_t, n_t, bank[3][:, P:2 * P], ALU.add))
            st.wait()
            V.tensor_tensor(n_t, n_t, ro["bih"][:, 256:384], ALU.add).then_inc(slot_dve, 1)
            dve.wait_ge(slot_act, 3)
            st(V.tensor_tensor(z_t, m0["slot2"], n_t, ALU.subtract))
            st.wait()
            st(V.tensor_tensor(z_t, z_t, rz_t[:, P:2 * P], ALU.mult))
            st.wait()
            V.tensor_tensor(sn_t, z_t, n_t, ALU.add).then_inc(slot_dve, 1)
            dve.wait_ge(slot_pe, 5)
            st(V.tensor_scalar(qk_t[:, 0, :], bank[5][0:32, 0:P], BQK[:, 0:1], None, ALU.add))
            st(V.tensor_scalar(qk_t[:, 1, :], bank[5][0:32, P:2 * P], BQK[:, 1:2], None, ALU.add))
            V.tensor_tensor(vv_t, bank[6][:, 0:P], ro["bv"], ALU.add).then_inc(slot_dve, 1)
            dve.wait_ge(slot_pe, 6)
            st(V.scalar_tensor_tensor(out=sc_t, in0=bank[7][:, 0:P], scalar=32 ** -0.5, in1=m1["blockneg"],
                                      op0=ALU.mult, op1=ALU.add))
            st.wait()
            V.tensor_reduce(cst[:, 2:3], sc_t, AX_X, ALU.max, negate=True).then_inc(slot_dve, 1)
            dve.wait_ge(slot_act, 5)
            st(V.reciprocal(cst[:, 7:8], cst[:, 3:4]))
            st.wait()
            V.tensor_scalar(pe_t, pe_t, cst[:, 7:8], None, ALU.mult).then_inc(slot_dve, 1)
            dve.wait_ge(slot_pe, 8)
            st(V.tensor_tensor(yy_t, sn_t, bank[6][:, P:2 * P], ALU.add))
            st.wait()
            yy3 = yy_t.unsqueeze(1)
            statistics(yy3, False, LN_EPS, 3, tiles=1)
            dve.wait_ge(rstd_ready, 3)
            st(V.tensor_scalar(yy_t, yy_t, MV[:, 0, 0:1], RS[:, 0:1], ALU.subtract, ALU.mult))
            st.wait()
            st(V.tensor_tensor(yy_t, yy_t, ro["ln_g"], ALU.mult))
            st.wait()
            V.tensor_tensor(yy_t, yy_t, ro["ln_b"], ALU.add).then_inc(slot_dve, 1)
            dve.wait_ge(slot_pe, 11)
            V.tensor_tensor(SVO[:, :, :], bank[0][0:64, 0:B * P].rearrange("p (b c) -> p b c", b=B),
                            ro["bo"][0:64, :].unsqueeze(1).broadcast_to([64, B, P]), ALU.add).then_inc(phase_done, 1)
            for g in range(NG):
                sl = slice(g * TG, (g + 1) * TG)
                dve.wait_ge(o_ready, g + 1)
                V.tensor_tensor(ACC[:, sl, :], ACC[:, sl, :], bank4[1], ALU.add).then_inc(x1_ready, 1)
            dve.wait_ge(x1_ready, NG)
            statistics(ACC, False, LN_EPS, 4)
            dve.wait_ge(rstd_ready, 4)
            for t in range(NT):
                st(normalise(XN, ACC, t))
            st.wait()
            statistics(XN, False, MOE_EPS, 5)
            dve.wait_ge(rstd_ready, 5)
            for t in range(NT):
                last = normalise(XL, XN, t)
                if t % TG == TG - 1:
                    last.then_inc(xl_ready, 1)
            root_input(True, RMS_EPS, 6)
            dve.wait_ge(rstd_ready, 6)
            for t in range(NT):
                last = scaled(XR, XN, t)
                if t % TG == TG - 1:
                    last.then_inc(xr2_ready, 1)
            dve.wait_ge(ld_m2, 16)
            V.tensor_scalar(BLR[:, :], m2["router"], co["rln_s"], None, ALU.mult).then_inc(col_ready, 1)
            for g in range(NG + 1):
                if g < NG:
                    dve.wait_ge(gate_ready, g + 1)
                    if g >= 2:
                        dve.wait_ge(hT_ready, g - 1)
                    r = g % 2
                    st(V.scalar_tensor_tensor(out=tv_t[r], in0=tg_t[r], scalar=1.0, in1=tv_t[r], op0=ALU.add, op1=ALU.mult))
                    st(V.tensor_scalar(ta_t[r], ta_t[r], 0.499, 0.5, ALU.mult, ALU.add))
                    if g >= 1:
                        dve.wait_ge(scan_ready, g)
                    st.wait()
                    init = 0.0 if g % GB == 0 else hh_t[(g - 1) % 2][:, GW - 1:GW]
                    V.tensor_tensor_scan(hh_t[r], ta_t[r], tv_t[r], init, ALU.mult, ALU.add).then_inc(scan_ready, 1)
                if g >= 1:
                    i = g - 1
                    sl = slice(i * TG, (i + 1) * TG)
                    dve.wait_ge(hT_ready, i + 1)
                    V.scalar_tensor_tensor(out=XN[:, sl, 0:C], in0=bank4[6], scalar=0.5, in1=XN[:, sl, 0:C],
                                           op0=ALU.mult, op1=ALU.add).then_inc(hT_used, 1)
            dve.wait_ge(rl_ready, 1)
            st(V.tensor_tensor(BLT[:, :], bank[1][:, 0:E], ro["router_b"], ALU.add))
            st.wait()
            st(V.tensor_tensor(LE[:, :, :], bank[0][:, 0:NT * E].rearrange("p (t e) -> p t e", t=NT),
                               BLT[:, :].unsqueeze(1).broadcast_to([P, NT, E]), ALU.add))
            st.wait()
            for t in range(NT):
                st(V.max(V8[:, t, :], LE[:, t, :]))
            st.wait()
            for t in range(NT):
                st(V.max_index(I8[:, t, :], V8[:, t, :], LE[:, t, :]))
            st.wait()
            V.tensor_tensor(LE[:, :, :], LE[:, :, :], V8[:, :, 0:1].broadcast_to([P, NT, E]),
                            ALU.subtract).then_inc(gates_ready, 1)
            dve.wait_ge(gates_ready, 2)
            st(V.tensor_copy(V8[:, :, 0:2], I8[:, :, 0:2]))
            st.wait()
            iota = ro["iota8"].unsqueeze(1).broadcast_to([P, NT, E])
            st(V.tensor_tensor(GT[:, :, :], iota, V8[:, :, 0:1].broadcast_to([P, NT, E]), ALU.is_equal))
            st(V.tensor_tensor(G2[:, :, :], iota, V8[:, :, 1:2].broadcast_to([P, NT, E]), ALU.is_equal))
            st.wait()
            st(V.tensor_tensor(GT[:, :, :], GT[:, :, :], G2[:, :, :], ALU.add))
            st.wait()
            st(V.tensor_tensor(GT[:, :, :], GT[:, :, :], LE[:, :, :], ALU.mult))
            st.wait()
            st(V.tensor_reduce(rden_t[:, :], GT[:, :, :], AX_X, ALU.add))
            st.wait()
            st(V.reciprocal(rden_t[:, :], rden_t[:, :]))
            st.wait()
            V.tensor_tensor(GT[:, :, :], GT[:, :, :], rden_t[:, :].unsqueeze(2).broadcast_to([P, NT, E]),
                            ALU.mult).then_inc(phase_done, 1)
            dve.wait_ge(hT_used, NG)
            statistics(XN, True, RMS_EPS, 7)
            dve.wait_ge(rstd_ready, 7)
            for t in range(NT):
                last = scaled(XR, XN, t)
                if t % TG == TG - 1:
                    last.then_inc(x3_ready, 1)
            for g in range(NG):
                o = 1 + 3 * (g % 2)
                for (hi, src, parts, r, went, split) in ((q_hi, bank[o], part[g % 2], rest[0], q_out, q_split),
                                                         (k_hi, bank[o + 1], part2[g % 2], rest[1], k_out, k_split)):
                    dve.wait_ge(hi, g + 1)
                    if g >= 1:
                        dve.wait_ge(split, g)
                    st(V.tensor_tensor(r, src, parts[0], ALU.subtract))
                    st.wait()
                    st(V.tensor_copy(parts[1], r))
                    st.wait()
                    V.tensor_tensor(parts[2], r, parts[1], ALU.subtract).then_inc(split, 1)
            dve.wait_ge(v_copied, NG)
            dve.wait_ge(q_split, NG)
            dve.wait_ge(k_split, NG)
            for r in range(2):
                dve.wait_ge(q_out[r], 48 * NG // 2)
                dve.wait_ge(k_out[r], 48 * NG // 2)
            V.memset(cst[:, 9:10], 0.0).then_inc(phase_done, 1)
            maskp = m2["maskprev"].bitcast(U32).unsqueeze(1).broadcast_to([P, HQ, P])
            PSQ = [PS[:, 2 * r:2 * r + 2, :].rearrange("p b (h k) -> p (b h) k", h=2) for r in range(2)]

            def softmax_input(i):
                c, r = i // NQ, i % 2
                first = c % (NT // B) == 0
                dve.wait_ge(s_ready, i + 1)
                if i >= 2:
                    dve.wait_ge(p_ready, i - 1)
                    dve.wait_ge(d_ready, i - 1)
                prev, cur = PSQ[r][:, :, 0:P], PSQ[r][:, :, P:2 * P]
                st(V.copy_predicated(cur, maskp, NGT if first else prev))
                st.wait()
                st(V.tensor_reduce(NM[:, r, :], cur, AX_X, ALU.max, negate=True))
                st.wait()
                V.tensor_tensor(D4[r], cur, NM[:, r, :].unsqueeze(2).broadcast_to([P, HQ, P]), ALU.add).then_inc(d_ready, 1)

            def v_difference(c):
                if c >= 2:
                    dve.wait_ge(pv_ready, NQ * (c - 1))
                n = max(c, 1)
                V.tensor_tensor(VD[:, c % 2, :, :], VN[:, n, :, :], VN[:, n - 1, :, :], ALU.subtract).then_inc(vd_ready, 1)

            def heads_out(c):
                dve.wait_ge(o_turned, NQ * (c + 1))
                if c >= 2 * TG and c % TG == 0:
                    dve.wait_ge(aoT_ready, c // TG - 1)
                if c >= 1:
                    dve.wait_ge(ao_ready, c)
                o3 = bank[7].rearrange("p (h d) -> p h d", h=NH)
                st(V.reciprocal(RC[:, :], o3[:, :, DH]))
                st.wait()
                V.tensor_tensor(AO[c // TG % 2][:, c % TG, :].rearrange("p (h d) -> p h d", h=NH), o3[:, :, 0:DH],
                                RC[:, :].unsqueeze(2).broadcast_to([P, NH, DH]), ALU.mult).then_inc(ao_ready, 1)

            def residual(g):
                sl = slice(g * TG, (g + 1) * TG)
                dve.wait_ge(at_ready, g + 1)
                V.tensor_tensor(XN[:, sl, 0:C], XN[:, sl, 0:C], bank4[6], ALU.add).then_inc(x3_done, 1)

            N = NT * NQ
            V.memset(bank[6][:, :], 0.0).then_inc(zero_bank, 1)
            for i in range(N + 8):
                if i % NQ == 2 and i < N:
                    v_difference(i // NQ)
                if i >= 6 and (i - 6) % NQ == NQ - 1 and (i - 6) // NQ < NT:
                    heads_out((i - 6) // NQ)
                if i < N:
                    softmax_input(i)
                if i >= 7 and (i - 7) % (TG * NQ) == TG * NQ - 1:
                    residual((i - 7) // (TG * NQ))
            dve.wait_ge(x3_done, NG)
            V.memset(cst[:, 9:10], 0.0).then_inc(phase_done, 1)
            statistics(XN, True, RMS_EPS, 8)
            dve.wait_ge(rstd_ready, 8)
            for t in range(NT):
                last = scaled(XF, XN, t)
                if t % TG == TG - 1:
                    last.then_inc(xf_ready, 1)

            def ff_add(i):
                sl = slice(i * TG, (i + 1) * TG)
                dve.wait_ge(ff_ready, i + 1)
                V.scalar_tensor_tensor(out=XN[:, sl, 0:C], in0=bank4[5 + i % 2], scalar=0.5, in1=XN[:, sl, 0:C],
                                       op0=ALU.mult, op1=ALU.add).then_inc(ff_used, 1)

            for g in range(NG + 1):
                if g < NG:
                    for f in range(NF):
                        n = g * NF + f
                        dve.wait_ge(th_ready, n + 1)
                        if f == 0 and g >= 2:
                            dve.wait_ge(ff_ready, g - 1)
                        if n >= 2:
                            dve.wait_ge(gu_used, n - 1)
                        st(V.scalar_tensor_tensor(out=t1_t[n % 2], in0=th_t[n % 2], scalar=1.0, in1=bank[1 + 2 * (n % 2)],
                                                  op0=ALU.add, op1=ALU.mult))
                        st.wait()
                        V.tensor_tensor(hf_t[g % 2][:, f * GW:(f + 1) * GW], t1_t[n % 2], bank[2 + 2 * (n % 2)],
                                        ALU.mult).then_inc(gu_used, 1)
                if g >= 1:
                    ff_add(g - 1)
            dve.wait_ge(ff_used, NG)
            st(V.tensor_tensor(ACC[:, :, :], ACC[:, :, :], XN[:, :, 0:C], ALU.add))
            st.wait()
            V.memset(cst[:, 9:10], 0.0).then_inc(phase_done, 1)
            dve.wait_ge(b1_mm, 1)
            V.tensor_tensor(B1C[:, :], bank[0][:, 0:E * NF], co["b1"], ALU.add).then_inc(b1_done, 1)
            for e in range(E):
                V.tensor_scalar(MW1[:, e, :], MW1[:, e, :], co["els"][:, e:e + 1], None, ALU.mult).then_inc(w1_scaled, 1)
            for g in range(NG):
                sl = slice(g * TG, (g + 1) * TG)
                dve.wait_ge(gb_ready, g + 1)
                V.tensor_tensor(ACC[:, sl, :], ACC[:, sl, :], bank4[6], ALU.add).then_inc(gb_used, 1)
            dve.wait_ge(gb_used, NG)
            for k in range(NG * E):
                g, e = k // E, k % E
                dve.wait_ge(dn_ready, k + 1)
                if k >= 1:
                    dve.wait_ge(dn_used, TG * k)
                for t in range(TG):
                    n = g * TG + t
                    V.scalar_tensor_tensor(out=ACC[:, n, :], in0=bank4[4 + k % 2][:, t, :], scalar=GT[:, n, e:e + 1],
                                           in1=ACC[:, n, :], op0=ALU.mult, op1=ALU.add).then_inc(dn_used, 1)


def kernel(**inp):
    import numpy as np
    import concourse.bacc as bacc
    from concourse import mybir as mb
    from concourse.bass_utils import run_bass_kernel_spmd

    def arr(name):
        return np.asarray(inp[name])

    def pack(spec, have):
        return np.ascontiguousarray(np.concatenate([have[n].reshape(have[n].shape[0], -1) for n, _ in spec], axis=1))

    a, f, t, m = "L0_attn_", "L0_ffn_", "L1_attn_", "L1_ffn_"
    slot = arr(f + "slot_init")
    w1 = arr(f + "w1")
    k, q = np.arange(P)[:, None], np.arange(P)[None, :]
    fp = np.float32
    mat0 = pack(MAT0, {"Wk": arr(a + "Wk").T, "Wv": arr(a + "Wv").T, "Wr": arr(a + "Wr").T, "Wo": arr(a + "Wo").T,
                       "w1a": w1[:C], "w1b": w1[C:], "slotT": slot.T, "slotT2": np.tile(slot.T, (1, B)),
                       "slot2": np.tile(slot, (B, 1)), "ident": np.eye(P, dtype=fp)})
    mat1 = pack(MAT1, {"Wih": arr(f + "Wih").T, "Whh": arr(f + "Whh").T, "wq": arr(f + "wq"), "wk": arr(f + "wk"),
                       "wv": arr(f + "wv"), "wvp": arr(f + "wvp"), "wo": arr(f + "wo"),
                       "blockneg": np.where(k // SLOTS == q // SLOTS, fp(0), fp(NEG))})
    wout = arr(t + "Wout").reshape(C, NF, P).transpose(2, 1, 0)
    mat2 = pack(MAT2, {"Wg": arr(t + "Wg").T, "Wv": arr(t + "Wv").T, "Wd": arr(t + "Wd").T, "Wqkv": arr(t + "Wqkv").T,
                       "Wo": arr(t + "Wo").T, "Wgate": arr(t + "Wgate").T, "Wup": arr(t + "Wup").T, "Wout": wout,
                       "maskprev": (q > k).astype(fp), "maskcur": (k <= q).astype(fp), "router": arr(m + "router_w").T})
    cols = pack(COLS, {"mk": arr(a + "time_mix_k")[:, None], "mv": arr(a + "time_mix_v")[:, None],
                       "mr": arr(a + "time_mix_r")[:, None], "decay": arr(a + "time_decay")[:, None],
                       "first": arr(a + "time_first")[:, None], "ln_w": arr(a + "ln_w")[:, None],
                       "ln_b": arr(a + "ln_b")[:, None], "bvp": arr(f + "bvp")[:, None],
                       "w_mix": arr(t + "w_rms_mix")[:, None], "bg": arr(t + "bg")[:, None], "bv": arr(t + "bv")[:, None],
                       "bd": arr(t + "bd")[:, None], "w_attn": arr(t + "w_rms_attn")[:, None],
                       "w_ffn": arr(t + "w_rms_ffn")[:, None], "rln_s": arr(m + "router_ln_scale")[:, None],
                       "rln_b": arr(m + "router_ln_bias")[:, None], "els": arr(m + "expert_ln_scale").T,
                       "elb": arr(m + "expert_ln_bias").T,
                       "b1": arr(m + "b1").reshape(E, NF, P).transpose(2, 0, 1)})
    rows = np.concatenate([arr(f + "b2"), arr(f + "tau"), arr(f + "bih"), arr(f + "bhh"), arr(f + "bv"), arr(f + "ln_g"),
                           arr(f + "ln_b"), arr(f + "bo"), arr(m + "router_b"), np.arange(E, dtype=fp)])
    host = {
        "x": arr("L0_attn_x").reshape(NTOK, C), "mat0": mat0, "mat1": mat1, "mat2": mat2, "cols": cols, "rows": rows,
        "w2s": arr(f + "w2"), "bqk": np.stack([arr(f + "bq"), arr(f + "bk")], axis=1), "b1s": arr(f + "b1")[:, None],
        "moe_w1": arr(m + "w1").transpose(2, 0, 1), "moe_w2": arr(m + "w2").reshape(E, C, NF, P).transpose(3, 0, 2, 1),
        "moe_b2": arr(m + "b2"),
    }
    nc = bacc.Bacc("TRN2", target_bir_lowering=False, num_devices=1)
    arrays, args = {}, []
    for name, v in host.items():
        v = np.ascontiguousarray(v)
        arrays[f"in_{name}"] = v
        args.append(nc.dram_tensor(f"in_{name}", v.shape, mb.dt.from_np(v.dtype), kind="ExternalInput").ap())
    out = nc.dram_tensor("out_x", (NTOK, C), F32, kind="ExternalOutput").ap()
    build(nc, *args, out)
    r = run_bass_kernel_spmd(nc, [arrays], core_ids=[0])
    return r.results[0]["out_x"].reshape(B, T, C)
```

```python
from contextlib import ExitStack

import concourse.bass as bass
from concourse import mybir

P = 128
F32 = mybir.dt.float32
BF16 = mybir.dt.bfloat16
U32 = mybir.dt.uint32
I32 = mybir.dt.int32
ALU = mybir.AluOpType
ACT = mybir.ActivationFunctionType
AX_X = mybir.AxisListType.X

B, T, C = 2, 2048, 128
NTOK = B * T
NT = NTOK // P
TG = 4
GW = TG * P
NG = NT // TG
GB = NG // B
SLOTS = 64
NH, DH, DHP = 16, 8, 9
NPART = 6
QP = (0, 0, 1, 1, 0, 2)
KP = (0, 1, 0, 1, 2, 0)
DFF, NF = 512, 4
E = 8
TOP = 2
BT = 2
BW = BT * P
NBLK = TOP * NTOK // BW + E
XTILES = BT * (NBLK + 1)
XW = C + 2
PAD_ID = TOP * NTOK
NEG = -1.0e30
LN_EPS, RMS_EPS, MOE_EPS = 1e-5, 1e-6, 1e-6
HQ = 4
NQ = NH // HQ
R3 = 3

MAT0 = [("Wk", 128), ("Wv", 128), ("Wr", 128), ("Wo", 128), ("w1a", 64), ("w1b", 64),
        ("slotT", 64), ("slotT2", 128), ("slot2", 128), ("ident", 128)]
MAT1 = [("Wih", 384), ("Whh", 384), ("wq", 32), ("wk", 32), ("wv", 128), ("wvp", 128), ("wo", 128), ("blockneg", 128)]
MAT2 = [("Wg", 128), ("Wv", 128), ("Wd", 128), ("Wqkv", 384), ("Wo", 128), ("Wgate", 512), ("Wup", 512),
        ("Wout", 512), ("maskprev", 128), ("maskcur", 128), ("router", 8),
        ("tri", 128), ("ones", 128)]
COLS = [("mk", 1), ("mv", 1), ("mr", 1), ("decay", 1), ("first", 1), ("ln_w", 1), ("ln_b", 1), ("bvp", 1),
        ("w_mix", 1), ("bg", 1), ("bv", 1), ("bd", 1), ("w_attn", 1), ("w_ffn", 1), ("rln_s", 1), ("rln_b", 1),
        ("els", 8), ("elb", 8), ("b1", 32)]
ROWS = [("b2", 64), ("tau", 1), ("bih", 384), ("bhh", 384), ("bv", 128), ("ln_g", 128), ("ln_b", 128),
        ("bo", 128), ("router_b", 8), ("iota8", 8), ("iota_blk", NTOK // BW)]


def places(pack):
    at, out = 0, {}
    for name, n in pack:
        out[name] = (at, at + n)
        at += n
    return out, at


def build(nc, x, mat0, mat1, mat2, cols, rows, w2s, bqk, b1s, moe_w1, moe_w2, moe_b2, ids, out):
    p0, n0 = places(MAT0)
    p1, n1 = places(MAT1)
    p2, n2 = places(MAT2)
    pc, ncol = places(COLS)
    pr, nrow = places(ROWS)
    x_v = x.rearrange("(t p) c -> p t c", p=P)
    out_v = out.rearrange("(t p) c -> p t c", p=P)
    q_dram = nc.dram_tensor("q_parts", [3, NH, DH, NTOK], BF16, kind="Internal").ap()
    k_dram = nc.dram_tensor("k_parts", [3, NH, DH, NTOK], BF16, kind="Internal").ap()

    xs_dram = nc.dram_tensor("x_sorted", [XTILES * P, XW], F32, kind="Internal").ap()
    y_dram = nc.dram_tensor("y_by_choice", [PAD_ID + NTOK + XTILES * P, C], F32, kind="Internal").ap()

    with ExitStack() as ctx:
        def sb(name, shape, dt=F32):
            return ctx.enter_context(nc.sbuf_tensor(name, shape, dt))

        def sem(name):
            return ctx.enter_context(nc.semaphore(name))

        M0, M1, M2 = sb("M0", [P, n0]), sb("M1", [P, n1]), sb("M2", [P, n2])
        CO, RO = sb("CO", [P, ncol]), sb("RO", [P, nrow])
        W2S, BQK, B1S = sb("W2S", [64, 64]), sb("BQK", [32, 2]), sb("B1S", [64, 1])
        B2E = sb("B2E", [E, P])
        ACC = sb("ACC", [P, NT, C])
        XN = sb("XN", [P, NT, C + 1])
        BIG = sb("BIG", [P, 4 * NTOK])
        SM = sb("SM", [P, 4096])

        m0 = {k: M0[:, a:b] for k, (a, b) in p0.items()}
        m1 = {k: M1[:, a:b] for k, (a, b) in p1.items()}
        m2 = {k: M2[:, a:b] for k, (a, b) in p2.items()}
        co = {k: CO[:, a:b] for k, (a, b) in pc.items()}
        ro = {k: RO[:, a:b] for k, (a, b) in pr.items()}
        ident = m0["ident"]

        ST = sb("ST", [P, NT, 6])
        MV = sb("MV", [P, NT, 2])
        VE = sb("VE", [P, NT])
        RS = sb("RS", [P, NT])
        MH = sb("MH", [P, NT])
        cst = sb("cst", [P, 16])
        DEC = sb("DEC", [P, GW])

        PS = ctx.enter_context(nc.psum_tensor("PS", [P, 8, 512], F32))
        bank = [PS[:, i, :] for i in range(8)]
        bank4 = [b.rearrange("p (t c) -> p t c", t=TG) for b in bank]

        XH = BIG[:, 0:NTOK].rearrange("p (t c) -> p t c", t=NT)
        XT = BIG[:, NTOK:NTOK + B * (T + 1)].rearrange("p (b t) -> p b t", b=B)
        o = NTOK + B * (T + 1) + 2
        LG = BIG[:, o:o + NT * SLOTS].rearrange("p (t s) -> p t s", t=NT)
        o += NT * SLOTS
        LR = BIG[:, o:o + NT * SLOTS].rearrange("p (t s) -> p t s", t=NT)
        o += NT * SLOTS
        xnT = [BIG[:, o + 512 * i:o + 512 * i + 512] for i in range(2)]
        o += 1024
        R2 = sb("R2", [P, 2048])
        mixed = [[BIG[:, o + 512 * j:o + 512 * j + 512] for j in range(3)], [R2[:, 512 * j:512 * j + 512] for j in range(3)]]
        assert o + 1536 <= 4 * NTOK
        V8 = sb("V8", [P, NT, 8])
        I8 = sb("I8", [P, NT, 8], U32)
        hT = [SM[0:64, 512 * i:512 * i + 512] for i in range(2)]
        rT = [SM[:, 1024 + 512 * i:1024 + 512 * i + 512] for i in range(2)]
        rw = [SM[:, 2048 + 512 * i:2048 + 512 * i + 512] for i in range(2)]
        SS = [SM[:, 3072 + 512 * i:3072 + 512 * i + 512] for i in range(2)]
        dif = sb("dif", [P, GW])

        ld_m0, ld_x, ld_m1, ld_m2 = sem("ld_m0"), [sem(f"ld_x{i}") for i in range(4)], sem("ld_m1"), sem("ld_m2")
        ld_small = sem("ld_small")
        ld_moe = sem("ld_moe")
        dve_step, act_step, pool_step = sem("dve_step"), sem("act_step"), sem("pool_step")
        var_ready, rstd_ready = sem("var_ready"), sem("rstd_ready")
        xh_ready, xn_ready = sem("xh_ready"), sem("xn_ready")
        xhT_ready, xt_ready, xnT_ready, xnTs_ready = sem("xhT_ready"), sem("xt_ready"), sem("xnT_ready"), sem("xnTs_ready")
        pre_ready = sem("pre_ready")
        h1_ready, h_ready, logit_ready, logit_used = sem("h1_ready"), sem("h_ready"), sem("logit_ready"), sem("logit_used")
        mix_ready, kvr_ready, kv_used, r_ready, rw_ready = sem("mix_ready"), sem("kvr_ready"), sem("kv_used"), sem("r_ready"), sem("rw_ready")
        y_ready, y_used = sem("y_ready"), sem("y_used")
        pre_mm, col_ready = sem("pre_mm"), sem("col_ready")
        slot_pe, slot_act, slot_dve, slot_pool = sem("slot_pe"), sem("slot_act"), sem("slot_dve"), sem("slot_pool")
        fills = sem("fills")
        phase_done = sem("phase_done")
        act_pre, q_hi, v8_ready, k_hi = sem("act_pre"), sem("q_hi"), sem("v8_ready"), sem("k_hi")

        def meet(eng, k):
            eng.wait_ge(phase_done, k)

        class Steps:
            def __init__(self, eng, s):
                self.eng, self.s, self.n = eng, s, 0

            def __call__(self, ins):
                self.n += 1
                ins.then_inc(self.s, 1)

            def wait(self):
                self.eng.wait_ge(self.s, self.n)

        block = ctx.enter_context(nc.Block())

        def slot_tile(i, n=P):
            return BIG[:, i:i + n]

        s1 = NTOK + B * (T + 1) + 2 + 2 * NT * SLOTS
        rden_t = sb("rden_t", [P, NT])
        si_t, siT_t = BIG[:, s1:s1 + 128], BIG[:, s1 + 128:s1 + 256]
        rz_t, hn_t = BIG[:, s1 + 256:s1 + 512], BIG[:, s1 + 512:s1 + 640]
        n_t, z_t = BIG[:, s1 + 640:s1 + 768], BIG[:, s1 + 768:s1 + 896]
        sn_t, snT_t = BIG[:, s1 + 896:s1 + 1024], BIG[:, s1 + 1024:s1 + 1152]
        qk_t = BIG[0:32, s1 + 1152:s1 + 1408].rearrange("p (a s) -> p a s", a=2)
        vv_t = BIG[:, s1 + 1408:s1 + 1536]
        sc_t, pe_t, pT_t = BIG[:, s1 + 1536:s1 + 1664], BIG[:, s1 + 1664:s1 + 1792], BIG[:, s1 + 1792:s1 + 1920]
        yy_t, yT_t, svT_t = BIG[:, s1 + 1920:s1 + 2048], BIG[:, s1 + 2048:s1 + 2176], BIG[:, s1 + 2176:s1 + 2304]
        col_t = sb("col_t", [P, 8])
        SVO = sb("SVO", [SLOTS, B, P])

        XL = BIG[:, 0:NT * XW].rearrange("p (t c) -> p t c", t=NT)
        XLT = BIG[:, NT * XW:NT * XW + NTOK]
        o = NTOK + B * (T + 1) + 2 + NT * SLOTS
        XR = BIG[:, o:o + NT * P].rearrange("p (t c) -> p t c", t=NT)
        assert o + NT * P <= 4 * NTOK
        aT = [SM[0:64, 512 * i:512 * i + 512] for i in range(2)]
        o += NT * P

        xrT = [SM[:, 1024 + 512 * i:1536 + 512 * i] for i in range(2)]
        tg_t = [SM[:, 2048 + 512 * i:2560 + 512 * i] for i in range(2)]
        tv_t = [SM[:, 3072 + 512 * i:3584 + 512 * i] for i in range(2)]
        ta_t = [R2[:, 512 * i:512 * i + 512] for i in range(2)]
        hh_t = [R2[:, 1024 + 512 * i:1536 + 512 * i] for i in range(2)]
        alphaT_ready, alphaTs_ready, o_ready, x1_ready = sem("alphaT_ready"), sem("alphaTs_ready"), sem("o_ready"), sem("x1_ready")
        xr2_ready, tr_ready, trs_ready = sem("xr2_ready"), sem("tr_ready"), sem("trs_ready")
        gvd_ready, gate_ready, gvd_used = sem("gvd_ready"), sem("gate_ready"), sem("gvd_used")
        scan_ready, hT_ready, hT_used = sem("scan_ready"), sem("hT_ready"), sem("hT_used")
        xl_ready, xlT_ready, xlTs_ready = sem("xl_ready"), sem("xlT_ready"), sem("xlTs_ready")
        rl_ready, gates_ready = sem("rl_ready"), sem("gates_ready")

        x3T = [SM[:, 512 * i:512 * i + 512] for i in range(2)]
        part = [[SM[:, 1024 + 768 * i + 256 * j:1280 + 768 * i + 256 * j].bitcast(BF16) for j in range(3)] for i in range(2)]
        part2 = [[R2[:, 768 * i + 256 * j:768 * i + 256 * j + 256].bitcast(BF16) for j in range(3)] for i in range(2)]
        rest = [SM[:, 2560 + 512 * i:3072 + 512 * i] for i in range(2)]
        VN = sb("VN", [P, NT, NH, DHP])
        VD = sb("VD", [P, 2, NH, DHP])
        x2_ready = sem("x2_ready")
        x3_ready, x3T_ready, x3Ts_ready = sem("x3_ready"), sem("x3T_ready"), sem("x3Ts_ready")
        qkv_ready, q_split, k_split, v_copied = sem("qkv_ready"), sem("q_split"), sem("k_split"), sem("v_copied")
        q_out, k_out = [sem("q_out0"), sem("q_out1")], [sem("k_out0"), sem("k_out1")]

        o = NT * XW
        CW = 2 * P
        QS = [BIG[0:48, o + 2048 * i:o + 2048 * i + 2048].bitcast(BF16).rearrange("p (h t) -> p h t", h=NH) for i in range(2)]
        o += 4096
        KS = [BIG[0:48, o + 3072 * i:o + 3072 * i + 3072].bitcast(BF16).rearrange("p (h t) -> p h t", h=NH) for i in range(2)]
        o += 6144
        assert o <= 4 * NTOK
        FN = 11
        SM2 = sb("SM2", [P, (2 + 3 * R3 - 8) * 512])
        assert FN * XW <= (2 + 3 * R3 - 8) * 512
        tiles4 = [a[:, 512 * i:512 * i + 512].rearrange("p (h k) -> p h k", h=HQ)
                  for a, n in ((SM, 8), (SM2, 3 * R3 - 6)) for i in range(n)]
        D4, P4, PT4, PC4 = tiles4[0:2], tiles4[2:2 + R3], tiles4[2 + R3:2 + 2 * R3], tiles4[2 + 2 * R3:2 + 3 * R3]
        ROT = 2 * NQ
        OT = [R2[:, P * i:P * i + P] for i in range(ROT)]
        AO = [R2[:, 1024 + P * i:1024 + P * i + P] for i in range(2)]
        aoT = [R2[:, 1280 + P * i:1280 + P * i + P] for i in range(2)]
        ot_copied, o_turned, zero_bank = sem("ot_copied"), sem("o_turned"), sem("zero_bank")
        NGT_t = sb("NGT", [P, HQ * P])
        NGT = NGT_t[:, :].rearrange("p (h k) -> p h k", h=HQ)
        PSQ = [PS[:, 2 * r:2 * r + 2, :].rearrange("p b (h k) -> p (b h) k", h=2) for r in range(2)]
        zero_col = cst[:, 4:5]
        BLT, G2 = sb("BLT", [P, E]), sb("G2", [P, NT, E])
        NM = sb("NM", [P, 2, HQ])
        RC = sb("RC", [P, NH])
        q_in, k_in = [sem("q_in0"), sem("q_in1")], [sem("k_in0"), sem("k_in1")]
        s_ready, s_used, d_ready, p_ready = sem("s_ready"), sem("s_used"), sem("d_ready"), sem("p_ready")
        pt_ready, pts_ready, pc_ready, pv_ready = sem("pt_ready"), sem("pts_ready"), sem("pc_ready"), sem("pv_ready")
        vd_ready, ao_ready, aoT_ready, aoTs_ready, at_ready, x3_done = sem("vd_ready"), sem("ao_ready"), sem("aoT_ready"), sem("aoTs_ready"), sem("at_ready"), sem("x3_done")

        XF = BIG[:, NTOK:2 * NTOK].rearrange("p (t c) -> p t c", t=NT)
        xfT = [SM[:, 512 * i:512 * i + 512] for i in range(2)]
        th_t = [SM[:, 1024 + 512 * i:1536 + 512 * i] for i in range(2)]
        t1_t = [SM[:, 2048 + 512 * i:2560 + 512 * i] for i in range(2)]
        hf_t = [BIG[:, 2 * NTOK + 2048 * i:2 * NTOK + 2048 * i + 2048] for i in range(2)]
        xf_ready, xfT_ready, xfTs_ready, gu_ready, th_ready, gu_used, ff_ready, ff_used = (
            sem("xf_ready"), sem("xfT_ready"), sem("xfTs_ready"), sem("gu_ready"), sem("th_ready"), sem("gu_used"),
            sem("ff_ready"), sem("ff_used"))

        MW1 = BIG[:, 0:NTOK].rearrange("p (e h) -> p e h", e=E)
        MW2 = BIG[:, 3 * NTOK:4 * NTOK].rearrange("p (e f d) -> p e f d", e=E, f=NF)
        o = 2 * NTOK
        HE = BIG[:, o:o + NF * BW].rearrange("p (f t) -> p f t", f=NF)
        o += NF * BW
        XTS = BIG[:, o:o + BW]
        o += BW
        XI = BIG[:, o:o + BT * XW].rearrange("p (t c) -> p t c", t=BT)
        o += BT * XW
        YB = [BIG[:, o + P * i:o + P * i + P] for i in range(BT)]
        YR = [[BIG[:, NTOK + 1024 * i + 512 * j:NTOK + 1024 * i + 512 * j + 512].rearrange("p (t c) -> p t c", t=TG)
               for j in range(TOP)] for i in range(4)]
        IDT = sb("IDT", [P, BT, 2])
        DST = sb("DST", [P, BT])
        DSTI = sb("DSTI", [P, BT], I32)
        IDS = sb("IDS", [P, XTILES])
        GT = sb("GT", [P, NT, E])
        LE = sb("LE", [P, NT, E])
        OH = [sb("OH0", [P, NT, E]), sb("OH1", [P, NT, E])]
        CUM = sb("CUM", [P, E, NT])
        POS = sb("POS", [P, NT, E])
        ONE = sb("ONE", [P, NT])
        CMP = sb("CMP", [P, E, NTOK // BW])
        NBL, BI, BS = sb("NBL", [P, E]), sb("BI", [P, E]), sb("BS", [P, E])
        BII = sb("BII", [P, E], I32)
        PJ, PJI = sb("PJ", [P, NT, TOP]), sb("PJI", [P, NT, TOP], I32)
        G12 = sb("G12", [P, TOP, NT])
        FT = SM2[:, 0:FN * XW].rearrange("p (t c) -> p t c", t=FN)
        ft_ready, ft_out, count_mm, pos_ready, xs_ready = sem("ft_ready"), sem("ft_out"), sem("count_mm"), sem("pos_ready"), sem("xs_ready")
        m_ready, ends_ready = sem("m_ready"), sem("ends_ready")
        xi_ready, xi_used, x_turned, xT_ready = sem("xi_ready"), sem("xi_used"), sem("x_turned"), sem("xT_ready")
        idx_ready, y_copied, y_sent, y_in = sem("idx_ready"), sem("y_copied"), sem("y_sent"), [sem(f"y_in{i}") for i in range(4)]
        out_ready = sem("out_ready")
        y_seen, loads_seen = sem("y_seen"), sem("loads_seen")
        B1C = sb("B1C", [P, E * NF])
        BLR = sb("BLR", [P, E])
        gTt = [SM[0:E, 512 * i:512 * i + 512] for i in range(2)]
        b1_mm, b1_done, w1_scaled = sem("b1_mm"), sem("b1_done"), sem("w1_scaled")
        gt_ready, gT_ready, gTs_ready, gb_ready, gb_used = sem("gt_ready"), sem("gT_ready"), sem("gTs_ready"), sem("gb_ready"), sem("gb_used")
        up_ready, act_ready, dn_ready, dn_used = sem("up_ready"), sem("act_ready"), sem("dn_ready"), sem("dn_used")
        st_out = sem("st_out")

        N = NT * NQ
        LAG_SUMS, LAG_HEADS, LAG_PROJ, LAG = 6, 7, 8, 10

        def ends_chunk(i):
            return 0 <= i < N and i % NQ == NQ - 1

        @block.sync
        def _(sp):
            sp.dma_start(M0[:, :], mat0).then_inc(ld_m0, 16)
            for i in range(4):
                sp.dma_start(ACC[:, 8 * i:8 * i + 8, :], x_v[:, 8 * i:8 * i + 8, :]).then_inc(ld_x[i], 16)
            for dst, src in ((CO, cols), (W2S, w2s), (BQK, bqk), (B1S, b1s), (B2E, moe_b2)):
                sp.dma_start(dst[:, :], src).then_inc(ld_small, 16)
            sp.dma_start(RO[:, :], rows.partition_broadcast(P)).then_inc(ld_small, 16)
            sp.dma_start(M1[:, :], mat1).then_inc(ld_m1, 16)
            sp.dma_start(M2[:, :], mat2).then_inc(ld_m2, 16)
            sp.dma_start(IDS[:, :], ids).then_inc(ld_small, 16)
            for n, t in enumerate(range(0, XTILES, FN)):
                w = min(FN, XTILES - t)
                sp.wait_ge(ft_ready, n + 1)
                sp.dma_start(xs_dram[t * P:(t + w) * P, :].rearrange("(t p) c -> p t c", p=P), FT[:, 0:w, :]).then_inc(ft_out, 16)
            for g in range(NG):
                for (split, parts, dram, went) in ((q_split, part, q_dram, q_out), (k_split, part2, k_dram, k_out)):
                    sp.wait_ge(split, g + 1)
                    for j in range(3):
                        sp.dma_start(dram[j].rearrange("h d t -> (h d) t")[:, g * GW:(g + 1) * GW],
                                     parts[g % 2][j]).then_inc(went[g % 2], 16)
            for r in range(2):
                sp.wait_ge(q_out[r], 16 * 3 * NG // 2)
                sp.wait_ge(k_out[r], 16 * 3 * NG // 2)
            meet(sp, 4)
            for i in range(NT // 2):
                if i >= 2:
                    sp.wait_ge(s_ready, 2 * NQ * (i - 1))
                first = i % (NT // 2 // B) == 0
                for p in range(NPART):
                    sp.dma_start(QS[i % 2][8 * p:8 * p + 8, :, :],
                                 q_dram[QP[p]].rearrange("h d t -> d h t")[:, :, i * CW:(i + 1) * CW]).then_inc(q_in[i % 2], 16)
                    lo = P if first else 0
                    sp.dma_start(KS[i % 2][8 * p:8 * p + 8, :, lo:3 * P],
                                 k_dram[KP[p]].rearrange("h d t -> d h t")[:, :, i * CW - P + lo:(i + 1) * CW]).then_inc(k_in[i % 2], 16)
            sp.wait_ge(xs_ready, 16 * NT * TOP)
            meet(sp, 5)
            sp.dma_start(MW1, moe_w1).then_inc(ld_moe, 16)
            sp.dma_start(MW2, moe_w2).then_inc(ld_moe, 16)
            meet(sp, 6)
            sp.wait_ge(ends_ready, 1)
            blocks = sp.value_load(BII[0:1, E - 1:E], min_val=E, max_val=NBLK)

            def block_rows(k):
                return xs_dram[bass.ts(k, BW), :].rearrange("(t p) c -> p t c", p=P)

            sp.dma_start(XI, block_rows(0)).then_inc(xi_ready, 16)
            with sp.Fori(0, blocks) as k:
                sp.wait_ge(xi_used, k + 1)
                sp.dma_start(XI, block_rows(k + 1)).then_inc(xi_ready, 16)
            sp.wait_ge(xi_ready, blocks * 16 + 16)
            sp.sem_inc(loads_seen, 1)
            sp.wait_ge(y_sent, blocks * (16 * BT) + 16)
            for g in range(NG + 1):
                if g < NG:
                    if g >= 4:
                        sp.wait_ge(out_ready, g - 3)
                    for j in range(TOP):
                        src = y_dram[j * NTOK + g * GW:j * NTOK + (g + 1) * GW, :].rearrange("(t p) c -> p t c", p=P)
                        sp.dma_start(YR[g % 4][j], src).then_inc(y_in[g % 4], 16)
                if g >= 1:
                    sp.wait_ge(out_ready, g)
                    sp.dma_start(out_v[:, (g - 1) * TG:g * TG, :], ACC[:, (g - 1) * TG:g * TG, :]).then_inc(st_out, 16)
            sp.wait_ge(st_out, 16 * NG)

        @block.gpsimd
        def _(pool):
            nc.gpsimd.memset(MH[:, :], -0.5).then_inc(pool_step, 1)
            pool.wait_ge(pool_step, 1)

            def rstd(n):
                pool.wait_ge(var_ready, n)
                nc.gpsimd.tensor_tensor(RS[:, :], VE[:, :], MH[:, :], ALU.pow).then_inc(rstd_ready, 1)

            nc.gpsimd.memset(XT[:, :, 0:1], 0.0).then_inc(fills, 1)
            nc.gpsimd.memset(XN[:, :, C:C + 1], 1.0).then_inc(fills, 1)
            nc.gpsimd.memset(VN[:, :, :, DH:DHP], 1.0).then_inc(fills, 1)
            nc.gpsimd.memset(FT[:, :, :], 0.0).then_inc(pool_step, 1)
            pool.wait_ge(pool_step, 2)
            nc.gpsimd.memset(FT[:, :, C + 1:C + 2], -1.0).then_inc(pool_step, 1)
            pool.wait_ge(ld_small, 16 * 7)
            pool.wait_ge(pool_step, 3)

            def fill(n):
                t = n * FN
                w = min(FN, XTILES - t)
                if n >= 1:
                    pool.wait_ge(ft_out, 16 * n)
                nc.gpsimd.tensor_copy(FT[:, 0:w, C:C + 1], IDS[:, t:t + w].unsqueeze(2)).then_inc(ft_ready, 1)

            rstd(1)
            rstd(2)
            for n in range((XTILES + FN - 1) // FN):
                fill(n)
            for n in range(3, 7):
                rstd(n)
            pool.wait_ge(ft_out, 16 * ((XTILES + FN - 1) // FN))
            pool.wait_ge(pos_ready, 1)
            for t in range(NT):
                for j in range(TOP):
                    pool.indirect_dma_start(xs_dram, bass.IndirectOffsetOnAxis(ap=PJI[:, t, j:j + 1], axis=0),
                                            XL[:, t, :], None).then_inc(xs_ready, 16)
                if t == 7:
                    rstd(7)
            meet(pool, 4)
            for i in range(NT * NQ):
                pool.wait_ge(pts_ready, i + 1)
                if i >= R3:
                    pool.wait_ge(pv_ready, i - R3 + 1)
                nc.gpsimd.tensor_tensor(PC4[i % R3], PT4[i % R3], m2["maskcur"].unsqueeze(1).broadcast_to([P, HQ, P]),
                                        ALU.mult).then_inc(pc_ready, 1)
            rstd(8)
            pool.wait_ge(ends_ready, 1)
            blocks = pool.value_load(BII[0:1, E - 1:E], min_val=E, max_val=NBLK)
            pool.dma_start(y_dram[PAD_ID + NTOK + XTILES * P - 1:, 0:NT], ONE[0:1, :]).then_inc(y_sent, 16)
            with pool.Fori(0, blocks) as k:
                for t in range(BT):
                    pool.wait_ge(y_copied, k * BT + (t + 2))
                    pool.sem_inc(y_seen, 1)
                    pool.indirect_dma_start(y_dram, bass.IndirectOffsetOnAxis(ap=DSTI[:, t:t + 1], axis=0),
                                            YB[t], None).then_inc(y_sent, 16)

        @block.tensor
        def _(pe):
            mm, tr = nc.tensor.matmul, nc.tensor.transpose

            def transposes(dst, src4, n=P):
                for t in range(TG):
                    last = tr(dst[0:n, t * P:(t + 1) * P], src4[:, t, 0:n], ident)
                return last

            pe.wait_ge(ld_m0, 16)
            pe.wait_ge(col_ready, 2)
            mm(bank[2][0:64, 0:1], m0["w1b"], col_t[:, 3:4], start=True, stop=True).then_inc(pre_mm, 1)
            for g in range(NG + 2):
                if g < NG:
                    pe.wait_ge(xh_ready, g + 1)
                    if g >= 1:
                        pe.wait_ge(xt_ready, g)
                    transposes(bank[0], XH[:, g * TG:(g + 1) * TG, :]).then_inc(xhT_ready, 1)
                    if g >= 1:
                        pe.wait_ge(xnTs_ready, g)
                    transposes(bank[1], XN[:, g * TG:(g + 1) * TG, :]).then_inc(xnT_ready, 1)
                if 1 <= g <= NG:
                    i = g - 1
                    pe.wait_ge(xnTs_ready, i + 1)
                    if i == 0:
                        pe.wait_ge(pre_ready, 1)
                    if i >= 1:
                        pe.wait_ge(h_ready, i)
                    mm(bank[2][0:64, :], m0["w1a"], xnT[i % 2], start=True, stop=True).then_inc(h1_ready, 1)
                    pe.wait_ge(mix_ready, i + 1)
                    if i >= 1:
                        pe.wait_ge(kv_used, i)
                        pe.wait_ge(r_ready, i)
                    for j, w in enumerate(("Wk", "Wv", "Wr")):
                        last = mm(bank[4 + j], m0[w], mixed[i % 2][j], start=True, stop=True)
                    last.then_inc(kvr_ready, 1)
                if g >= 2:
                    i = g - 2
                    pe.wait_ge(h_ready, i + 1)
                    if i == 0:
                        pe.wait_ge(col_ready, 3)
                    if i >= 1:
                        pe.wait_ge(logit_used, i)
                    for t in range(TG):
                        last = mm(bank[3][:, t * 64:(t + 1) * 64], hT[i % 2][:, t * P:(t + 1) * P], W2S[:, :],
                                  start=True, stop=True)
                    last.then_inc(logit_ready, 1)
                    pe.wait_ge(rw_ready, i + 1)
                    if i >= 1:
                        pe.wait_ge(y_used, i)
                    for t in range(TG):
                        last = mm(bank4[7][:, t, :], rw[i % 2][:, t * P:(t + 1) * P], m0["Wo"], start=True, stop=True)
                    last.then_inc(y_ready, 1)
            meet(pe, 1)
            pe.wait_ge(slot_dve, 1)
            for b in range(B):
                for t in range(NT // B):
                    n = b * (NT // B) + t
                    last = mm(bank[b][64 * b:64 * b + 64, 0:C + 1], LG[:, n, :], XN[:, n, :],
                              start=(t == 0), stop=(t == NT // B - 1))
            last.then_inc(slot_pe, 1)
            pe.wait_ge(ld_m1, 16)
            for j in range(2):
                mm(bank[2][:, j * P:(j + 1) * P], m0["slotT2"], m1["Whh"][:, j * P:(j + 1) * P], start=(j == 0), stop=False,
                   skip_group_check=True)
            mm(bank[3][:, 0:P], m0["slotT2"], m1["Whh"][:, 256:384], start=True, stop=True)
            pe.wait_ge(slot_dve, 2)
            tr(bank[4][:, 0:P], si_t, ident).then_inc(slot_pe, 1)
            pe.wait_ge(slot_act, 1)
            for j in range(2):
                mm(bank[2][:, j * P:(j + 1) * P], siT_t, m1["Wih"][:, j * P:(j + 1) * P], start=False, stop=(j == 1),
                   skip_group_check=True)
            mm(bank[3][:, P:2 * P], siT_t, m1["Wih"][:, 256:384], start=True, stop=True).then_inc(slot_pe, 1)
            pe.wait_ge(slot_dve, 5)
            tr(bank[4][:, 0:P], sn_t, ident).then_inc(slot_pe, 1)
            pe.wait_ge(slot_act, 4)
            mm(bank[5][0:32, 0:P], m1["wq"], snT_t, start=True, stop=True)
            mm(bank[5][0:32, P:2 * P], m1["wk"], snT_t, start=True, stop=True)
            mm(bank[6][:, 0:P], snT_t, m1["wv"], start=True, stop=True).then_inc(slot_pe, 1)
            pe.wait_ge(slot_dve, 6)
            mm(bank[7][:, 0:P], qk_t[:, 0, :], qk_t[:, 1, :], start=True, stop=True).then_inc(slot_pe, 1)
            pe.wait_ge(slot_dve, 8)
            tr(bank[4][:, 0:P], pe_t, ident).then_inc(slot_pe, 1)
            pe.wait_ge(slot_act, 6)
            mm(bank[6][:, P:2 * P], pT_t, vv_t, start=True, stop=True).then_inc(slot_pe, 1)
            pe.wait_ge(slot_dve, 9)
            tr(bank[4][:, 0:P], yy_t, ident).then_inc(slot_pe, 1)
            pe.wait_ge(slot_act, 7)
            mm(bank[5][:, 0:P], m1["wvp"], yT_t, start=True, stop=True).then_inc(slot_pe, 1)
            pe.wait_ge(slot_act, 8)
            for b in range(B):
                last = mm(bank[0][0:64, b * P:(b + 1) * P], svT_t[:, 64 * b:64 * b + 64], m1["wo"], start=True, stop=True)
            last.then_inc(slot_pe, 1)
            meet(pe, 2)
            for g in range(NG + 1):
                if g < NG:
                    if g >= 1:
                        pe.wait_ge(alphaTs_ready, g)
                    transposes(bank[0], LG[:, g * TG:(g + 1) * TG, :], n=SLOTS).then_inc(alphaT_ready, 1)
                if g >= 1:
                    i = g - 1
                    pe.wait_ge(alphaTs_ready, i + 1)
                    if i >= 1:
                        pe.wait_ge(x1_ready, i)
                    for t in range(TG):
                        last = mm(bank4[1][:, t, :], aT[i % 2][:, t * P:(t + 1) * P], SVO[:, i // GB, :], start=True, stop=True)
                    last.then_inc(o_ready, 1)
            pe.wait_ge(ld_m2, 16)
            for g in range(NG + 3):
                if g < NG:
                    pe.wait_ge(xr2_ready, g + 1)
                    if g >= 1:
                        pe.wait_ge(trs_ready, g)
                    transposes(bank[2], XR[:, g * TG:(g + 1) * TG, :]).then_inc(tr_ready, 1)
                if 1 <= g <= NG:
                    i = g - 1
                    pe.wait_ge(trs_ready, i + 1)
                    if i >= 1:
                        pe.wait_ge(gate_ready, i)
                    for j, w in enumerate(("Wg", "Wv", "Wd")):
                        last = mm(bank[3 + j], m2[w], xrT[i % 2], start=True, stop=True)
                    last.then_inc(gvd_ready, 1)
                if 2 <= g <= NG + 1:
                    i = g - 2
                    pe.wait_ge(scan_ready, i + 1)
                    if i >= 1:
                        pe.wait_ge(hT_used, i)
                    for t in range(TG):
                        last = tr(bank4[6][:, t, :], hh_t[i % 2][:, t * P:(t + 1) * P], ident)
                    last.then_inc(hT_ready, 1)
            for g in range(NG):
                pe.wait_ge(xl_ready, g + 1)
                if g >= 1:
                    pe.wait_ge(xlTs_ready, g)
                transposes(bank[7], XL[:, g * TG:(g + 1) * TG, :]).then_inc(xlT_ready, 1)
            mm(bank[1][:, 0:E], co["rln_b"].broadcast_to([P, P]), m2["router"], start=True, stop=True)
            pe.wait_ge(col_ready, 4)
            for t in range(NT):
                if t % TG == 0:
                    pe.wait_ge(xlTs_ready, t // TG + 1)
                last = mm(bank[0][:, t * E:(t + 1) * E], XLT[:, t * P:(t + 1) * P], BLR[:, :], start=True, stop=True)
            last.then_inc(rl_ready, 1)
            pe.wait_ge(m_ready, 1)
            M2d = POS[:, :, :].rearrange("p t e -> p (t e)")
            mm(bank[2][:, 0:NT * E], m2["tri"], M2d, start=True, stop=True)
            mm(bank[3][:, 0:NT * E], m2["ones"], M2d, start=True, stop=True).then_inc(count_mm, 1)
            pe.wait_ge(gt_ready, 1)
            for g in range(NG + 1):
                if g < NG:
                    if g >= 2:
                        pe.wait_ge(gTs_ready, g - 1)
                    transposes(bank[6 + g % 2], GT[:, g * TG:(g + 1) * TG, :], n=E).then_inc(gT_ready, 1)
                if g >= 1:
                    i = g - 1
                    pe.wait_ge(gTs_ready, i + 1)
                    if i >= 2:
                        pe.wait_ge(gb_used, i - 1)
                    for t in range(TG):
                        last = mm(bank4[4 + i % 2][:, t, :], gTt[i % 2][:, t * P:(t + 1) * P], B2E[:, :], start=True, stop=True)
                    last.then_inc(gb_ready, 1)
            meet(pe, 3)
            for g in range(NG + 1):
                if g < NG:
                    pe.wait_ge(x3_ready, g + 1)
                    if g >= 1:
                        pe.wait_ge(x3Ts_ready, g)
                    transposes(bank[0], XR[:, g * TG:(g + 1) * TG, :]).then_inc(x3T_ready, 1)
                if g >= 1:
                    i = g - 1
                    pe.wait_ge(x3Ts_ready, i + 1)
                    if i >= 2:
                        pe.wait_ge(q_split, i - 1)
                        pe.wait_ge(k_split, i - 1)
                        pe.wait_ge(v_copied, i - 1)
                    o = 1 + 3 * (i % 2)
                    mm(bank[o], m2["Wqkv"][:, 0:P], x3T[i % 2], start=True, stop=True)
                    mm(bank[o + 1], m2["Wqkv"][:, P:2 * P], x3T[i % 2], start=True, stop=True)
                    for t in range(TG):
                        last = mm(bank4[o + 2][:, t, :], x3T[i % 2][:, t * P:(t + 1) * P], m2["Wqkv"][:, 2 * P:3 * P],
                                  start=True, stop=True)
                    last.then_inc(qkv_ready, 1)
            meet(pe, 4)

            def scores(i):
                c, hq = i // NQ, i % NQ
                r = (c // 2) % 2
                if i % (2 * NQ) == 0:
                    n = 16 * NPART * (c // 4 + 1)
                    pe.wait_ge(q_in[r], n)
                    pe.wait_ge(k_in[r], n)
                if i >= 2:
                    pe.wait_ge(p_ready, i - 1)
                first = c % (NT // B) == 0
                for h in range(HQ):
                    lo = P if first else 0
                    k0 = (c % 2) * P
                    last = mm(bank[2 * (i % 2) + h // 2][:, (h % 2) * 2 * P + lo:(h % 2 + 1) * 2 * P],
                              QS[r][:, hq * HQ + h, (c % 2) * P:(c % 2 + 1) * P],
                              KS[r][:, hq * HQ + h, k0 + lo:k0 + 2 * P], start=True, stop=True)
                last.then_inc(s_ready, 1)

            def weights_turn(i):
                pe.wait_ge(p_ready, i + 1)
                if i >= 2:
                    pe.wait_ge(pts_ready, i - 1)
                for h in range(HQ):
                    last = tr(bank[4 + i % 2][:, h * P:(h + 1) * P], P4[i % R3][:, h, :], ident)
                last.then_inc(pt_ready, 1)

            def weighted(i):
                c, hq = i // NQ, i % NQ
                first = c % (NT // B) == 0
                pe.wait_ge(pc_ready, i + 1)
                if i >= 1:
                    pe.wait_ge(ot_copied, i)
                if hq == 0 and not first:
                    pe.wait_ge(vd_ready, c + 1)
                for h in range(HQ):
                    hh = hq * HQ + h
                    dst = bank[6][32 * h:32 * h + DHP, 0:P]
                    if first:
                        last = mm(dst, VN[:, c, hh, :], PT4[i % R3][:, h, :], start=True, stop=True)
                    else:
                        mm(dst, VN[:, c - 1, hh, :], PT4[i % R3][:, h, :], start=True, stop=False)
                        last = mm(dst, VD[:, c % 2, hh, :], PC4[i % R3][:, h, :], start=False, stop=True)
                last.then_inc(pv_ready, 1)

            def sums_turn(c):
                pe.wait_ge(ot_copied, NQ * (c + 1))
                if c >= 1:
                    pe.wait_ge(x3_done, c)
                for hq in range(NQ):
                    last = tr(bank[7][:, hq * P:(hq + 1) * P], OT[(c * NQ + hq) % ROT], ident)
                last.then_inc(o_turned, 1)

            def heads_turn(c):
                pe.wait_ge(ao_ready, c + 1)
                tr(bank[7][:, 0:P], AO[c % 2], ident).then_inc(aoT_ready, 1)

            def out_proj(c):
                pe.wait_ge(aoTs_ready, c + 1)
                mm(bank[7][:, 0:P], aoT[c % 2], m2["Wo"], start=True, stop=True).then_inc(at_ready, 1)

            pe.wait_ge(zero_bank, 1)
            for i in range(N + LAG):
                if i < N:
                    scores(i)
                if 2 <= i <= N + 1:
                    weights_turn(i - 2)
                if ends_chunk(i - LAG_SUMS):
                    sums_turn((i - LAG_SUMS) // NQ)
                if 4 <= i <= N + 3:
                    weighted(i - 4)
                if ends_chunk(i - LAG_HEADS):
                    heads_turn((i - LAG_HEADS) // NQ)
                if ends_chunk(i - LAG_PROJ):
                    out_proj((i - LAG_PROJ) // NQ)
            meet(pe, 5)

            def gate_up(i):
                for f in range(NF):
                    n = i * NF + f
                    if n >= 2:
                        pe.wait_ge(gu_used, n - 1)
                    mm(bank[1 + 2 * (n % 2)], m2["Wgate"][:, f * P:(f + 1) * P], xfT[i % 2], start=True, stop=True)
                    mm(bank[2 + 2 * (n % 2)], m2["Wup"][:, f * P:(f + 1) * P], xfT[i % 2], start=True,
                       stop=True).then_inc(gu_ready, 1)

            for g in range(NG + 2):
                if g < NG:
                    pe.wait_ge(xf_ready, g + 1)
                    if g >= 1:
                        pe.wait_ge(xfTs_ready, g)
                    transposes(bank[0], XF[:, g * TG:(g + 1) * TG, :]).then_inc(xfT_ready, 1)
                if 1 <= g <= NG:
                    pe.wait_ge(xfTs_ready, g)
                    gate_up(g - 1)
                if g >= 2:
                    i = g - 2
                    pe.wait_ge(gu_used, NF * (i + 1))
                    if i >= 2:
                        pe.wait_ge(ff_used, i - 1)
                    for t in range(TG):
                        for f in range(NF):
                            last = mm(bank4[5 + i % 2][:, t, :], hf_t[i % 2][:, f * GW + t * P:f * GW + (t + 1) * P],
                                      m2["Wout"][:, f * P:(f + 1) * P], start=(f == 0), stop=(f == NF - 1))
                    last.then_inc(ff_ready, 1)
            pe.wait_ge(ld_moe, 32)
            for e in range(E):
                for f in range(NF):
                    last = mm(bank[7][:, e * NF + f:e * NF + f + 1], MW1[:, e, f * P:(f + 1) * P], co["elb"][:, e:e + 1],
                              start=True, stop=True)
            last.then_inc(b1_mm, 1)
            meet(pe, 6)
            ends = [0] + [pe.value_load(BII[0:1, e:e + 1], min_val=e + 1, max_val=NBLK) for e in range(E)]

            def turn_block():
                for t in range(BT):
                    last = tr(bank[4][:, t * P:(t + 1) * P], XI[:, t, 0:C], ident)
                last.then_inc(x_turned, 1)

            pe.sem_inc(dn_ready, 1)
            pe.wait_ge(xi_ready, 16)
            turn_block()
            pe.wait_ge(w1_scaled, E)
            pe.wait_ge(b1_done, 1)
            for e in range(E):
                with pe.Fori(ends[e], ends[e + 1]) as k:
                    pe.wait_ge(xT_ready, k + 1)
                    pe.wait_ge(act_ready, k * NF + 1)
                    for f in range(NF):
                        mm(bank[f][:, 0:BW], MW1[:, e, f * P:(f + 1) * P], XTS, start=True, stop=True).then_inc(up_ready, 1)
                    pe.wait_ge(xi_ready, k * 16 + 32)
                    turn_block()
                    for t in range(BT):
                        pe.wait_ge(y_copied, k * BT + 1)
                        for f in range(NF):
                            if t == 0:
                                pe.wait_ge(act_ready, k * NF + (f + 2))
                            last = mm(bank[5 + t][:, 0:P], HE[:, f, t * P:(t + 1) * P], MW2[:, e, f, :],
                                      start=(f == 0), stop=(f == NF - 1))
                        last.then_inc(dn_ready, 1)

        @block.scalar
        def _(act):
            A = nc.scalar.activation
            act.wait_ge(ld_small, 16 * 7)
            A(col_t[:, 4:5], co["decay"], ACT.Tanh, scale=0.5).then_inc(act_pre, 1)
            A(col_t[:, 1:2], co["first"], ACT.Exp).then_inc(act_pre, 1)
            A(col_t[:, 2:3], ro["tau"], ACT.Abs).then_inc(act_pre, 1)
            act.wait_ge(pre_ready, 1)
            for g in range(NG + 1):
                if g < NG:
                    b, o = g // GB, 1 + (g % GB) * GW
                    act.wait_ge(xhT_ready, g + 1)
                    A(XT[:, b, o:o + GW], bank[0], ACT.Identity, bias=co["ln_b"], scale=co["ln_w"]).then_inc(xt_ready, 1)
                    act.wait_ge(xnT_ready, g + 1)
                    if g >= 2:
                        act.wait_ge(h1_ready, g - 1)
                    nc.scalar.copy(xnT[g % 2], bank[1]).then_inc(xnTs_ready, 1)
                if g >= 1:
                    i = g - 1
                    act.wait_ge(h1_ready, i + 1)
                    if i >= 2:
                        act.wait_ge(logit_ready, i - 1)
                    A(hT[i % 2], bank[2][0:64, :], ACT.Gelu, bias=B1S[:, :]).then_inc(h_ready, 1)
                    act.wait_ge(kvr_ready, i + 1)
                    if i >= 2:
                        act.wait_ge(rw_ready, i - 1)
                    A(rT[i % 2], bank[6], ACT.Tanh, scale=0.5).then_inc(r_ready, 1)
            act.wait_ge(v8_ready, 1)
            A(LG, LG, ACT.Exp).then_inc(v8_ready, 1)
            act.wait_ge(slot_pe, 2)
            nc.scalar.copy(siT_t, bank[4][:, 0:P]).then_inc(slot_act, 1)
            act.wait_ge(slot_dve, 3)
            A(rz_t, rz_t, ACT.Tanh, scale=0.5).then_inc(slot_act, 1)
            act.wait_ge(slot_dve, 4)
            A(n_t, n_t, ACT.Tanh).then_inc(slot_act, 1)
            act.wait_ge(slot_pe, 4)
            nc.scalar.copy(snT_t, bank[4][:, 0:P]).then_inc(slot_act, 1)
            act.wait_ge(slot_dve, 7)
            A(pe_t, sc_t, ACT.Exp, bias=cst[:, 2:3], accum_out=cst[:, 3:4]).then_inc(slot_act, 1)
            act.wait_ge(slot_pe, 7)
            nc.scalar.copy(pT_t, bank[4][:, 0:P]).then_inc(slot_act, 1)
            act.wait_ge(slot_pe, 9)
            nc.scalar.copy(yT_t, bank[4][:, 0:P]).then_inc(slot_act, 1)
            act.wait_ge(slot_pe, 10)
            A(svT_t, bank[5][:, 0:P], ACT.Identity, bias=co["bvp"]).then_inc(slot_act, 1)
            for g in range(NG):
                act.wait_ge(alphaT_ready, g + 1)
                if g >= 2:
                    act.wait_ge(o_ready, g - 1)
                nc.scalar.copy(aT[g % 2], bank[0][0:64, :]).then_inc(alphaTs_ready, 1)
            for g in range(NG + 1):
                if g < NG:
                    act.wait_ge(tr_ready, g + 1)
                    if g >= 2:
                        act.wait_ge(gvd_ready, g - 1)
                    A(xrT[g % 2], bank[2], ACT.Identity, bias=zero_col, scale=co["w_mix"]).then_inc(trs_ready, 1)
                if g >= 1:
                    i = g - 1
                    act.wait_ge(gvd_ready, i + 1)
                    if i >= 2:
                        act.wait_ge(scan_ready, i - 1)
                    A(tg_t[i % 2], bank[3], ACT.Tanh, scale=0.5, bias=cst[:, 0:1])
                    A(tv_t[i % 2], bank[4], ACT.Tanh, bias=co["bv"])
                    A(ta_t[i % 2], bank[5], ACT.Tanh, scale=0.5, bias=cst[:, 1:2]).then_inc(gate_ready, 1)
            for g in range(NG):
                act.wait_ge(xlT_ready, g + 1)
                nc.scalar.copy(XLT[:, g * GW:(g + 1) * GW], bank[7]).then_inc(xlTs_ready, 1)
            act.wait_ge(gates_ready, 1)
            A(LE[:, :, :], LE[:, :, :], ACT.Exp).then_inc(gates_ready, 1)
            for g in range(NG):
                act.wait_ge(gT_ready, g + 1)
                if g >= 2:
                    act.wait_ge(gb_ready, g - 1)
                nc.scalar.copy(gTt[g % 2], bank[6 + g % 2][0:E, :]).then_inc(gTs_ready, 1)
            for g in range(NG + 1):
                if g < NG:
                    act.wait_ge(x3T_ready, g + 1)
                    if g >= 2:
                        act.wait_ge(qkv_ready, g - 1)
                    A(x3T[g % 2], bank[0], ACT.Identity, bias=zero_col, scale=co["w_attn"]).then_inc(x3Ts_ready, 1)
                if g >= 1:
                    i = g - 1
                    o = 1 + 3 * (i % 2)
                    act.wait_ge(qkv_ready, i + 1)
                    if i >= 2:
                        act.wait_ge(q_out[i % 2], 48 * (i // 2))
                        act.wait_ge(k_out[i % 2], 48 * (i // 2))
                    A(part[i % 2][0], bank[o], ACT.Copy, scale=DH ** -0.5).then_inc(q_hi, 1)
                    nc.scalar.copy(part2[i % 2][0], bank[o + 1]).then_inc(k_hi, 1)
                    nc.scalar.copy(VN[:, i * TG:(i + 1) * TG, :, 0:DH],
                                   bank[o + 2].rearrange("p (t h d) -> p t h d", t=TG, h=NH)).then_inc(v_copied, 1)
            def exps(i):
                act.wait_ge(d_ready, i + 1)
                if i >= R3:
                    act.wait_ge(pt_ready, i - R3 + 1)
                for h in range(HQ):
                    last = A(P4[i % R3][:, h, :], PSQ[i % 2][:, h, P:2 * P], ACT.Exp, bias=NM[:, i % 2, h:h + 1])
                last.then_inc(p_ready, 1)

            def turned(i):
                act.wait_ge(pt_ready, i + 1)
                if i >= R3:
                    act.wait_ge(pv_ready, i - R3 + 1)
                    act.wait_ge(pc_ready, i - R3 + 1)
                nc.scalar.copy(PT4[i % R3], bank4[4 + i % 2]).then_inc(pts_ready, 1)

            for i in range(N + LAG):
                if 5 <= i <= N + 4:
                    j = i - 5
                    act.wait_ge(pv_ready, j + 1)
                    if j >= ROT:
                        act.wait_ge(o_turned, (j - ROT) // NQ + 1)
                    nc.scalar.copy(OT[j % ROT], bank[6][:, 0:P]).then_inc(ot_copied, 1)
                if ends_chunk(i - LAG_HEADS - 1):
                    c = (i - LAG_HEADS - 1) // NQ
                    act.wait_ge(aoT_ready, c + 1)
                    if c >= 2:
                        act.wait_ge(at_ready, c - 1)
                    nc.scalar.copy(aoT[c % 2], bank[7][:, 0:P]).then_inc(aoTs_ready, 1)
                if 2 <= i <= N + 1:
                    turned(i - 2)
                if i < N:
                    exps(i)
            for g in range(NG + 1):
                if g < NG:
                    act.wait_ge(xfT_ready, g + 1)
                    if g >= 2:
                        act.wait_ge(gu_ready, NF * (g - 1))
                    A(xfT[g % 2], bank[0], ACT.Identity, bias=zero_col, scale=co["w_ffn"]).then_inc(xfTs_ready, 1)
                if g >= 1:
                    for f in range(NF):
                        n = (g - 1) * NF + f
                        act.wait_ge(gu_ready, n + 1)
                        if n >= 2:
                            act.wait_ge(gu_used, n - 1)
                        A(th_t[n % 2], bank[1 + 2 * (n % 2)], ACT.Tanh, scale=0.5).then_inc(th_ready, 1)
            meet(act, 6)
            act.wait_ge(b1_done, 1)
            act.sem_inc(act_ready, 1)
            ends = [0] + [act.value_load(BII[0:1, e:e + 1], min_val=e + 1, max_val=NBLK) for e in range(E)]
            for e in range(E):
                with act.Fori(ends[e], ends[e + 1]) as k:
                    act.wait_ge(dn_ready, k * BT + 1)
                    for f in range(NF):
                        act.wait_ge(up_ready, k * NF + (f + 1))
                        A(HE[:, f, :], bank[f][:, 0:BW], ACT.Gelu, bias=B1C[:, e * NF + f:e * NF + f + 1]).then_inc(act_ready, 1)

        @block.vector
        def _(dve):
            V = nc.vector
            st = Steps(dve, dve_step)

            def statistics(src, rms, eps, n, first=0, tiles=NT):
                for t in range(tiles):
                    if src is ACC and n == 1 and t % 8 == 0:
                        dve.wait_ge(ld_x[t // 8], 16)
                    st(V.bn_stats(ST[:, t, :], src[:, t, 0:C]))
                st.wait()
                for t in range(tiles):
                    st(V.bn_aggr(MV[:, t, :], ST[:, t, :]))
                st.wait()
                root_input(rms, eps, n, tiles)

            def root_input(rms, eps, n, tiles=NT):
                if n >= 2:
                    dve.wait_ge(rstd_ready, n - 1)
                m, v = MV[:, 0:tiles, 0], MV[:, 0:tiles, 1]
                if rms:
                    st(V.tensor_tensor(VE[:, 0:tiles], m, m, ALU.mult))
                    st.wait()
                    st(V.tensor_tensor(VE[:, 0:tiles], VE[:, 0:tiles], v, ALU.add))
                    st.wait()
                    V.tensor_scalar(VE[:, 0:tiles], VE[:, 0:tiles], eps, None, ALU.add).then_inc(var_ready, 1)
                elif tiles == NT:
                    V.tensor_scalar(VE[:, :], v, eps, None, ALU.add).then_inc(var_ready, 1)
                else:
                    V.tensor_scalar(VE[:, 0:tiles], v, eps, None, ALU.add).then_inc(var_ready, 1)

            def normalise(dst, src, t):
                return V.tensor_scalar(dst[:, t, 0:C], src[:, t, 0:C], MV[:, t, 0:1], RS[:, t:t + 1], ALU.subtract, ALU.mult)

            def scaled(dst, src, t):
                return V.tensor_scalar(dst[:, t, 0:C], src[:, t, 0:C], RS[:, t:t + 1], None, ALU.mult)

            dve.wait_ge(ld_small, 16 * 7)
            dve.wait_ge(act_pre, 3)
            st(V.tensor_scalar(col_t[:, 0:1], col_t[:, 4:5], 0.5, 0.5, ALU.mult, ALU.add))
            st(V.tensor_scalar(cst[:, 0:1], co["bg"], 0.5, None, ALU.mult))
            st(V.tensor_scalar(cst[:, 1:2], co["bd"], 0.5, None, ALU.mult))
            st(V.memset(cst[:, 4:5], 0.0))
            st(V.memset(NGT_t[:, :], NEG))
            dve.wait_ge(ld_m0, 16)
            st(V.tensor_reduce(col_t[:, 5:6], m0["slotT"], AX_X, ALU.add))
            st.wait()
            st(V.tensor_scalar(col_t[:, 6:7], col_t[:, 2:3], 0.1, None, ALU.add))
            st(V.tensor_copy(DEC[:, :], col_t[:, 0:1].broadcast_to([P, GW])))
            V.tensor_scalar(col_t[:, 3:4], col_t[:, 5:6], 1.0 / SLOTS, None, ALU.mult).then_inc(col_ready, 2)
            st.wait()
            st(V.reciprocal(col_t[:, 7:8], col_t[:, 6:7]))
            st.wait()
            st(V.tensor_scalar(ro["b2"], ro["b2"], col_t[:, 7:8], None, ALU.mult))
            V.tensor_scalar(W2S[:, :], W2S[:, :], col_t[0:64, 7:8], None, ALU.mult).then_inc(col_ready, 1)
            dve.wait_ge(pre_mm, 1)
            V.tensor_tensor(B1S[:, :], B1S[:, :], bank[2][0:64, 0:1], ALU.add).then_inc(pre_ready, 1)
            dve.wait_ge(fills, 3)
            statistics(ACC, False, LN_EPS, 1)
            dve.wait_ge(rstd_ready, 1)
            for t in range(NT):
                st(normalise(XN, ACC, t))
            st.wait()
            st(V.tensor_tensor(ACC[:, :, :], ACC[:, :, :], XN[:, :, 0:C], ALU.add))
            statistics(XN, False, LN_EPS, 2)
            dve.wait_ge(rstd_ready, 2)
            for g in range(NG + 3):
                if g < NG:
                    for t in range(TG):
                        last = normalise(XH, XN, g * TG + t)
                    last.then_inc(xh_ready, 1)
                if 1 <= g <= NG:
                    i = g - 1
                    b, o = i // GB, (i % GB) * GW
                    dve.wait_ge(xt_ready, i + 1)
                    if i >= 2:
                        dve.wait_ge(kvr_ready, i - 1)
                    if i >= 1:
                        dve.wait_ge(mix_ready, i)
                    prev, cur = XT[:, b, o:o + GW], XT[:, b, o + 1:o + 1 + GW]
                    st(V.tensor_tensor(dif[:, :], cur, prev, ALU.subtract))
                    st.wait()
                    for j, w in enumerate(("mk", "mv", "mr")):
                        last = V.scalar_tensor_tensor(out=mixed[i % 2][j], in0=dif[:, :], scalar=co[w], in1=prev,
                                                      op0=ALU.mult, op1=ALU.add)
                    last.then_inc(mix_ready, 1)
                if 2 <= g <= NG + 1:
                    i = g - 2
                    dve.wait_ge(kvr_ready, i + 1)
                    dve.wait_ge(r_ready, i + 1)
                    if i >= 2:
                        dve.wait_ge(y_ready, i - 1)
                    if i >= 1:
                        dve.wait_ge(rw_ready, i)
                    init = 0.0 if i % GB == 0 else SS[(i - 1) % 2][:, GW - 1:GW]
                    st(V.tensor_tensor_scan(SS[i % 2], DEC[:, :], bank[4], init, ALU.mult, ALU.add))
                    st.wait()
                    st(V.scalar_tensor_tensor(out=rw[i % 2], in0=SS[i % 2], scalar=col_t[:, 1:2], in1=bank[4],
                                              op0=ALU.mult, op1=ALU.add))
                    st.wait()
                    V.tensor_tensor(rw[i % 2], rw[i % 2], bank[5], ALU.mult).then_inc(kv_used, 1)
                    dve.wait_ge(kv_used, i + 1)
                    V.scalar_tensor_tensor(out=rw[i % 2], in0=rT[i % 2], scalar=1.0, in1=rw[i % 2],
                                           op0=ALU.add, op1=ALU.mult).then_inc(rw_ready, 1)
                    dve.wait_ge(logit_ready, i + 1)
                    sl = slice(i * TG, (i + 1) * TG)
                    V.tensor_tensor(LG[:, sl, :], bank[3][:, 0:TG * SLOTS].rearrange("p (t s) -> p t s", t=TG),
                                    ro["b2"].unsqueeze(1).broadcast_to([P, TG, SLOTS]), ALU.add).then_inc(logit_used, 1)
                    dve.wait_ge(logit_used, i + 1)
                    for t in range(i * TG, (i + 1) * TG):
                        st(V.max(V8[:, t, :], LG[:, t, :]))
                    st.wait()
                    for t in range(i * TG, (i + 1) * TG):
                        st(V.match_replace(LR[:, t, :], V8[:, t, :], LG[:, t, :], NEG))
                if g >= 3:
                    i = g - 3
                    dve.wait_ge(y_ready, i + 1)
                    sl = slice(i * TG, (i + 1) * TG)
                    V.scalar_tensor_tensor(out=ACC[:, sl, :], in0=bank4[7], scalar=0.5, in1=ACC[:, sl, :],
                                           op0=ALU.mult, op1=ALU.add).then_inc(y_used, 1)
            st.wait()
            dve.wait_ge(y_used, NG)
            st(V.tensor_tensor(LR, LR, LG, ALU.not_equal))
            st.wait()
            V.tensor_tensor(LG, LG, V8[:, :, 0:1].broadcast_to([P, NT, SLOTS]), ALU.subtract).then_inc(v8_ready, 1)
            dve.wait_ge(v8_ready, 1)
            V.memset(cst[:, 9:10], 0.0).then_inc(phase_done, 1)
            dve.wait_ge(v8_ready, 2)
            st(V.tensor_tensor(LG, LG, LR, ALU.mult))
            st.wait()
            st(V.tensor_reduce(rden_t[:, :], LG, AX_X, ALU.add))
            st.wait()
            st(V.reciprocal(rden_t[:, :], rden_t[:, :]))
            st.wait()
            V.tensor_tensor(LG, LG, rden_t[:, :].unsqueeze(2).broadcast_to([P, NT, SLOTS]), ALU.mult).then_inc(slot_dve, 1)
            dve.wait_ge(slot_pe, 1)
            for b in range(B):
                s = slice(64 * b, 64 * b + 64)
                st(V.tensor_scalar(cst[s, 5:6], bank[b][s, C:C + 1], 1e-8, None, ALU.add))
            st.wait()
            st(V.reciprocal(cst[:, 6:7], cst[:, 5:6]))
            st.wait()
            for b in range(B):
                s = slice(64 * b, 64 * b + 64)
                last = V.tensor_scalar(si_t[s, :], bank[b][s, 0:C], cst[s, 6:7], None, ALU.mult)
                if b == 0:
                    st(last)
            last.then_inc(slot_dve, 1)
            dve.wait_ge(slot_pe, 3)
            dve.wait_ge(ld_m1, 16)
            st(V.tensor_tensor(rz_t, bank[2][:, 0:256], ro["bih"][:, 0:256], ALU.add))
            st(V.tensor_tensor(hn_t, bank[3][:, 0:P], ro["bhh"][:, 256:384], ALU.add))
            st.wait()
            V.tensor_tensor(rz_t, rz_t, ro["bhh"][:, 0:256], ALU.add).then_inc(slot_dve, 1)
            dve.wait_ge(slot_act, 2)
            st(V.tensor_scalar(rz_t, rz_t, 0.5, 0.5, ALU.mult, ALU.add))
            st.wait()
            st(V.tensor_tensor(n_t, rz_t[:, 0:P], hn_t, ALU.mult))
            st.wait()
            st(V.tensor_tensor(n_t, n_t, bank[3][:, P:2 * P], ALU.add))
            st.wait()
            V.tensor_tensor(n_t, n_t, ro["bih"][:, 256:384], ALU.add).then_inc(slot_dve, 1)
            dve.wait_ge(slot_act, 3)
            st(V.tensor_tensor(z_t, m0["slot2"], n_t, ALU.subtract))
            st.wait()
            st(V.tensor_tensor(z_t, z_t, rz_t[:, P:2 * P], ALU.mult))
            st.wait()
            V.tensor_tensor(sn_t, z_t, n_t, ALU.add).then_inc(slot_dve, 1)
            dve.wait_ge(slot_pe, 5)
            st(V.tensor_scalar(qk_t[:, 0, :], bank[5][0:32, 0:P], BQK[:, 0:1], None, ALU.add))
            st(V.tensor_scalar(qk_t[:, 1, :], bank[5][0:32, P:2 * P], BQK[:, 1:2], None, ALU.add))
            V.tensor_tensor(vv_t, bank[6][:, 0:P], ro["bv"], ALU.add).then_inc(slot_dve, 1)
            dve.wait_ge(slot_pe, 6)
            st(V.scalar_tensor_tensor(out=sc_t, in0=bank[7][:, 0:P], scalar=32 ** -0.5, in1=m1["blockneg"],
                                      op0=ALU.mult, op1=ALU.add))
            st.wait()
            V.tensor_reduce(cst[:, 2:3], sc_t, AX_X, ALU.max, negate=True).then_inc(slot_dve, 1)
            dve.wait_ge(slot_act, 5)
            st(V.reciprocal(cst[:, 7:8], cst[:, 3:4]))
            st.wait()
            V.tensor_scalar(pe_t, pe_t, cst[:, 7:8], None, ALU.mult).then_inc(slot_dve, 1)
            dve.wait_ge(slot_pe, 8)
            st(V.tensor_tensor(yy_t, sn_t, bank[6][:, P:2 * P], ALU.add))
            st.wait()
            yy3 = yy_t.unsqueeze(1)
            statistics(yy3, False, LN_EPS, 3, tiles=1)
            dve.wait_ge(rstd_ready, 3)
            st(V.tensor_scalar(yy_t, yy_t, MV[:, 0, 0:1], RS[:, 0:1], ALU.subtract, ALU.mult))
            st.wait()
            st(V.tensor_tensor(yy_t, yy_t, ro["ln_g"], ALU.mult))
            st.wait()
            V.tensor_tensor(yy_t, yy_t, ro["ln_b"], ALU.add).then_inc(slot_dve, 1)
            dve.wait_ge(slot_pe, 11)
            V.tensor_tensor(SVO[:, :, :], bank[0][0:64, 0:B * P].rearrange("p (b c) -> p b c", b=B),
                            ro["bo"][0:64, :].unsqueeze(1).broadcast_to([64, B, P]), ALU.add).then_inc(phase_done, 1)
            for g in range(NG):
                sl = slice(g * TG, (g + 1) * TG)
                dve.wait_ge(o_ready, g + 1)
                V.tensor_tensor(ACC[:, sl, :], ACC[:, sl, :], bank4[1], ALU.add).then_inc(x1_ready, 1)
            dve.wait_ge(x1_ready, NG)
            statistics(ACC, False, LN_EPS, 4)
            dve.wait_ge(rstd_ready, 4)
            for t in range(NT):
                st(normalise(XN, ACC, t))
            st.wait()
            statistics(XN, False, MOE_EPS, 5)
            dve.wait_ge(rstd_ready, 5)
            st(V.tensor_scalar(XL[:, :, C:C + 1], IDS[:, 0:NT].unsqueeze(2), float(-PAD_ID), None, ALU.add))
            for t in range(NT):
                last = normalise(XL, XN, t)
                if t % TG == TG - 1:
                    last.then_inc(xl_ready, 1)
            root_input(True, RMS_EPS, 6)
            dve.wait_ge(rstd_ready, 6)
            for t in range(NT):
                last = scaled(XR, XN, t)
                if t % TG == TG - 1:
                    last.then_inc(xr2_ready, 1)
            dve.wait_ge(ld_m2, 16)
            V.tensor_scalar(BLR[:, :], m2["router"], co["rln_s"], None, ALU.mult).then_inc(col_ready, 1)
            for g in range(NG + 1):
                if g < NG:
                    dve.wait_ge(gate_ready, g + 1)
                    if g >= 2:
                        dve.wait_ge(hT_ready, g - 1)
                    r = g % 2
                    st(V.scalar_tensor_tensor(out=tv_t[r], in0=tg_t[r], scalar=1.0, in1=tv_t[r], op0=ALU.add, op1=ALU.mult))
                    st(V.tensor_scalar(ta_t[r], ta_t[r], 0.499, 0.5, ALU.mult, ALU.add))
                    if g >= 1:
                        dve.wait_ge(scan_ready, g)
                    st.wait()
                    init = 0.0 if g % GB == 0 else hh_t[(g - 1) % 2][:, GW - 1:GW]
                    V.tensor_tensor_scan(hh_t[r], ta_t[r], tv_t[r], init, ALU.mult, ALU.add).then_inc(scan_ready, 1)
                if g >= 1:
                    i = g - 1
                    sl = slice(i * TG, (i + 1) * TG)
                    dve.wait_ge(hT_ready, i + 1)
                    V.scalar_tensor_tensor(out=XN[:, sl, 0:C], in0=bank4[6], scalar=0.5, in1=XN[:, sl, 0:C],
                                           op0=ALU.mult, op1=ALU.add).then_inc(hT_used, 1)
            dve.wait_ge(rl_ready, 1)
            st(V.tensor_tensor(BLT[:, :], bank[1][:, 0:E], ro["router_b"], ALU.add))
            st.wait()
            st(V.tensor_tensor(LE[:, :, :], bank[0][:, 0:NT * E].rearrange("p (t e) -> p t e", t=NT),
                               BLT[:, :].unsqueeze(1).broadcast_to([P, NT, E]), ALU.add))
            st.wait()
            for t in range(NT):
                st(V.max(V8[:, t, :], LE[:, t, :]))
            st.wait()
            for t in range(NT):
                st(V.max_index(I8[:, t, :], V8[:, t, :], LE[:, t, :]))
            st.wait()
            V.tensor_tensor(LE[:, :, :], LE[:, :, :], V8[:, :, 0:1].broadcast_to([P, NT, E]),
                            ALU.subtract).then_inc(gates_ready, 1)
            dve.wait_ge(gates_ready, 2)
            st(V.tensor_copy(V8[:, :, 0:2], I8[:, :, 0:2]))
            st.wait()
            iota = ro["iota8"].unsqueeze(1).broadcast_to([P, NT, E])
            st(V.tensor_copy(XL[:, :, C + 1:C + 2], V8[:, :, 0:1]))
            for j in range(TOP):
                st(V.tensor_tensor(OH[j][:, :, :], iota, V8[:, :, j:j + 1].broadcast_to([P, NT, E]), ALU.is_equal))
            st(V.memset(ONE[:, :], 1.0))
            st.wait()
            V.tensor_tensor(POS[:, :, :], OH[0][:, :, :], OH[1][:, :, :], ALU.add).then_inc(m_ready, 1)
            dve.wait_ge(m_ready, 1)
            st(V.tensor_tensor(GT[:, :, :], POS[:, :, :], LE[:, :, :], ALU.mult))
            st.wait()
            st(V.tensor_reduce(rden_t[:, :], GT[:, :, :], AX_X, ALU.add))
            st.wait()
            st(V.reciprocal(rden_t[:, :], rden_t[:, :]))
            st.wait()
            st(V.tensor_tensor(GT[:, :, :], GT[:, :, :], rden_t[:, :].unsqueeze(2).broadcast_to([P, NT, E]), ALU.mult))
            st.wait()
            V.memset(cst[:, 10:11], 0.0).then_inc(gt_ready, 1)
            for j in range(TOP):
                st(V.tensor_tensor(G2[:, :, :], GT[:, :, :], OH[j][:, :, :], ALU.mult))
                st.wait()
                st(V.tensor_reduce(G12[:, j, :], G2[:, :, :], AX_X, ALU.add))
                st.wait()
            dve.wait_ge(count_mm, 1)
            total = bank[3][:, 0:NT * E].rearrange("p (t e) -> p t e", t=NT)
            before = bank[2][:, 0:NT * E].rearrange("p (t e) -> p t e", t=NT)
            for e in range(E):
                st(V.tensor_tensor_scan(CUM[:, e, :], ONE[:, :], total[:, :, e], 0.0, ALU.mult, ALU.add))
            st.wait()
            nw = NTOK // BW
            st(V.tensor_tensor(CMP[:, :, :], CUM[:, :, NT - 1:NT].broadcast_to([P, E, nw]),
                               ro["iota_blk"].unsqueeze(1).broadcast_to([P, E, nw]), ALU.is_gt))
            st(V.tensor_tensor(POS[:, :, :], CUM[:, :, :].rearrange("p e t -> p t e"), total, ALU.subtract))
            st.wait()
            st(V.tensor_reduce(NBL[:, :], CMP[:, :, :], AX_X, ALU.add))
            st(V.tensor_tensor(POS[:, :, :], POS[:, :, :], before, ALU.add))
            st.wait()
            st(V.tensor_scalar(NBL[:, :], NBL[:, :], 1.0, None, ALU.max))
            st.wait()
            st(V.tensor_tensor_scan(BI[:, :], ONE[:, 0:E], NBL[:, :], 0.0, ALU.mult, ALU.add))
            st.wait()
            st(V.tensor_tensor(BS[:, :], BI[:, :], NBL[:, :], ALU.subtract))
            V.tensor_copy(BII[:, :], BI[:, :]).then_inc(ends_ready, 1)
            st.wait()
            st(V.tensor_scalar(BS[:, :], BS[:, :], float(BW), None, ALU.mult))
            st.wait()
            st(V.tensor_tensor(POS[:, :, :], POS[:, :, :], BS[:, :].unsqueeze(1).broadcast_to([P, NT, E]), ALU.add))
            st.wait()
            for j in range(TOP):
                st(V.tensor_tensor(OH[j][:, :, :], OH[j][:, :, :], POS[:, :, :], ALU.mult))
                st.wait()
                st(V.tensor_reduce(PJ[:, :, j], OH[j][:, :, :], AX_X, ALU.add))
            st.wait()
            V.tensor_copy(PJI[:, :, :], PJ[:, :, :]).then_inc(pos_ready, 1)
            for g in range(NG):
                sl = slice(g * TG, (g + 1) * TG)
                dve.wait_ge(gb_ready, g + 1)
                V.tensor_tensor(ACC[:, sl, :], ACC[:, sl, :], bank4[4 + g % 2], ALU.add).then_inc(gb_used, 1)
            dve.wait_ge(gb_used, NG)
            V.memset(cst[:, 9:10], 0.0).then_inc(phase_done, 1)
            dve.wait_ge(hT_used, NG)
            statistics(XN, True, RMS_EPS, 7)
            dve.wait_ge(rstd_ready, 7)
            for t in range(NT):
                last = scaled(XR, XN, t)
                if t % TG == TG - 1:
                    last.then_inc(x3_ready, 1)
            for g in range(NG):
                o = 1 + 3 * (g % 2)
                for (hi, src, scale, parts, r, split) in ((q_hi, bank[o], DH ** -0.5, part[g % 2], rest[0], q_split),
                                                          (k_hi, bank[o + 1], 1.0, part2[g % 2], rest[1], k_split)):
                    dve.wait_ge(hi, g + 1)
                    if g >= 1:
                        dve.wait_ge(split, g)
                    st(V.scalar_tensor_tensor(out=r, in0=src, scalar=scale, in1=parts[0], op0=ALU.mult, op1=ALU.subtract))
                    st.wait()
                    st(V.tensor_copy(parts[1], r))
                    st.wait()
                    V.tensor_tensor(parts[2], r, parts[1], ALU.subtract).then_inc(split, 1)
            dve.wait_ge(v_copied, NG)
            dve.wait_ge(q_split, NG)
            dve.wait_ge(k_split, NG)
            for r in range(2):
                dve.wait_ge(q_out[r], 48 * NG // 2)
                dve.wait_ge(k_out[r], 48 * NG // 2)
            V.memset(cst[:, 9:10], 0.0).then_inc(phase_done, 1)
            maskp = m2["maskprev"].bitcast(U32).unsqueeze(1).broadcast_to([P, HQ, P])
            def softmax_input(i):
                c, r = i // NQ, i % 2
                first = c % (NT // B) == 0
                dve.wait_ge(s_ready, i + 1)
                if i >= 2:
                    dve.wait_ge(p_ready, i - 1)
                prev, cur = PSQ[r][:, :, 0:P], PSQ[r][:, :, P:2 * P]
                st(V.copy_predicated(cur, maskp, NGT if first else prev))
                st.wait()
                V.tensor_reduce(NM[:, r, :], cur, AX_X, ALU.max, negate=True).then_inc(d_ready, 1)

            def v_difference(c):
                if c >= 2:
                    dve.wait_ge(pv_ready, NQ * (c - 1))
                n = max(c, 1)
                V.tensor_tensor(VD[:, c % 2, :, :], VN[:, n, :, :], VN[:, n - 1, :, :], ALU.subtract).then_inc(vd_ready, 1)

            def heads_out(c):
                dve.wait_ge(o_turned, c + 1)
                if c >= 2:
                    dve.wait_ge(aoT_ready, c - 1)
                if c >= 1:
                    dve.wait_ge(ao_ready, c)
                o3 = bank[7].rearrange("p (h d) -> p h d", h=NH)
                st(V.reciprocal(RC[:, :], o3[:, :, DH]))
                st.wait()
                V.tensor_tensor(AO[c % 2].rearrange("p (h d) -> p h d", h=NH), o3[:, :, 0:DH],
                                RC[:, :].unsqueeze(2).broadcast_to([P, NH, DH]), ALU.mult).then_inc(ao_ready, 1)

            def residual(c):
                dve.wait_ge(at_ready, c + 1)
                V.tensor_tensor(XN[:, c, 0:C], XN[:, c, 0:C], bank[7][:, 0:P], ALU.add).then_inc(x3_done, 1)

            V.memset(bank[6][:, :], 0.0).then_inc(zero_bank, 1)
            for i in range(N + LAG):
                if i < N:
                    softmax_input(i)
                if i % NQ == 2 and i < N:
                    v_difference(i // NQ)
                if ends_chunk(i - LAG_SUMS):
                    heads_out((i - LAG_SUMS) // NQ)
                if ends_chunk(i - LAG_PROJ - 1):
                    residual((i - LAG_PROJ - 1) // NQ)
            dve.wait_ge(x3_done, NT)
            V.memset(cst[:, 9:10], 0.0).then_inc(phase_done, 1)
            statistics(XN, True, RMS_EPS, 8)
            dve.wait_ge(rstd_ready, 8)
            dve.wait_ge(xs_ready, 16 * NT * TOP)
            for t in range(NT):
                last = scaled(XF, XN, t)
                if t % TG == TG - 1:
                    last.then_inc(xf_ready, 1)

            def ff_add(i):
                sl = slice(i * TG, (i + 1) * TG)
                dve.wait_ge(ff_ready, i + 1)
                V.scalar_tensor_tensor(out=XN[:, sl, 0:C], in0=bank4[5 + i % 2], scalar=0.5, in1=XN[:, sl, 0:C],
                                       op0=ALU.mult, op1=ALU.add).then_inc(ff_used, 1)

            for g in range(NG + 1):
                if g < NG:
                    for f in range(NF):
                        n = g * NF + f
                        dve.wait_ge(th_ready, n + 1)
                        if f == 0 and g >= 2:
                            dve.wait_ge(ff_ready, g - 1)
                        if n >= 2:
                            dve.wait_ge(gu_used, n - 1)
                        st(V.scalar_tensor_tensor(out=t1_t[n % 2], in0=th_t[n % 2], scalar=1.0, in1=bank[1 + 2 * (n % 2)],
                                                  op0=ALU.add, op1=ALU.mult))
                        st.wait()
                        V.tensor_tensor(hf_t[g % 2][:, f * GW:(f + 1) * GW], t1_t[n % 2], bank[2 + 2 * (n % 2)],
                                        ALU.mult).then_inc(gu_used, 1)
                if g >= 1:
                    ff_add(g - 1)
            dve.wait_ge(b1_mm, 1)
            V.tensor_tensor(B1C[:, :], bank[7][:, 0:E * NF], co["b1"], ALU.add).then_inc(b1_done, 1)
            for e in range(E):
                V.tensor_scalar(MW1[:, e, :], MW1[:, e, :], co["els"][:, e:e + 1], None, ALU.mult).then_inc(w1_scaled, 1)
            dve.wait_ge(ff_used, NG)
            st(V.tensor_tensor(ACC[:, :, :], ACC[:, :, :], XN[:, :, 0:C], ALU.add))
            st.wait()
            V.memset(cst[:, 9:10], 0.0).then_inc(phase_done, 1)
            ends = [0] + [dve.value_load(BII[0:1, e:e + 1], min_val=e + 1, max_val=NBLK) for e in range(E)]
            dve.sem_inc(y_copied, 1)
            dve.wait_ge(x_turned, 1)
            V.tensor_copy(XTS, bank[4][:, 0:BW]).then_inc(xT_ready, 1)
            V.tensor_copy(IDT[:, :, :], XI[:, :, C:XW]).then_inc(xi_used, 1)
            for e in range(E):
                with dve.Fori(ends[e], ends[e + 1]) as k:
                    dve.wait_ge(x_turned, k + 2)
                    dve.wait_ge(up_ready, k * NF + NF)
                    V.tensor_copy(XTS, bank[4][:, 0:BW]).then_inc(xT_ready, 1)
                    dve.wait_ge(y_sent, k * (16 * BT) + 16)
                    dve.wait_ge(xi_used, k + 1)
                    V.tensor_scalar(DST[:, :], IDT[:, :, 1], float(e), float(NTOK), ALU.not_equal, ALU.mult).then_inc(idx_ready, 1)
                    dve.wait_ge(idx_ready, k * 2 + 1)
                    V.tensor_tensor(DSTI[:, :], DST[:, :], IDT[:, :, 0], ALU.add).then_inc(idx_ready, 1)
                    dve.wait_ge(idx_ready, k * 2 + 2)
                    V.tensor_copy(IDT[:, :, :], XI[:, :, C:XW]).then_inc(xi_used, 1)
                    for t in range(BT):
                        dve.wait_ge(dn_ready, k * BT + (t + 2))
                        V.tensor_copy(YB[t], bank[5 + t][:, 0:P]).then_inc(y_copied, 1)
            for g in range(NG):
                dve.wait_ge(y_in[g % 4], 16 * TOP * (g // 4 + 1))
                for j in range(TOP):
                    for t in range(TG):
                        n = g * TG + t
                        last = V.scalar_tensor_tensor(out=ACC[:, n, :], in0=YR[g % 4][j][:, t, :], scalar=G12[:, j, n:n + 1],
                                                      in1=ACC[:, n, :], op0=ALU.mult, op1=ALU.add)
                        if j == 0 or t < TG - 1:
                            st(last)
                    if j == 0:
                        st.wait()
                last.then_inc(out_ready, 1)


def kernel(**inp):
    import numpy as np
    import concourse.bacc as bacc
    from concourse import mybir as mb
    from concourse.bass_utils import run_bass_kernel_spmd

    def arr(name):
        return np.asarray(inp[name])

    def pack(spec, have):
        return np.ascontiguousarray(np.concatenate([have[n].reshape(have[n].shape[0], -1) for n, _ in spec], axis=1))

    a, f, t, m = "L0_attn_", "L0_ffn_", "L1_attn_", "L1_ffn_"
    slot = arr(f + "slot_init")
    w1 = arr(f + "w1")
    k, q = np.arange(P)[:, None], np.arange(P)[None, :]
    fp = np.float32
    mat0 = pack(MAT0, {"Wk": arr(a + "Wk").T, "Wv": arr(a + "Wv").T, "Wr": arr(a + "Wr").T, "Wo": arr(a + "Wo").T,
                       "w1a": w1[:C], "w1b": w1[C:], "slotT": slot.T, "slotT2": np.tile(slot.T, (1, B)),
                       "slot2": np.tile(slot, (B, 1)), "ident": np.eye(P, dtype=fp)})
    mat1 = pack(MAT1, {"Wih": arr(f + "Wih").T, "Whh": arr(f + "Whh").T, "wq": arr(f + "wq"), "wk": arr(f + "wk"),
                       "wv": arr(f + "wv"), "wvp": arr(f + "wvp"), "wo": arr(f + "wo"),
                       "blockneg": np.where(k // SLOTS == q // SLOTS, fp(0), fp(NEG))})
    wout = arr(t + "Wout").reshape(C, NF, P).transpose(2, 1, 0)
    mat2 = pack(MAT2, {"Wg": arr(t + "Wg").T, "Wv": arr(t + "Wv").T, "Wd": arr(t + "Wd").T, "Wqkv": arr(t + "Wqkv").T,
                       "Wo": arr(t + "Wo").T, "Wgate": arr(t + "Wgate").T, "Wup": arr(t + "Wup").T, "Wout": wout,
                       "maskprev": (q > k).astype(fp), "maskcur": (k <= q).astype(fp), "router": arr(m + "router_w").T,
                       "tri": (k < q).astype(fp), "ones": np.ones((P, P), fp)})
    cols = pack(COLS, {"mk": arr(a + "time_mix_k")[:, None], "mv": arr(a + "time_mix_v")[:, None],
                       "mr": arr(a + "time_mix_r")[:, None], "decay": arr(a + "time_decay")[:, None],
                       "first": arr(a + "time_first")[:, None], "ln_w": arr(a + "ln_w")[:, None],
                       "ln_b": arr(a + "ln_b")[:, None], "bvp": arr(f + "bvp")[:, None],
                       "w_mix": arr(t + "w_rms_mix")[:, None], "bg": arr(t + "bg")[:, None], "bv": arr(t + "bv")[:, None],
                       "bd": arr(t + "bd")[:, None], "w_attn": arr(t + "w_rms_attn")[:, None],
                       "w_ffn": arr(t + "w_rms_ffn")[:, None], "rln_s": arr(m + "router_ln_scale")[:, None],
                       "rln_b": arr(m + "router_ln_bias")[:, None], "els": arr(m + "expert_ln_scale").T,
                       "elb": arr(m + "expert_ln_bias").T,
                       "b1": arr(m + "b1").reshape(E, NF, P).transpose(2, 0, 1)})
    rows = np.concatenate([arr(f + "b2"), arr(f + "tau"), arr(f + "bih"), arr(f + "bhh"), arr(f + "bv"), arr(f + "ln_g"),
                           arr(f + "ln_b"), arr(f + "bo"), arr(m + "router_b"), np.arange(E, dtype=fp),
                           np.arange(NTOK // BW, dtype=fp) * fp(BW)])
    host = {
        "x": arr("L0_attn_x").reshape(NTOK, C), "mat0": mat0, "mat1": mat1, "mat2": mat2, "cols": cols, "rows": rows,
        "w2s": arr(f + "w2"), "bqk": np.stack([arr(f + "bq"), arr(f + "bk")], axis=1), "b1s": arr(f + "b1")[:, None],
        "moe_w1": arr(m + "w1").transpose(2, 0, 1), "moe_w2": arr(m + "w2").reshape(E, C, NF, P).transpose(3, 0, 2, 1),
        "moe_b2": arr(m + "b2"),
        "ids": (PAD_ID + np.arange(XTILES)[None, :] * P + np.arange(P)[:, None]).astype(fp),
    }
    nc = bacc.Bacc("TRN2", target_bir_lowering=False, num_devices=1)
    arrays, args = {}, []
    for name, v in host.items():
        v = np.ascontiguousarray(v)
        arrays[f"in_{name}"] = v
        args.append(nc.dram_tensor(f"in_{name}", v.shape, mb.dt.from_np(v.dtype), kind="ExternalInput").ap())
    out = nc.dram_tensor("out_x", (NTOK, C), F32, kind="ExternalOutput").ap()
    build(nc, *args, out)
    r = run_bass_kernel_spmd(nc, [arrays], core_ids=[0])
    return r.results[0]["out_x"].reshape(B, T, C)
```

```python
from contextlib import ExitStack

import concourse.bass as bass
from concourse import mybir

P = 128
F32 = mybir.dt.float32
BF16 = mybir.dt.bfloat16
U32 = mybir.dt.uint32
I32 = mybir.dt.int32
ALU = mybir.AluOpType
ACT = mybir.ActivationFunctionType
AX_X = mybir.AxisListType.X

B, T, C = 2, 2048, 128
NTOK = B * T
NT = NTOK // P
TG = 4
GW = TG * P
NG = NT // TG
QT = NT // 4
GB = NG // B
SLOTS = 64
NH, DH, DHP = 16, 8, 9
NPART = 6
QP = (0, 0, 1, 1, 0, 2)
KP = (0, 1, 0, 1, 2, 0)
DFF, NF = 512, 4
E = 8
TOP = 2
BT = 2
BW = BT * P
NBLK = TOP * NTOK // BW + E
XTILES = BT * (NBLK + 1)
XW = C + 2
PAD_ID = TOP * NTOK
NEG = -1.0e30
ROOTS = ([("x", 0), ("x", 1), ("xn", 0), ("x", 2), ("xn", 1), ("x", 3), ("xn", 2), ("xn", 3), ("slots", 0)]
         + [("x1", 0), ("x1", 1), ("x1n", 0), ("x1", 2), ("x1n", 1), ("x1", 3), ("x1n", 2), ("x1n", 3)]
         + [("x2", q) for q in range(4)] + [("x3", q) for q in range(4)])
LN_EPS, RMS_EPS, MOE_EPS = 1e-5, 1e-6, 1e-6
HQ = 4
NQ = NH // HQ
R3 = 3

MAT0 = [("Wk", 128), ("Wv", 128), ("Wr", 128), ("Wo", 128), ("w1a", 64), ("w1b", 64),
        ("slotT", 64), ("slotT2", 128), ("slot2", 128), ("ident", 128)]
MAT1 = [("Wih", 384), ("Whh", 384), ("wq", 32), ("wk", 32), ("wv", 128), ("wvp", 128), ("wo", 128), ("blockneg", 128)]
MAT2 = [("Wg", 128), ("Wv", 128), ("Wd", 128), ("Wqkv", 384), ("Wo", 128), ("Wgate", 512), ("Wup", 512),
        ("Wout", 512), ("maskprev", 128), ("maskcur", 128), ("router", 8),
        ("tri", 128), ("ones", 128)]
COLS = [("mk", 1), ("mv", 1), ("mr", 1), ("decay", 1), ("first", 1), ("ln_w", 1), ("ln_b", 1), ("bvp", 1),
        ("w_mix", 1), ("bg", 1), ("bv", 1), ("bd", 1), ("w_attn", 1), ("w_ffn", 1), ("rln_s", 1), ("rln_b", 1),
        ("els", 8), ("elb", 8), ("b1", 32)]
ROWS = [("b2", 64), ("tau", 1), ("bih", 384), ("bhh", 384), ("bv", 128), ("ln_g", 128), ("ln_b", 128),
        ("bo", 128), ("router_b", 8), ("iota8", 8), ("iota_blk", NTOK // BW)]


def root_no(of, q):
    return ROOTS.index((of, q)) + 1


def quarter(q):
    return slice(q * QT, (q + 1) * QT)


def places(pack):
    at, out = 0, {}
    for name, n in pack:
        out[name] = (at, at + n)
        at += n
    return out, at


def build(nc, x, mat0, mat1, mat2, cols, rows, w2s, bqk, b1s, moe_w1, moe_w2, moe_b2, ids, out):
    p0, n0 = places(MAT0)
    p1, n1 = places(MAT1)
    p2, n2 = places(MAT2)
    pc, ncol = places(COLS)
    pr, nrow = places(ROWS)
    x_v = x.rearrange("(t p) c -> p t c", p=P)
    out_v = out.rearrange("(t p) c -> p t c", p=P)
    q_dram = nc.dram_tensor("q_parts", [3, NH, DH, NTOK], BF16, kind="Internal").ap()
    k_dram = nc.dram_tensor("k_parts", [3, NH, DH, NTOK], BF16, kind="Internal").ap()

    xs_dram = nc.dram_tensor("x_sorted", [XTILES * P, XW], F32, kind="Internal").ap()
    y_dram = nc.dram_tensor("y_by_choice", [PAD_ID + NTOK + XTILES * P, C], F32, kind="Internal").ap()

    with ExitStack() as ctx:
        def sb(name, shape, dt=F32):
            return ctx.enter_context(nc.sbuf_tensor(name, shape, dt))

        def sem(name):
            return ctx.enter_context(nc.semaphore(name))

        M0, M1, M2 = sb("M0", [P, n0]), sb("M1", [P, n1]), sb("M2", [P, n2])
        CO, RO = sb("CO", [P, ncol]), sb("RO", [P, nrow])
        W2S, BQK, B1S = sb("W2S", [64, 64]), sb("BQK", [32, 2]), sb("B1S", [64, 1])
        B2E = sb("B2E", [E, P])
        ACC = sb("ACC", [P, NT, C])
        XN = sb("XN", [P, NT, C + 1])
        BIG = sb("BIG", [P, 4 * NTOK])
        SM = sb("SM", [P, 4096])

        m0 = {k: M0[:, a:b] for k, (a, b) in p0.items()}
        m1 = {k: M1[:, a:b] for k, (a, b) in p1.items()}
        m2 = {k: M2[:, a:b] for k, (a, b) in p2.items()}
        co = {k: CO[:, a:b] for k, (a, b) in pc.items()}
        ro = {k: RO[:, a:b] for k, (a, b) in pr.items()}
        ident = m0["ident"]

        ST = sb("ST", [P, NT, 6])
        MV = sb("MV", [P, NT, 2])
        VE = sb("VE", [P, NT])
        RS, RS1 = sb("RS", [P, NT]), sb("RS1", [P, NT])
        VE2, RS2 = sb("VE2", [P, NT]), sb("RS2", [P, NT])
        MH = sb("MH", [P, NT])
        cst = sb("cst", [P, 16])
        DEC = sb("DEC", [P, GW])

        PS = ctx.enter_context(nc.psum_tensor("PS", [P, 8, 512], F32))
        bank = [PS[:, i, :] for i in range(8)]
        bank4 = [b.rearrange("p (t c) -> p t c", t=TG) for b in bank]

        XH = BIG[:, 0:NTOK].rearrange("p (t c) -> p t c", t=NT)
        XT = BIG[:, NTOK:NTOK + B * (T + 1)].rearrange("p (b t) -> p b t", b=B)
        o = NTOK + B * (T + 1) + 2
        LG = BIG[:, o:o + NT * SLOTS].rearrange("p (t s) -> p t s", t=NT)
        o += NT * SLOTS
        LR = BIG[:, o:o + NT * SLOTS].rearrange("p (t s) -> p t s", t=NT)
        o += NT * SLOTS
        xnT = [BIG[:, o + 512 * i:o + 512 * i + 512] for i in range(2)]
        o += 1024
        R2 = sb("R2", [P, 2048])
        mixed = [[BIG[:, o + 512 * j:o + 512 * j + 512] for j in range(3)], [R2[:, 512 * j:512 * j + 512] for j in range(3)]]
        assert o + 1536 <= 4 * NTOK
        V8 = sb("V8", [P, NT, 8])
        I8 = sb("I8", [P, NT, 8], U32)
        hT = [SM[0:64, 512 * i:512 * i + 512] for i in range(2)]
        rT = [SM[:, 1024 + 512 * i:1024 + 512 * i + 512] for i in range(2)]
        rw = [SM[:, 2048 + 512 * i:2048 + 512 * i + 512] for i in range(2)]
        SS = [SM[:, 3072 + 512 * i:3072 + 512 * i + 512] for i in range(2)]
        dif = [sb("dif", [P, GW])[:, :], R2[:, 1536:2048]]

        ld_m0, ld_x, ld_m1, ld_m2 = sem("ld_m0"), [sem(f"ld_x{i}") for i in range(4)], sem("ld_m1"), sem("ld_m2")
        ld_small = sem("ld_small")
        ld_w1, ld_w2, x3_added = sem("ld_w1"), sem("ld_w2"), sem("x3_added")
        dve_step, act_step, pool_step = sem("dve_step"), sem("act_step"), sem("pool_step")
        xn_quarter, xn_added, dif_ready = sem("xn_quarter"), sem("xn_added"), sem("dif_ready")
        alpha_max, alpha_exp, alpha_ready = sem("alpha_max"), sem("alpha_exp"), sem("alpha_ready")
        var_ready, rstd_ready = sem("var_ready"), sem("rstd_ready")
        xh_ready, xn_ready = sem("xh_ready"), sem("xn_ready")
        xhT_ready, xt_ready, xnT_ready, xnTs_ready = sem("xhT_ready"), sem("xt_ready"), sem("xnT_ready"), sem("xnTs_ready")
        pre_ready = sem("pre_ready")
        h1_ready, h_ready, logit_ready, logit_used = sem("h1_ready"), sem("h_ready"), sem("logit_ready"), sem("logit_used")
        mix_ready, kvr_ready, kv_used, r_ready, rw_ready = sem("mix_ready"), sem("kvr_ready"), sem("kv_used"), sem("r_ready"), sem("rw_ready")
        y_ready, y_used = sem("y_ready"), sem("y_used")
        pre_mm, col_ready = sem("pre_mm"), sem("col_ready")
        slot_pe, slot_act, slot_dve, slot_pool = sem("slot_pe"), sem("slot_act"), sem("slot_dve"), sem("slot_pool")
        fills = sem("fills")
        phase_done = sem("phase_done")
        act_pre, q_hi, v8_ready, k_hi = sem("act_pre"), sem("q_hi"), sem("v8_ready"), sem("k_hi")

        def meet(eng, k):
            eng.wait_ge(phase_done, k)

        class Steps:
            def __init__(self, eng, s):
                self.eng, self.s, self.n = eng, s, 0

            def __call__(self, ins):
                self.n += 1
                ins.then_inc(self.s, 1)

            def wait(self):
                self.eng.wait_ge(self.s, self.n)

        def batch(b):
            return slice(b * NT // B, (b + 1) * NT // B)

        block = ctx.enter_context(nc.Block())

        def slot_tile(i, n=P):
            return BIG[:, i:i + n]

        s1 = NTOK + B * (T + 1) + 2 + 2 * NT * SLOTS
        rden_t = sb("rden_t", [P, NT])
        si_t, siT_t = BIG[:, s1:s1 + 128], BIG[:, s1 + 128:s1 + 256]
        rz_t, hn_t = BIG[:, s1 + 256:s1 + 512], BIG[:, s1 + 512:s1 + 640]
        n_t, z_t = BIG[:, s1 + 640:s1 + 768], BIG[:, s1 + 768:s1 + 896]
        sn_t, snT_t = BIG[:, s1 + 896:s1 + 1024], BIG[:, s1 + 1024:s1 + 1152]
        qk_t = BIG[0:32, s1 + 1152:s1 + 1408].rearrange("p (a s) -> p a s", a=2)
        vv_t = BIG[:, s1 + 1408:s1 + 1536]
        sc_t, pe_t, pT_t = BIG[:, s1 + 1536:s1 + 1664], BIG[:, s1 + 1664:s1 + 1792], BIG[:, s1 + 1792:s1 + 1920]
        yy_t, yT_t, svT_t = BIG[:, s1 + 1920:s1 + 2048], BIG[:, s1 + 2048:s1 + 2176], BIG[:, s1 + 2176:s1 + 2304]
        col_t = sb("col_t", [P, 8])
        SVO = sb("SVO", [SLOTS, B, P])

        XL = BIG[:, 0:NT * XW].rearrange("p (t c) -> p t c", t=NT)
        XLT = BIG[:, NT * XW:NT * XW + NTOK]
        o = NTOK + B * (T + 1) + 2 + NT * SLOTS
        XR = BIG[:, o:o + NT * P].rearrange("p (t c) -> p t c", t=NT)
        assert o + NT * P <= 4 * NTOK
        AT = BIG[0:SLOTS, 0:NTOK]
        o += NT * P

        xrT = [SM[:, 1024 + 512 * i:1536 + 512 * i] for i in range(2)]
        tg_t = [SM[:, 2048 + 512 * i:2560 + 512 * i] for i in range(2)]
        tv_t = [SM[:, 3072 + 512 * i:3584 + 512 * i] for i in range(2)]
        ta_t = [R2[:, 512 * i:512 * i + 512] for i in range(2)]
        hh_t = [R2[:, 1024 + 512 * i:1536 + 512 * i] for i in range(2)]
        alphaT_ready, alphaTs_ready, o_ready, x1_ready = sem("alphaT_ready"), sem("alphaTs_ready"), sem("o_ready"), sem("x1_ready")
        xr2_ready, tr_ready, trs_ready = sem("xr2_ready"), sem("tr_ready"), sem("trs_ready")
        gvd_ready, gate_ready, gvd_used = sem("gvd_ready"), sem("gate_ready"), sem("gvd_used")
        scan_ready, hT_ready, hT_used = sem("scan_ready"), sem("hT_ready"), sem("hT_used")
        xl_ready, xl_last, xlT_ready, xlTs_ready = sem("xl_ready"), sem("xl_last"), sem("xlT_ready"), sem("xlTs_ready")
        rl_ready, gates_ready = sem("rl_ready"), sem("gates_ready")

        x3T = [SM[:, 512 * i:512 * i + 512] for i in range(2)]
        part = [[SM[:, 1024 + 768 * i + 256 * j:1280 + 768 * i + 256 * j].bitcast(BF16) for j in range(3)] for i in range(2)]
        part2 = [[R2[:, 768 * i + 256 * j:768 * i + 256 * j + 256].bitcast(BF16) for j in range(3)] for i in range(2)]
        rest = [SM[:, 2560 + 512 * i:3072 + 512 * i] for i in range(2)]
        VN = sb("VN", [P, NT, NH, DHP])
        VD = sb("VD", [P, 2, NH, DHP])
        x2_ready = sem("x2_ready")
        x3_ready, x3T_ready, x3Ts_ready = sem("x3_ready"), sem("x3T_ready"), sem("x3Ts_ready")
        qkv_ready, q_split, k_split, v_copied = sem("qkv_ready"), sem("q_split"), sem("k_split"), sem("v_copied")
        q_out, k_out = [sem("q_out0"), sem("q_out1")], [sem("k_out0"), sem("k_out1")]

        o = NT * XW
        CW = 2 * P
        QS = [BIG[0:48, o + 2048 * i:o + 2048 * i + 2048].bitcast(BF16).rearrange("p (h t) -> p h t", h=NH) for i in range(2)]
        o += 4096
        KS = [BIG[0:48, o + 3072 * i:o + 3072 * i + 3072].bitcast(BF16).rearrange("p (h t) -> p h t", h=NH) for i in range(2)]
        o += 6144
        assert o <= 4 * NTOK
        FN = 11
        SM2 = sb("SM2", [P, (2 + 3 * R3 - 8) * 512])
        assert FN * XW <= (2 + 3 * R3 - 8) * 512
        tiles4 = [a[:, 512 * i:512 * i + 512].rearrange("p (h k) -> p h k", h=HQ)
                  for a, n in ((SM, 8), (SM2, 3 * R3 - 6)) for i in range(n)]
        P4, PT4, PC4 = [tiles4[0], tiles4[1], tiles4[7]], [tiles4[5], tiles4[6], tiles4[8]], tiles4[2:5]
        ROT = 2 * NQ
        OT = [R2[:, P * i:P * i + P] for i in range(ROT)]
        AO = [R2[:, 1024 + P * i:1024 + P * i + P] for i in range(2)]
        aoT = [R2[:, 1280 + P * i:1280 + P * i + P] for i in range(2)]
        ot_copied, o_turned, zero_bank = sem("ot_copied"), sem("o_turned"), sem("zero_bank")
        NGT_t = sb("NGT", [P, HQ * P])
        NGT = NGT_t[:, :].rearrange("p (h k) -> p h k", h=HQ)
        PSQ = [PS[:, 2 * r:2 * r + 2, :].rearrange("p b (h k) -> p (b h) k", h=2) for r in range(2)]
        zero_col = cst[:, 4:5]
        BLT, G2 = sb("BLT", [P, E]), sb("G2", [P, NT, E])
        NM = sb("NM", [P, 2, HQ])
        RC = sb("RC", [P, NH])
        q_in, k_in = [sem("q_in0"), sem("q_in1")], [sem("k_in0"), sem("k_in1")]
        s_ready, s_used, d_ready, p_ready = sem("s_ready"), sem("s_used"), sem("d_ready"), sem("p_ready")
        pt_ready, pts_ready, pc_ready, pv_ready = sem("pt_ready"), sem("pts_ready"), sem("pc_ready"), sem("pv_ready")
        vd_ready, ao_ready, aoT_ready, aoTs_ready, at_ready, x3_done = sem("vd_ready"), sem("ao_ready"), sem("aoT_ready"), sem("aoTs_ready"), sem("at_ready"), sem("x3_done")

        XF = BIG[:, NTOK:2 * NTOK].rearrange("p (t c) -> p t c", t=NT)
        xfT = [SM[:, 512 * i:512 * i + 512] for i in range(2)]
        th_t = [SM[:, 1024 + 512 * i:1536 + 512 * i] for i in range(2)]
        t1_t = [SM[:, 2048 + 512 * i:2560 + 512 * i] for i in range(2)]
        hf_t = [BIG[:, 2 * NTOK + 2048 * i:2 * NTOK + 2048 * i + 2048] for i in range(2)]
        xf_ready, xfT_ready, xfTs_ready, gu_ready, th_ready, gu_used, ff_ready, ff_used = (
            sem("xf_ready"), sem("xfT_ready"), sem("xfTs_ready"), sem("gu_ready"), sem("th_ready"), sem("gu_used"),
            sem("ff_ready"), sem("ff_used"))

        MW1 = BIG[:, 0:NTOK].rearrange("p (e h) -> p e h", e=E)
        MW2 = BIG[:, 3 * NTOK:4 * NTOK].rearrange("p (e f d) -> p e f d", e=E, f=NF)
        o = 2 * NTOK
        HE = BIG[:, o:o + NF * BW].rearrange("p (f t) -> p f t", f=NF)
        o += NF * BW
        XTS = BIG[:, o:o + BW]
        o += BW
        XI = BIG[:, o:o + BT * XW].rearrange("p (t c) -> p t c", t=BT)
        o += BT * XW
        YB = [BIG[:, o + P * i:o + P * i + P] for i in range(BT)]
        YR = [[BIG[:, 1024 * i + 512 * j:1024 * i + 512 * j + 512].rearrange("p (t c) -> p t c", t=TG)
               for j in range(TOP)] for i in range(NG)]
        IDT = sb("IDT", [P, BT, 2])
        IDN = sb("IDN", [P, BT, 2])
        DST = sb("DST", [P, BT, 2])
        DSTI = sb("DSTI", [P, BT], I32)
        IDS = sb("IDS", [P, XTILES])
        GT = sb("GT", [P, NT, E])
        LE = sb("LE", [P, NT, E])
        OH = [sb("OH0", [P, NT, E]), sb("OH1", [P, NT, E])]
        CUM = sb("CUM", [P, E, NT])
        POS = sb("POS", [P, NT, E])
        ONE = sb("ONE", [P, NT])
        CMP = sb("CMP", [P, E, NTOK // BW])
        NBL, BI, BS = sb("NBL", [P, E]), sb("BI", [P, E]), sb("BS", [P, E])
        BII = sb("BII", [P, E], I32)
        PJ, PJI = sb("PJ", [P, NT, TOP]), sb("PJI", [P, NT, TOP], I32)
        G12 = sb("G12", [P, TOP, NT])
        FT = SM2[:, 0:FN * XW].rearrange("p (t c) -> p t c", t=FN)
        ft_ready, ft_out, count_mm, pos_ready, xs_ready = sem("ft_ready"), sem("ft_out"), sem("count_mm"), sem("pos_ready"), sem("xs_ready")
        m_ready, ends_ready = sem("m_ready"), sem("ends_ready")
        xi_ready, xi_used, x_turned, xT_ready = sem("xi_ready"), sem("xi_used"), sem("x_turned"), sem("xT_ready")
        idx_ready, y_copied, y_sent, y_in = sem("idx_ready"), sem("y_copied"), [sem(f"y_sent{t}") for t in range(BT)], [sem(f"y_in{g}") for g in range(NG)]
        out_ready = sem("out_ready")
        y_seen, loads_seen = sem("y_seen"), sem("loads_seen")
        B1C = sb("B1C", [P, E * NF])
        BLR = sb("BLR", [P, E])
        gTt = [SM[0:E, 512 * i:512 * i + 512] for i in range(2)]
        b1_mm, b1_done, w1_scaled = sem("b1_mm"), sem("b1_done"), sem("w1_scaled")
        gt_ready, gT_ready, gTs_ready, gb_ready, gb_used = sem("gt_ready"), sem("gT_ready"), sem("gTs_ready"), sem("gb_ready"), sem("gb_used")
        up_ready, act_ready, dn_ready, dn_used = sem("up_ready"), sem("act_ready"), sem("dn_ready"), sem("dn_used")
        st_out = sem("st_out")

        N = NT * NQ
        LAG_SUMS, LAG_HEADS, LAG_PROJ, LAG = 6, 7, 8, 11

        assert E * NF == NT

        def bias_columns(c):
            return range(2 * c - NT, 2 * c - NT + 2) if c >= NT // 2 else ()

        def ends_chunk(i):
            return 0 <= i < N and i % NQ == NQ - 1

        @block.sync
        def _(sp):
            def load_x(q):
                sp.dma_start(ACC[:, quarter(q), :], x_v[:, quarter(q), :]).then_inc(ld_x[q], 16)

            load_x(0)
            load_x(1)
            sp.dma_start(M0[:, :], mat0).then_inc(ld_m0, 16)
            for dst, src in ((CO, cols), (W2S, w2s), (BQK, bqk), (B1S, b1s), (B2E, moe_b2)):
                sp.dma_start(dst[:, :], src).then_inc(ld_small, 16)
            sp.dma_start(RO[:, :], rows.partition_broadcast(P)).then_inc(ld_small, 16)
            sp.dma_start(IDS[:, :], ids).then_inc(ld_small, 16)
            load_x(2)
            load_x(3)
            sp.dma_start(M1[:, :], mat1).then_inc(ld_m1, 16)
            sp.dma_start(M2[:, :], mat2).then_inc(ld_m2, 16)
            for n, t in enumerate(range(0, XTILES, FN)):
                w = min(FN, XTILES - t)
                sp.wait_ge(ft_ready, n + 1)
                sp.dma_start(xs_dram[t * P:(t + w) * P, :].rearrange("(t p) c -> p t c", p=P), FT[:, 0:w, :]).then_inc(ft_out, 16)
            def load_pair(i):
                if i >= 2:
                    sp.wait_ge(s_ready, 2 * NQ * (i - 1))
                if i % 2 == 0:
                    sp.wait_ge(q_out[i // 2 % 2], 48 * (i // 4 + 1))
                    sp.wait_ge(k_out[i // 2 % 2], 48 * (i // 4 + 1))
                first = i % (NT // 2 // B) == 0
                for p in range(NPART):
                    sp.dma_start(QS[i % 2][8 * p:8 * p + 8, :, :],
                                 q_dram[QP[p]].rearrange("h d t -> d h t")[:, :, i * CW:(i + 1) * CW]).then_inc(q_in[i % 2], 16)
                    lo = P if first else 0
                    sp.dma_start(KS[i % 2][8 * p:8 * p + 8, :, lo:3 * P],
                                 k_dram[KP[p]].rearrange("h d t -> d h t")[:, :, i * CW - P + lo:(i + 1) * CW]).then_inc(k_in[i % 2], 16)

            for g in range(NG):
                if g == NG - 2:
                    sp.wait_ge(x3T_ready, NG // 2)
                    load_pair(0)
                if g == NG - 1:
                    sp.wait_ge(x3T_ready, NG)
                    load_pair(1)
                for (split, parts, dram, went) in ((q_split, part, q_dram, q_out), (k_split, part2, k_dram, k_out)):
                    sp.wait_ge(split, g + 1)
                    for j in range(3):
                        sp.dma_start(dram[j].rearrange("h d t -> (h d) t")[:, g * GW:(g + 1) * GW],
                                     parts[g % 2][j]).then_inc(went[g % 2], 16)
            for i in range(2, NT // 2):
                if i == 4:
                    sp.wait_ge(xs_ready, 16 * NT * TOP)
                    sp.dma_start(MW1, moe_w1).then_inc(ld_w1, 16)
                load_pair(i)
            meet(sp, 5)
            sp.dma_start(MW2, moe_w2).then_inc(ld_w2, 16)
            sp.wait_ge(ff_ready, NG - 1)
            sp.wait_ge(ends_ready, 1)
            blocks = sp.value_load(BII[0:1, E - 1:E], min_val=E, max_val=NBLK)

            def block_rows(k):
                return xs_dram[bass.ts(k, BW), :].rearrange("(t p) c -> p t c", p=P)

            sp.dma_start(XI, block_rows(0)).then_inc(xi_ready, 16)
            with sp.Fori(0, blocks) as k:
                sp.wait_ge(xi_used, k + 1)
                sp.dma_start(XI, block_rows(k + 1)).then_inc(xi_ready, 16)
            sp.wait_ge(xi_ready, blocks * 16 + 16)
            sp.sem_inc(loads_seen, 1)
            for t in range(BT):
                sp.wait_ge(y_sent[t], blocks * 16 + 16)
                sp.sem_inc(loads_seen, 1)
            for g in range(NG):
                for j in range(TOP):
                    src = y_dram[j * NTOK + g * GW:j * NTOK + (g + 1) * GW, :].rearrange("(t p) c -> p t c", p=P)
                    sp.dma_start(YR[g][j], src).then_inc(y_in[g], 16)
            for g in range(NG):
                sp.wait_ge(out_ready, g + 1)
                sp.dma_start(out_v[:, g * TG:(g + 1) * TG, :], ACC[:, g * TG:(g + 1) * TG, :]).then_inc(st_out, 16)
            sp.wait_ge(st_out, 16 * NG)

        @block.gpsimd
        def _(pool):
            nc.gpsimd.memset(MH[:, :], -0.5).then_inc(pool_step, 1)
            pool.wait_ge(pool_step, 1)

            def root(of, q):
                sl = slice(0, 1) if of == "slots" else quarter(q)
                pool.wait_ge(var_ready, root_no(of, q))
                if of == "x1n":
                    nc.gpsimd.tensor_tensor(RS2[:, sl], VE2[:, sl], MH[:, sl], ALU.pow)
                dst = RS1 if of in ("x", "x1") else RS
                nc.gpsimd.tensor_tensor(dst[:, sl], VE[:, sl], MH[:, sl], ALU.pow).then_inc(rstd_ready, 1)

            nc.gpsimd.memset(XT[:, :, 0:1], 0.0).then_inc(fills, 1)
            nc.gpsimd.memset(XN[:, :, C:C + 1], 1.0).then_inc(fills, 1)
            nc.gpsimd.memset(VN[:, :, :, DH:DHP], 1.0).then_inc(fills, 1)
            for of, q in ROOTS[:8]:
                root(of, q)
            nc.gpsimd.memset(FT[:, :, :], 0.0).then_inc(pool_step, 1)
            pool.wait_ge(pool_step, 2)
            nc.gpsimd.memset(FT[:, :, C + 1:C + 2], -1.0).then_inc(pool_step, 1)
            pool.wait_ge(ld_small, 16 * 7)
            pool.wait_ge(pool_step, 3)

            def difference(i):
                b, o = i // GB, (i % GB) * GW
                pool.wait_ge(xt_ready, i + 1)
                if i >= 2:
                    pool.wait_ge(mix_ready, i - 1)
                nc.gpsimd.tensor_tensor(dif[i % 2], XT[:, b, o + 1:o + 1 + GW], XT[:, b, o:o + GW],
                                        ALU.subtract).then_inc(dif_ready, 1)

            def fill(n):
                t = n * FN
                w = min(FN, XTILES - t)
                if n >= 1:
                    pool.wait_ge(ft_out, 16 * n)
                nc.gpsimd.tensor_copy(FT[:, 0:w, C:C + 1], IDS[:, t:t + w].unsqueeze(2)).then_inc(ft_ready, 1)

            NFILL = (XTILES + FN - 1) // FN
            for n in range(max(NFILL, NG)):
                if n < NG:
                    difference(n)
                if 1 <= n <= 4:
                    q = n - 1
                    pool.wait_ge(xn_quarter, n)
                    nc.gpsimd.tensor_tensor(ACC[:, quarter(q), :], ACC[:, quarter(q), :], XN[:, quarter(q), 0:C],
                                            ALU.add).then_inc(xn_added, 1)
                if n < NFILL:
                    fill(n)
            for of, q in ROOTS[8:17]:
                root(of, q)
            pool.wait_ge(rstd_ready, root_no("x1n", 3))
            for q in range(4):
                pool.wait_ge(xn_quarter, 4 + q + 1)
                nc.gpsimd.tensor_tensor(XR[:, quarter(q), :], XN[:, quarter(q), 0:C],
                                        RS2[:, quarter(q)].unsqueeze(2).broadcast_to([P, QT, C]), ALU.mult).then_inc(xr2_ready, 1)
            pool.wait_ge(ft_out, 16 * NFILL)
            pool.wait_ge(pos_ready, 1)
            X2_ROOTS = (6, 11, 17, 23)
            for t in range(NT):
                for j in range(TOP):
                    pool.indirect_dma_start(xs_dram, bass.IndirectOffsetOnAxis(ap=PJI[:, t, j:j + 1], axis=0),
                                            XL[:, t, :], None).then_inc(xs_ready, 16)
                if t in X2_ROOTS:
                    root("x2", X2_ROOTS.index(t))
            meet(pool, 4)
            for r in range(2):
                pool.wait_ge(q_out[r], 48 * NG // 2)
            for i in range(NT * NQ):
                if i >= QT * NQ + LAG and (i - LAG) % (QT * NQ) == 0:
                    q = (i - LAG) // (QT * NQ) - 1
                    root("x3", q)
                pool.wait_ge(pts_ready, i + 1)
                if i >= R3:
                    pool.wait_ge(pv_ready, i - R3 + 1)
                nc.gpsimd.tensor_tensor(PC4[i % R3], PT4[i % R3], m2["maskcur"].unsqueeze(1).broadcast_to([P, HQ, P]),
                                        ALU.mult).then_inc(pc_ready, 1)
            root("x3", 3)
            for g in range(NG):
                sl = slice(g * TG, (g + 1) * TG)
                nc.gpsimd.tensor_tensor(ACC[:, sl, :], ACC[:, sl, :], XN[:, sl, 0:C], ALU.add).then_inc(x3_added, 1)
            pool.wait_ge(ends_ready, 1)
            blocks = pool.value_load(BII[0:1, E - 1:E], min_val=E, max_val=NBLK)
            for t in range(BT):
                pool.dma_start(y_dram[PAD_ID + NTOK + XTILES * P - 1 - t, 0:NT].unsqueeze(0), ONE[0:1, :]).then_inc(y_sent[t], 16)
            with pool.Fori(0, blocks) as k:
                for t in range(BT):
                    pool.wait_ge(y_copied, k * BT + (t + 2))
                    pool.sem_inc(y_seen, 1)
                    pool.indirect_dma_start(y_dram, bass.IndirectOffsetOnAxis(ap=DSTI[:, t:t + 1], axis=0),
                                            YB[t], None).then_inc(y_sent[t], 16)

        @block.tensor
        def _(pe):
            mm, tr = nc.tensor.matmul, nc.tensor.transpose

            def transposes(dst, src4, n=P):
                for t in range(TG):
                    last = tr(dst[0:n, t * P:(t + 1) * P], src4[:, t, 0:n], ident)
                return last

            pe.wait_ge(ld_m0, 16)
            pe.wait_ge(col_ready, 2)
            mm(bank[2][0:64, 0:1], m0["w1b"], col_t[:, 3:4], start=True, stop=True).then_inc(pre_mm, 1)
            for g in range(NG + 2):
                if g < NG:
                    pe.wait_ge(xh_ready, g + 1)
                    if g >= 1:
                        pe.wait_ge(xt_ready, g)
                    transposes(bank[0], XH[:, g * TG:(g + 1) * TG, :]).then_inc(xhT_ready, 1)
                    if g >= 1:
                        pe.wait_ge(xnTs_ready, g)
                    transposes(bank[1], XN[:, g * TG:(g + 1) * TG, :]).then_inc(xnT_ready, 1)
                if 1 <= g <= NG:
                    i = g - 1
                    pe.wait_ge(xnTs_ready, i + 1)
                    if i == 0:
                        pe.wait_ge(pre_ready, 1)
                    if i >= 1:
                        pe.wait_ge(h_ready, i)
                    mm(bank[2][0:64, :], m0["w1a"], xnT[i % 2], start=True, stop=True).then_inc(h1_ready, 1)
                if g >= 2:
                    i = g - 2
                    pe.wait_ge(h_ready, i + 1)
                    if i == 0:
                        pe.wait_ge(col_ready, 3)
                    if i >= 1:
                        pe.wait_ge(logit_used, i)
                    for t in range(TG):
                        last = mm(bank[3][:, t * 64:(t + 1) * 64], hT[i % 2][:, t * P:(t + 1) * P], W2S[:, :],
                                  start=True, stop=True)
                    last.then_inc(logit_ready, 1)
                if 1 <= g <= NG:
                    i = g - 1
                    pe.wait_ge(mix_ready, i + 1)
                    if i >= 1:
                        pe.wait_ge(kv_used, i)
                        pe.wait_ge(r_ready, i)
                    for j, w in enumerate(("Wk", "Wv", "Wr")):
                        last = mm(bank[4 + j], m0[w], mixed[i % 2][j], start=True, stop=True)
                    last.then_inc(kvr_ready, 1)
                if g >= 2:
                    i = g - 2
                    pe.wait_ge(rw_ready, i + 1)
                    if i >= 1:
                        pe.wait_ge(y_used, i)
                    for t in range(TG):
                        last = mm(bank4[7][:, t, :], rw[i % 2][:, t * P:(t + 1) * P], m0["Wo"], start=True, stop=True)
                    last.then_inc(y_ready, 1)
            meet(pe, 1)
            for b in range(B):
                pe.wait_ge(alpha_ready, b + 1)
                for t in range(NT // B):
                    n = b * (NT // B) + t
                    last = mm(bank[b][64 * b:64 * b + 64, 0:C + 1], LG[:, n, :], XN[:, n, :],
                              start=(t == 0), stop=(t == NT // B - 1))
            last.then_inc(slot_pe, 1)

            def alpha_turn(g):
                if g >= 1:
                    pe.wait_ge(alphaTs_ready, g)
                transposes(bank[1], LG[:, g * TG:(g + 1) * TG, :], n=SLOTS).then_inc(alphaT_ready, 1)

            pe.wait_ge(ld_m1, 16)
            for j in range(2):
                mm(bank[2][:, j * P:(j + 1) * P], m0["slotT2"], m1["Whh"][:, j * P:(j + 1) * P], start=(j == 0), stop=False,
                   skip_group_check=True)
            mm(bank[3][:, 0:P], m0["slotT2"], m1["Whh"][:, 256:384], start=True, stop=True)
            pe.wait_ge(slot_dve, 2)
            tr(bank[4][:, 0:P], si_t, ident).then_inc(slot_pe, 1)
            alpha_turn(0)
            pe.wait_ge(slot_act, 1)
            for j in range(2):
                mm(bank[2][:, j * P:(j + 1) * P], siT_t, m1["Wih"][:, j * P:(j + 1) * P], start=False, stop=(j == 1),
                   skip_group_check=True)
            mm(bank[3][:, P:2 * P], siT_t, m1["Wih"][:, 256:384], start=True, stop=True).then_inc(slot_pe, 1)
            alpha_turn(1)
            pe.wait_ge(slot_dve, 5)
            tr(bank[4][:, 0:P], sn_t, ident).then_inc(slot_pe, 1)
            alpha_turn(2)
            pe.wait_ge(slot_act, 4)
            mm(bank[5][0:32, 0:P], m1["wq"], snT_t, start=True, stop=True)
            mm(bank[5][0:32, P:2 * P], m1["wk"], snT_t, start=True, stop=True)
            mm(bank[6][:, 0:P], snT_t, m1["wv"], start=True, stop=True).then_inc(slot_pe, 1)
            alpha_turn(3)
            pe.wait_ge(slot_dve, 6)
            mm(bank[7][:, 0:P], qk_t[:, 0, :], qk_t[:, 1, :], start=True, stop=True).then_inc(slot_pe, 1)
            alpha_turn(4)
            pe.wait_ge(slot_dve, 8)
            tr(bank[4][:, 0:P], pe_t, ident).then_inc(slot_pe, 1)
            alpha_turn(5)
            pe.wait_ge(slot_act, 6)
            mm(bank[6][:, P:2 * P], pT_t, vv_t, start=True, stop=True).then_inc(slot_pe, 1)
            alpha_turn(6)
            pe.wait_ge(slot_dve, 9)
            tr(bank[4][:, 0:P], yy_t, ident).then_inc(slot_pe, 1)
            alpha_turn(7)
            pe.wait_ge(slot_act, 7)
            mm(bank[5][:, 0:P], m1["wvp"], yT_t, start=True, stop=True).then_inc(slot_pe, 1)
            pe.wait_ge(slot_act, 8)
            for b in range(B):
                last = mm(bank[0][0:64, b * P:(b + 1) * P], svT_t[:, 64 * b:64 * b + 64], m1["wo"], start=True, stop=True)
            last.then_inc(slot_pe, 1)
            meet(pe, 2)
            pe.wait_ge(alphaTs_ready, NG)
            for g in range(NG):
                if g >= 2:
                    pe.wait_ge(x1_ready, g - 1)
                for t in range(TG):
                    o = g * GW + t * P
                    last = mm(bank4[1 + g % 2][:, t, :], AT[:, o:o + P], SVO[:, g // GB, :], start=True, stop=True)
                last.then_inc(o_ready, 1)
            pe.wait_ge(ld_m2, 16)
            pe.wait_ge(x1_ready, NG)
            mm(bank[1][:, 0:E], co["rln_b"].broadcast_to([P, P]), m2["router"], start=True, stop=True)
            pe.wait_ge(col_ready, 4)
            for g in range(NG + 1):
                if g < NG:
                    if g < NG - QT // TG:
                        pe.wait_ge(xl_ready, g + 1)
                    else:
                        pe.wait_ge(xl_last, g - (NG - QT // TG) + 1)
                    if g >= 1:
                        pe.wait_ge(xlTs_ready, g)
                    transposes(bank[7], XL[:, g * TG:(g + 1) * TG, :]).then_inc(xlT_ready, 1)
                if g >= 1:
                    pe.wait_ge(xlTs_ready, g)
                    for t in range((g - 1) * TG, g * TG):
                        last = mm(bank[0][:, t * E:(t + 1) * E], XLT[:, t * P:(t + 1) * P], BLR[:, :], start=True, stop=True)
            last.then_inc(rl_ready, 1)

            def row_counts():
                pe.wait_ge(m_ready, 1)
                M2d = POS[:, :, :].rearrange("p t e -> p (t e)")
                mm(bank[1][:, 0:NT * E], m2["tri"], M2d, start=True, stop=True)
                mm(bank[0][:, 0:NT * E], m2["ones"], M2d, start=True, stop=True).then_inc(count_mm, 1)

            def gates_turn(i):
                if i == 0:
                    pe.wait_ge(gt_ready, 1)
                if i >= 1:
                    pe.wait_ge(gTs_ready, i)
                transposes(bank[7], GT[:, i * TG:(i + 1) * TG, :], n=E).then_inc(gT_ready, 1)

            def gates_bias(i):
                pe.wait_ge(gTs_ready, i + 1)
                if i == 0:
                    pe.wait_ge(pos_ready, 1)
                if i >= 2:
                    pe.wait_ge(gb_used, i - 1)
                for t in range(TG):
                    last = mm(bank4[i % 2][:, t, :], gTt[i % 2][:, t * P:(t + 1) * P], B2E[:, :], start=True, stop=True)
                last.then_inc(gb_ready, 1)

            for g in range(NG + 2):
                if g < NG:
                    pe.wait_ge(xr2_ready, g * TG // QT + 1)
                    if g >= 1:
                        pe.wait_ge(trs_ready, g)
                    transposes(bank[2], XR[:, g * TG:(g + 1) * TG, :]).then_inc(tr_ready, 1)
                if 1 <= g <= NG:
                    i = g - 1
                    pe.wait_ge(trs_ready, i + 1)
                    if i >= 1:
                        pe.wait_ge(gate_ready, i)
                    for j, w in enumerate(("Wg", "Wv", "Wd")):
                        last = mm(bank[3 + j], m2[w], xrT[i % 2], start=True, stop=True)
                    last.then_inc(gvd_ready, 1)
                if g >= 2:
                    i = g - 2
                    pe.wait_ge(scan_ready, i + 1)
                    if i >= 1:
                        pe.wait_ge(hT_used, i)
                    for t in range(TG):
                        last = tr(bank4[6][:, t, :], hh_t[i % 2][:, t * P:(t + 1) * P], ident)
                    last.then_inc(hT_ready, 1)
                if g == 1:
                    row_counts()
                if 1 <= g <= NG:
                    gates_turn(g - 1)
                if g >= 2:
                    gates_bias(g - 2)
            meet(pe, 3)
            for g in range(NG + 1):
                if g < NG:
                    pe.wait_ge(x3_ready, g + 1)
                    if g >= 1:
                        pe.wait_ge(x3Ts_ready, g)
                    transposes(bank[0], XR[:, g * TG:(g + 1) * TG, :]).then_inc(x3T_ready, 1)
                if g >= 1:
                    i = g - 1
                    pe.wait_ge(x3Ts_ready, i + 1)
                    if i >= 2:
                        pe.wait_ge(q_split, i - 1)
                        pe.wait_ge(k_split, i - 1)
                        pe.wait_ge(v_copied, i - 1)
                    o = 1 + 3 * (i % 2)
                    mm(bank[o], m2["Wqkv"][:, 0:P], x3T[i % 2], start=True, stop=True)
                    mm(bank[o + 1], m2["Wqkv"][:, P:2 * P], x3T[i % 2], start=True, stop=True)
                    for t in range(TG):
                        last = mm(bank4[o + 2][:, t, :], x3T[i % 2][:, t * P:(t + 1) * P], m2["Wqkv"][:, 2 * P:3 * P],
                                  start=True, stop=True)
                    last.then_inc(qkv_ready, 1)
            meet(pe, 4)

            def scores(i):
                c, hq = i // NQ, i % NQ
                r = (c // 2) % 2
                if i % (2 * NQ) == 0:
                    n = 16 * NPART * (c // 4 + 1)
                    pe.wait_ge(q_in[r], n)
                    pe.wait_ge(k_in[r], n)
                if i >= 2:
                    pe.wait_ge(p_ready, i - 1)
                first = c % (NT // B) == 0
                for h in range(HQ):
                    lo = P if first else 0
                    k0 = (c % 2) * P
                    last = mm(bank[2 * (i % 2) + h // 2][:, (h % 2) * 2 * P + lo:(h % 2 + 1) * 2 * P],
                              QS[r][:, hq * HQ + h, (c % 2) * P:(c % 2 + 1) * P],
                              KS[r][:, hq * HQ + h, k0 + lo:k0 + 2 * P], start=True, stop=True)
                last.then_inc(s_ready, 1)

            def weights_turn(i):
                pe.wait_ge(p_ready, i + 1)
                if i >= 2:
                    pe.wait_ge(pts_ready, i - 1)
                for h in range(HQ):
                    last = tr(bank[4 + i % 2][:, h * P:(h + 1) * P], P4[i % R3][:, h, :], ident)
                last.then_inc(pt_ready, 1)

            def weighted(i):
                c, hq = i // NQ, i % NQ
                first = c % (NT // B) == 0
                pe.wait_ge(pc_ready, i + 1)
                if i >= 1:
                    pe.wait_ge(ot_copied, i)
                if hq == 0 and not first:
                    pe.wait_ge(vd_ready, c + 1)
                for h in range(HQ):
                    hh = hq * HQ + h
                    dst = bank[6][32 * h:32 * h + DHP, 0:P]
                    if first:
                        last = mm(dst, VN[:, c, hh, :], PT4[i % R3][:, h, :], start=True, stop=True)
                    else:
                        mm(dst, VN[:, c - 1, hh, :], PT4[i % R3][:, h, :], start=True, stop=False)
                        last = mm(dst, VD[:, c % 2, hh, :], PC4[i % R3][:, h, :], start=False, stop=True)
                last.then_inc(pv_ready, 1)

            def sums_turn(c):
                pe.wait_ge(ot_copied, NQ * (c + 1))
                if c >= 1:
                    pe.wait_ge(x3_done, c)
                for hq in range(NQ):
                    last = tr(bank[7][:, hq * P:(hq + 1) * P], OT[(c * NQ + hq) % ROT], ident)
                last.then_inc(o_turned, 1)

            def heads_turn(c):
                pe.wait_ge(ao_ready, c + 1)
                tr(bank[7][:, 0:P], AO[c % 2], ident).then_inc(aoT_ready, 1)

            def out_proj(c):
                pe.wait_ge(aoTs_ready, c + 1)
                last = mm(bank[7][:, 0:P], aoT[c % 2], m2["Wo"], start=True, stop=True)
                if c == NT // 2:
                    pe.wait_ge(ld_w1, 16)
                for j, n in enumerate(bias_columns(c)):
                    e, f = n // NF, n % NF
                    last = mm(bank[7][:, P + j:P + j + 1], MW1[:, e, f * P:(f + 1) * P], co["elb"][:, e:e + 1],
                              start=True, stop=True)
                last.then_inc(at_ready, 1)

            pe.wait_ge(zero_bank, 1)
            for i in range(N + LAG):
                if i < N:
                    scores(i)
                if 2 <= i <= N + 1:
                    weights_turn(i - 2)
                if ends_chunk(i - LAG_SUMS):
                    sums_turn((i - LAG_SUMS) // NQ)
                if 4 <= i <= N + 3:
                    weighted(i - 4)
                if ends_chunk(i - LAG_HEADS):
                    heads_turn((i - LAG_HEADS) // NQ)
                if ends_chunk(i - LAG_PROJ):
                    out_proj((i - LAG_PROJ) // NQ)
            ends = [0] + [pe.value_load(BII[0:1, e:e + 1], min_val=e + 1, max_val=NBLK) for e in range(E)]
            meet(pe, 5)

            def gate_up(i):
                for f in range(NF):
                    n = i * NF + f
                    if n >= 2:
                        pe.wait_ge(gu_used, n - 1)
                    mm(bank[1 + 2 * (n % 2)], m2["Wgate"][:, f * P:(f + 1) * P], xfT[i % 2], start=True, stop=True)
                    mm(bank[2 + 2 * (n % 2)], m2["Wup"][:, f * P:(f + 1) * P], xfT[i % 2], start=True,
                       stop=True).then_inc(gu_ready, 1)

            for g in range(NG + 2):
                if g < NG:
                    pe.wait_ge(xf_ready, g + 1)
                    if g >= 1:
                        pe.wait_ge(xfTs_ready, g)
                    transposes(bank[0], XF[:, g * TG:(g + 1) * TG, :]).then_inc(xfT_ready, 1)
                if 1 <= g <= NG:
                    pe.wait_ge(xfTs_ready, g)
                    gate_up(g - 1)
                if g >= 2:
                    i = g - 2
                    pe.wait_ge(gu_used, NF * (i + 1))
                    if i >= 2:
                        pe.wait_ge(ff_used, i - 1)
                    for t in range(TG):
                        for f in range(NF):
                            last = mm(bank4[5 + i % 2][:, t, :], hf_t[i % 2][:, f * GW + t * P:f * GW + (t + 1) * P],
                                      m2["Wout"][:, f * P:(f + 1) * P], start=(f == 0), stop=(f == NF - 1))
                    last.then_inc(ff_ready, 1)

            def turn_block():
                for t in range(BT):
                    last = tr(bank[4][:, t * P:(t + 1) * P], XI[:, t, 0:C], ident)
                last.then_inc(x_turned, 1)

            pe.sem_inc(dn_ready, 1)
            pe.wait_ge(xi_ready, 16)
            turn_block()
            pe.wait_ge(w1_scaled, E)
            pe.wait_ge(ld_w2, 16)
            for e in range(E):
                with pe.Fori(ends[e], ends[e + 1]) as k:
                    pe.wait_ge(xT_ready, k + 1)
                    pe.wait_ge(act_ready, k * NF + 1)
                    for f in range(NF):
                        mm(bank[f][:, 0:BW], MW1[:, e, f * P:(f + 1) * P], XTS, start=True, stop=True).then_inc(up_ready, 1)
                    pe.wait_ge(xi_ready, k * 16 + 32)
                    turn_block()
                    for t in range(BT):
                        pe.wait_ge(y_copied, k * BT + 1)
                        for f in range(NF):
                            if t == 0:
                                pe.wait_ge(act_ready, k * NF + (f + 2))
                            last = mm(bank[5 + t][:, 0:P], HE[:, f, t * P:(t + 1) * P], MW2[:, e, f, :],
                                      start=(f == 0), stop=(f == NF - 1))
                        last.then_inc(dn_ready, 1)

        @block.scalar
        def _(act):
            A = nc.scalar.activation
            act.wait_ge(ld_small, 16 * 7)
            A(col_t[:, 4:5], co["decay"], ACT.Tanh, scale=0.5).then_inc(act_pre, 1)
            A(col_t[:, 1:2], co["first"], ACT.Exp).then_inc(act_pre, 1)
            A(col_t[:, 2:3], ro["tau"], ACT.Abs).then_inc(act_pre, 1)
            def second_norm(g):
                if g * TG % QT == 0:
                    act.wait_ge(rstd_ready, root_no("xn", g * TG // QT))
                    act.wait_ge(xn_quarter, g * TG // QT + 1)
                for t in range(g * TG, (g + 1) * TG):
                    last = A(XH[:, t, :], XN[:, t, 0:C], ACT.Identity, bias=zero_col, scale=RS[:, t:t + 1])
                last.then_inc(xh_ready, 1)

            second_norm(0)
            second_norm(1)
            for g in range(NG + 1):
                if g < NG:
                    b, o = g // GB, 1 + (g % GB) * GW
                    act.wait_ge(xhT_ready, g + 1)
                    A(XT[:, b, o:o + GW], bank[0], ACT.Identity, bias=co["ln_b"], scale=co["ln_w"]).then_inc(xt_ready, 1)
                    act.wait_ge(xnT_ready, g + 1)
                    if g >= 2:
                        act.wait_ge(h1_ready, g - 1)
                    nc.scalar.copy(xnT[g % 2], bank[1]).then_inc(xnTs_ready, 1)
                if g >= 1:
                    i = g - 1
                    act.wait_ge(h1_ready, i + 1)
                    if i == 0:
                        act.wait_ge(pre_ready, 1)
                    if i >= 2:
                        act.wait_ge(logit_ready, i - 1)
                    A(hT[i % 2], bank[2][0:64, :], ACT.Gelu, bias=B1S[:, :]).then_inc(h_ready, 1)
                if g + 2 < NG:
                    second_norm(g + 2)
                if g >= 1:
                    i = g - 1
                    act.wait_ge(kvr_ready, i + 1)
                    if i >= 2:
                        act.wait_ge(rw_ready, i - 1)
                    A(rT[i % 2], bank[6], ACT.Tanh, scale=0.5).then_inc(r_ready, 1)
            for b in range(B):
                act.wait_ge(alpha_max, b + 1)
                A(LG[:, batch(b), :], LG[:, batch(b), :], ACT.Exp).then_inc(alpha_exp, 1)

            def alpha_copy(g):
                act.wait_ge(alphaT_ready, g + 1)
                nc.scalar.copy(AT[:, g * GW:(g + 1) * GW], bank[1][0:64, :]).then_inc(alphaTs_ready, 1)

            act.wait_ge(slot_pe, 2)
            nc.scalar.copy(siT_t, bank[4][:, 0:P]).then_inc(slot_act, 1)
            alpha_copy(0)
            act.wait_ge(slot_dve, 3)
            A(rz_t, rz_t, ACT.Tanh, scale=0.5).then_inc(slot_act, 1)
            alpha_copy(1)
            act.wait_ge(slot_dve, 4)
            A(n_t, n_t, ACT.Tanh).then_inc(slot_act, 1)
            act.wait_ge(slot_pe, 4)
            nc.scalar.copy(snT_t, bank[4][:, 0:P]).then_inc(slot_act, 1)
            alpha_copy(2)
            alpha_copy(3)
            alpha_copy(4)
            act.wait_ge(slot_dve, 7)
            A(pe_t, sc_t, ACT.Exp, bias=cst[:, 2:3], accum_out=cst[:, 3:4]).then_inc(slot_act, 1)
            act.wait_ge(slot_pe, 7)
            nc.scalar.copy(pT_t, bank[4][:, 0:P]).then_inc(slot_act, 1)
            alpha_copy(5)
            alpha_copy(6)
            act.wait_ge(slot_pe, 9)
            nc.scalar.copy(yT_t, bank[4][:, 0:P]).then_inc(slot_act, 1)
            alpha_copy(7)
            act.wait_ge(slot_pe, 10)
            A(svT_t, bank[5][:, 0:P], ACT.Identity, bias=co["bvp"]).then_inc(slot_act, 1)
            act.wait_ge(o_ready, NG)
            for g in range(NG + 1):
                if g < NG - QT // TG:
                    if g * TG % QT == 0:
                        act.wait_ge(rstd_ready, root_no("x1n", g * TG // QT))
                        act.wait_ge(xn_quarter, 4 + g * TG // QT + 1)
                    for t in range(g * TG, (g + 1) * TG):
                        last = A(XL[:, t, 0:C], XN[:, t, 0:C], ACT.Identity, bias=zero_col, scale=RS[:, t:t + 1])
                    last.then_inc(xl_ready, 1)
                if g >= 1:
                    i = g - 1
                    act.wait_ge(xlT_ready, i + 1)
                    nc.scalar.copy(XLT[:, i * GW:(i + 1) * GW], bank[7]).then_inc(xlTs_ready, 1)
            act.wait_ge(gates_ready, 1)
            A(LE[:, :, :], LE[:, :, :], ACT.Exp).then_inc(gates_ready, 1)
            for g in range(NG + 1):
                if g < NG:
                    act.wait_ge(tr_ready, g + 1)
                    if g >= 2:
                        act.wait_ge(gvd_ready, g - 1)
                    A(xrT[g % 2], bank[2], ACT.Identity, bias=zero_col, scale=co["w_mix"]).then_inc(trs_ready, 1)
                if g >= 1:
                    i = g - 1
                    act.wait_ge(gvd_ready, i + 1)
                    if i >= 2:
                        act.wait_ge(scan_ready, i - 1)
                    A(tg_t[i % 2], bank[3], ACT.Tanh, scale=0.5, bias=cst[:, 0:1])
                    A(tv_t[i % 2], bank[4], ACT.Tanh, bias=co["bv"])
                    A(ta_t[i % 2], bank[5], ACT.Tanh, scale=0.5, bias=cst[:, 1:2]).then_inc(gate_ready, 1)
                    act.wait_ge(gT_ready, i + 1)
                    if i >= 2:
                        act.wait_ge(gb_ready, i - 1)
                    nc.scalar.copy(gTt[i % 2], bank[7][0:E, :]).then_inc(gTs_ready, 1)

            def scale_x2(g):
                if g * TG % QT == 0:
                    act.wait_ge(rstd_ready, root_no("x2", g * TG // QT))
                for t in range(g * TG, (g + 1) * TG):
                    last = A(XR[:, t, :], XN[:, t, 0:C], ACT.Identity, bias=zero_col, scale=RS[:, t:t + 1])
                last.then_inc(x3_ready, 1)

            scale_x2(0)
            for g in range(NG + 1):
                if g + 1 < NG:
                    scale_x2(g + 1)
                if g < NG:
                    act.wait_ge(x3T_ready, g + 1)
                    if g >= 2:
                        act.wait_ge(qkv_ready, g - 1)
                    A(x3T[g % 2], bank[0], ACT.Identity, bias=zero_col, scale=co["w_attn"]).then_inc(x3Ts_ready, 1)
                if g >= 1:
                    i = g - 1
                    o = 1 + 3 * (i % 2)
                    act.wait_ge(qkv_ready, i + 1)
                    if i >= 2:
                        act.wait_ge(q_out[i % 2], 48 * (i // 2))
                        act.wait_ge(k_out[i % 2], 48 * (i // 2))
                    A(part[i % 2][0], bank[o], ACT.Copy, scale=DH ** -0.5).then_inc(q_hi, 1)
                    nc.scalar.copy(part2[i % 2][0], bank[o + 1]).then_inc(k_hi, 1)
                    nc.scalar.copy(VN[:, i * TG:(i + 1) * TG, :, 0:DH],
                                   bank[o + 2].rearrange("p (t h d) -> p t h d", t=TG, h=NH)).then_inc(v_copied, 1)
            def sums_copied(j):
                act.wait_ge(pv_ready, j + 1)
                if j == 0:
                    for r in range(2):
                        act.wait_ge(k_out[r], 48 * NG // 2)
                if j >= ROT:
                    act.wait_ge(o_turned, (j - ROT) // NQ + 1)
                nc.scalar.copy(OT[j % ROT], bank[6][:, 0:P]).then_inc(ot_copied, 1)

            def exps(i):
                act.wait_ge(d_ready, i + 1)
                if i >= R3:
                    act.wait_ge(pt_ready, i - R3 + 1)
                for h in range(HQ):
                    if h == 1 and i >= 4:
                        sums_copied(i - 4)
                    last = A(P4[i % R3][:, h, :], PSQ[i % 2][:, h, P:2 * P], ACT.Exp, bias=NM[:, i % 2, h:h + 1])
                last.then_inc(p_ready, 1)

            def turned(i):
                act.wait_ge(pt_ready, i + 1)
                if i >= R3:
                    act.wait_ge(pv_ready, i - R3 + 1)
                    act.wait_ge(pc_ready, i - R3 + 1)
                nc.scalar.copy(PT4[i % R3], bank4[4 + i % 2]).then_inc(pts_ready, 1)

            for i in range(N + LAG):
                if ends_chunk(i - LAG_HEADS - 1):
                    c = (i - LAG_HEADS - 1) // NQ
                    act.wait_ge(aoT_ready, c + 1)
                    if c >= 2:
                        act.wait_ge(at_ready, c - 1)
                    nc.scalar.copy(aoT[c % 2], bank[7][:, 0:P]).then_inc(aoTs_ready, 1)
                if 2 <= i <= N + 1:
                    turned(i - 2)
                if i < N:
                    exps(i)
                elif i < N + 4:
                    sums_copied(i - 4)
            ends = [0] + [act.value_load(BII[0:1, e:e + 1], min_val=e + 1, max_val=NBLK) for e in range(E)]
            meet(act, 5)
            act.wait_ge(xs_ready, 16 * NT * TOP)

            def scale_x3(g):
                if g * TG % QT == 0:
                    act.wait_ge(rstd_ready, root_no("x3", g * TG // QT))
                for t in range(g * TG, (g + 1) * TG):
                    last = A(XF[:, t, :], XN[:, t, 0:C], ACT.Identity, bias=zero_col, scale=RS[:, t:t + 1])
                last.then_inc(xf_ready, 1)

            scale_x3(0)
            for g in range(NG + 1):
                if g + 1 < NG:
                    scale_x3(g + 1)
                if g < NG:
                    act.wait_ge(xfT_ready, g + 1)
                    if g >= 2:
                        act.wait_ge(gu_ready, NF * (g - 1))
                    A(xfT[g % 2], bank[0], ACT.Identity, bias=zero_col, scale=co["w_ffn"]).then_inc(xfTs_ready, 1)
                if g >= 1:
                    for f in range(NF):
                        n = (g - 1) * NF + f
                        act.wait_ge(gu_ready, n + 1)
                        if n >= 2:
                            act.wait_ge(gu_used, n - 1)
                        A(th_t[n % 2], bank[1 + 2 * (n % 2)], ACT.Tanh, scale=0.5).then_inc(th_ready, 1)
            A(cst[:, 12:13], zero_col, ACT.Gelu)
            act.wait_ge(ff_ready, NG)
            act.sem_inc(act_ready, 1)
            for e in range(E):
                with act.Fori(ends[e], ends[e + 1]) as k:
                    act.wait_ge(dn_ready, k * BT + 1)
                    for f in range(NF):
                        act.wait_ge(up_ready, k * NF + (f + 1))
                        A(HE[:, f, :], bank[f][:, 0:BW], ACT.Gelu, bias=B1C[:, e * NF + f:e * NF + f + 1]).then_inc(act_ready, 1)

        @block.vector
        def _(dve):
            V = nc.vector
            st = Steps(dve, dve_step)

            def statistics(of, q, src, eps, eps2=None):
                sl = slice(0, 1) if of == "slots" else quarter(q)
                if of == "x":
                    dve.wait_ge(ld_x[q], 16)
                for t in range(sl.start, sl.stop):
                    st(V.bn_stats(ST[:, t, :], src[:, t, 0:C]))
                st.wait()
                for t in range(sl.start, sl.stop):
                    st(V.bn_aggr(MV[:, t, :], ST[:, t, :]))
                st.wait()
                root_input(of, q, sl, eps, eps2)

            def root_input(of, q, sl, eps, eps2=None):
                n = root_no(of, q)
                before = [i + 1 for i, (_, p) in enumerate(ROOTS[:n - 1]) if p == q]
                if before:
                    dve.wait_ge(rstd_ready, before[-1])
                m, v = MV[:, sl, 0], MV[:, sl, 1]
                if eps2 is not None:
                    ve = VE2[:, sl] if eps is not None else VE[:, sl]
                    st(V.tensor_tensor(ve, m, m, ALU.mult))
                    st.wait()
                    st(V.tensor_tensor(ve, ve, v, ALU.add))
                    st.wait()
                    last = V.tensor_scalar(ve, ve, eps2, None, ALU.add)
                    if eps is not None:
                        st(last)
                        st.wait()
                if eps is not None:
                    last = V.tensor_scalar(VE[:, sl], v, eps, None, ALU.add)
                last.then_inc(var_ready, 1)

            def first_norm(of, q, src):
                dve.wait_ge(rstd_ready, root_no(of, q))
                for t in range(q * QT, (q + 1) * QT):
                    last = V.tensor_scalar(XN[:, t, 0:C], src[:, t, 0:C], MV[:, t, 0:1], RS1[:, t:t + 1], ALU.subtract, ALU.mult)
                    if t < (q + 1) * QT - 1:
                        st(last)
                last.then_inc(xn_quarter, 1)
                dve.wait_ge(xn_quarter, q + 1 + (4 if of == "x1" else 0))

            def second_moments(of, q, eps, eps2=None):
                sl = quarter(q)
                st(V.tensor_tensor(VE2[:, sl], MV[:, sl, 1], RS1[:, sl], ALU.mult))
                st.wait()
                st(V.tensor_tensor(VE2[:, sl], VE2[:, sl], RS1[:, sl], ALU.mult))
                st.wait()
                last = V.tensor_scalar(VE[:, sl], VE2[:, sl], eps, None, ALU.add)
                if eps2 is not None:
                    st(last)
                    st.wait()
                    last = V.tensor_scalar(VE2[:, sl], VE2[:, sl], eps2, None, ALU.add)
                last.then_inc(var_ready, 1)

            def two_norms(first, second, src, eps, eps2, between=None, before=lambda q: None):
                for q in range(2):
                    before(q)
                    statistics(first, q, src, LN_EPS)
                if between:
                    between()
                for q in range(4):
                    dve.wait_ge(rstd_ready, root_no(first, q))
                    second_moments(second, q, eps, eps2)
                    first_norm(first, q, src)
                    if q + 2 < 4:
                        before(q + 2)
                        statistics(first, q + 2, src, LN_EPS)

            def constants():
                dve.wait_ge(ld_small, 16 * 7)
                dve.wait_ge(act_pre, 3)
                st(V.tensor_scalar(col_t[:, 0:1], col_t[:, 4:5], 0.5, 0.5, ALU.mult, ALU.add))
                st(V.tensor_scalar(cst[:, 0:1], co["bg"], 0.5, None, ALU.mult))
                st(V.tensor_scalar(cst[:, 1:2], co["bd"], 0.5, None, ALU.mult))
                st(V.memset(cst[:, 4:5], 0.0))
                st(V.memset(NGT_t[:, :], NEG))
                dve.wait_ge(ld_m0, 16)
                st(V.tensor_reduce(col_t[:, 5:6], m0["slotT"], AX_X, ALU.add))
                st.wait()
                st(V.tensor_scalar(col_t[:, 6:7], col_t[:, 2:3], 0.1, None, ALU.add))
                st(V.tensor_copy(DEC[:, :], col_t[:, 0:1].broadcast_to([P, GW])))
                V.tensor_scalar(col_t[:, 3:4], col_t[:, 5:6], 1.0 / SLOTS, None, ALU.mult).then_inc(col_ready, 2)
                st.wait()
                st(V.reciprocal(col_t[:, 7:8], col_t[:, 6:7]))
                st.wait()
                st(V.tensor_scalar(ro["b2"], ro["b2"], col_t[:, 7:8], None, ALU.mult))
                V.tensor_scalar(W2S[:, :], W2S[:, :], col_t[0:64, 7:8], None, ALU.mult).then_inc(col_ready, 1)
                dve.wait_ge(pre_mm, 1)
                V.tensor_tensor(B1S[:, :], B1S[:, :], bank[2][0:64, 0:1], ALU.add).then_inc(pre_ready, 1)
                dve.wait_ge(fills, 3)

            two_norms("x", "xn", ACC, LN_EPS, None, constants)

            def alpha_start(b):
                st.wait()
                sl = batch(b)
                st(V.tensor_tensor(LR[:, sl, :], LR[:, sl, :], LG[:, sl, :], ALU.not_equal))
                st.wait()
                V.tensor_tensor(LG[:, sl, :], LG[:, sl, :], V8[:, sl, 0:1].broadcast_to([P, NT // B, SLOTS]),
                                ALU.subtract).then_inc(alpha_max, 1)

            for g in range(NG + 3):
                if g == GB + 2:
                    alpha_start(0)
                if 1 <= g <= NG:
                    i = g - 1
                    b, o = i // GB, (i % GB) * GW
                    dve.wait_ge(dif_ready, i + 1)
                    if i >= 2:
                        dve.wait_ge(kvr_ready, i - 1)
                    prev = XT[:, b, o:o + GW]
                    for j, w in enumerate(("mk", "mv", "mr")):
                        last = V.scalar_tensor_tensor(out=mixed[i % 2][j], in0=dif[i % 2], scalar=co[w], in1=prev,
                                                      op0=ALU.mult, op1=ALU.add)
                    last.then_inc(mix_ready, 1)
                if 2 <= g <= NG + 1:
                    i = g - 2
                    dve.wait_ge(kvr_ready, i + 1)
                    dve.wait_ge(r_ready, i + 1)
                    if i >= 2:
                        dve.wait_ge(y_ready, i - 1)
                    if i >= 1:
                        dve.wait_ge(rw_ready, i)
                    init = 0.0 if i % GB == 0 else SS[(i - 1) % 2][:, GW - 1:GW]
                    st(V.tensor_tensor_scan(SS[i % 2], DEC[:, :], bank[4], init, ALU.mult, ALU.add))
                    st.wait()
                    st(V.scalar_tensor_tensor(out=rw[i % 2], in0=SS[i % 2], scalar=col_t[:, 1:2], in1=bank[4],
                                              op0=ALU.mult, op1=ALU.add))
                    st.wait()
                    V.tensor_tensor(rw[i % 2], rw[i % 2], bank[5], ALU.mult).then_inc(kv_used, 1)
                    dve.wait_ge(kv_used, i + 1)
                    V.scalar_tensor_tensor(out=rw[i % 2], in0=rT[i % 2], scalar=1.0, in1=rw[i % 2],
                                           op0=ALU.add, op1=ALU.mult).then_inc(rw_ready, 1)
                    dve.wait_ge(logit_ready, i + 1)
                    sl = slice(i * TG, (i + 1) * TG)
                    V.tensor_tensor(LG[:, sl, :], bank[3][:, 0:TG * SLOTS].rearrange("p (t s) -> p t s", t=TG),
                                    ro["b2"].unsqueeze(1).broadcast_to([P, TG, SLOTS]), ALU.add).then_inc(logit_used, 1)
                    dve.wait_ge(logit_used, i + 1)
                    for t in range(i * TG, (i + 1) * TG):
                        st(V.max(V8[:, t, :], LG[:, t, :]))
                    st.wait()
                    for t in range(i * TG, (i + 1) * TG):
                        st(V.match_replace(LR[:, t, :], V8[:, t, :], LG[:, t, :], NEG))
                if g >= 3:
                    i = g - 3
                    dve.wait_ge(y_ready, i + 1)
                    dve.wait_ge(xn_added, i * TG // QT + 1)
                    sl = slice(i * TG, (i + 1) * TG)
                    V.scalar_tensor_tensor(out=ACC[:, sl, :], in0=bank4[7], scalar=0.5, in1=ACC[:, sl, :],
                                           op0=ALU.mult, op1=ALU.add).then_inc(y_used, 1)
            st.wait()
            dve.wait_ge(y_used, NG)
            V.memset(cst[:, 9:10], 0.0).then_inc(phase_done, 1)
            alpha_start(1)
            for b in range(B):
                sl = batch(b)
                dve.wait_ge(alpha_exp, b + 1)
                st(V.tensor_tensor(LG[:, sl, :], LG[:, sl, :], LR[:, sl, :], ALU.mult))
                st.wait()
                st(V.tensor_reduce(rden_t[:, sl], LG[:, sl, :], AX_X, ALU.add))
                st.wait()
                st(V.reciprocal(rden_t[:, sl], rden_t[:, sl]))
                st.wait()
                V.tensor_tensor(LG[:, sl, :], LG[:, sl, :], rden_t[:, sl].unsqueeze(2).broadcast_to([P, NT // B, SLOTS]),
                                ALU.mult).then_inc(alpha_ready, 1)
            dve.wait_ge(slot_pe, 1)
            dve.wait_ge(alpha_ready, B)
            V.memset(cst[:, 11:12], 0.0).then_inc(slot_dve, 1)
            for b in range(B):
                s = slice(64 * b, 64 * b + 64)
                st(V.tensor_scalar(cst[s, 5:6], bank[b][s, C:C + 1], 1e-8, None, ALU.add))
            st.wait()
            st(V.reciprocal(cst[:, 6:7], cst[:, 5:6]))
            st.wait()
            for b in range(B):
                s = slice(64 * b, 64 * b + 64)
                last = V.tensor_scalar(si_t[s, :], bank[b][s, 0:C], cst[s, 6:7], None, ALU.mult)
                if b == 0:
                    st(last)
            last.then_inc(slot_dve, 1)
            dve.wait_ge(slot_pe, 3)
            dve.wait_ge(ld_m1, 16)
            st(V.tensor_tensor(rz_t, bank[2][:, 0:256], ro["bih"][:, 0:256], ALU.add))
            st(V.tensor_tensor(hn_t, bank[3][:, 0:P], ro["bhh"][:, 256:384], ALU.add))
            st.wait()
            V.tensor_tensor(rz_t, rz_t, ro["bhh"][:, 0:256], ALU.add).then_inc(slot_dve, 1)
            dve.wait_ge(slot_act, 2)
            st(V.tensor_scalar(rz_t, rz_t, 0.5, 0.5, ALU.mult, ALU.add))
            st.wait()
            st(V.tensor_tensor(n_t, rz_t[:, 0:P], hn_t, ALU.mult))
            st.wait()
            st(V.tensor_tensor(n_t, n_t, bank[3][:, P:2 * P], ALU.add))
            st.wait()
            V.tensor_tensor(n_t, n_t, ro["bih"][:, 256:384], ALU.add).then_inc(slot_dve, 1)
            dve.wait_ge(slot_act, 3)
            st(V.tensor_tensor(z_t, m0["slot2"], n_t, ALU.subtract))
            st.wait()
            st(V.tensor_tensor(z_t, z_t, rz_t[:, P:2 * P], ALU.mult))
            st.wait()
            V.tensor_tensor(sn_t, z_t, n_t, ALU.add).then_inc(slot_dve, 1)
            dve.wait_ge(slot_pe, 5)
            st(V.tensor_scalar(qk_t[:, 0, :], bank[5][0:32, 0:P], BQK[:, 0:1], None, ALU.add))
            st(V.tensor_scalar(qk_t[:, 1, :], bank[5][0:32, P:2 * P], BQK[:, 1:2], None, ALU.add))
            V.tensor_tensor(vv_t, bank[6][:, 0:P], ro["bv"], ALU.add).then_inc(slot_dve, 1)
            dve.wait_ge(slot_pe, 6)
            st(V.scalar_tensor_tensor(out=sc_t, in0=bank[7][:, 0:P], scalar=32 ** -0.5, in1=m1["blockneg"],
                                      op0=ALU.mult, op1=ALU.add))
            st.wait()
            V.tensor_reduce(cst[:, 2:3], sc_t, AX_X, ALU.max, negate=True).then_inc(slot_dve, 1)
            dve.wait_ge(slot_act, 5)
            st(V.reciprocal(cst[:, 7:8], cst[:, 3:4]))
            st.wait()
            V.tensor_scalar(pe_t, pe_t, cst[:, 7:8], None, ALU.mult).then_inc(slot_dve, 1)
            dve.wait_ge(slot_pe, 8)
            st(V.tensor_tensor(yy_t, sn_t, bank[6][:, P:2 * P], ALU.add))
            st.wait()
            yy3 = yy_t.unsqueeze(1)
            statistics("slots", 0, yy3, LN_EPS)
            dve.wait_ge(rstd_ready, root_no("slots", 0))
            st(V.tensor_scalar(yy_t, yy_t, MV[:, 0, 0:1], RS[:, 0:1], ALU.subtract, ALU.mult))
            st.wait()
            st(V.tensor_tensor(yy_t, yy_t, ro["ln_g"], ALU.mult))
            st.wait()
            V.tensor_tensor(yy_t, yy_t, ro["ln_b"], ALU.add).then_inc(slot_dve, 1)
            dve.wait_ge(slot_pe, 11)
            V.tensor_tensor(SVO[:, :, :], bank[0][0:64, 0:B * P].rearrange("p (b c) -> p b c", b=B),
                            ro["bo"][0:64, :].unsqueeze(1).broadcast_to([64, B, P]), ALU.add).then_inc(phase_done, 1)
            def x1_quarter(q):
                for g in range(q * QT // TG, (q + 1) * QT // TG):
                    sl = slice(g * TG, (g + 1) * TG)
                    dve.wait_ge(o_ready, g + 1)
                    V.tensor_tensor(ACC[:, sl, :], ACC[:, sl, :], bank4[1 + g % 2], ALU.add).then_inc(x1_ready, 1)
                dve.wait_ge(x1_ready, (q + 1) * QT // TG)
                if q == 3:
                    dve.wait_ge(ld_m2, 16)
                    V.tensor_scalar(BLR[:, :], m2["router"], co["rln_s"], None, ALU.mult).then_inc(col_ready, 1)
                    st(V.tensor_scalar(XL[:, :, C:C + 1], IDS[:, 0:NT].unsqueeze(2), float(-PAD_ID), None, ALU.add))

            two_norms("x1", "x1n", ACC, MOE_EPS, RMS_EPS, before=x1_quarter)
            dve.wait_ge(rstd_ready, root_no("x1n", 3))
            for t in range(NT - QT, NT):
                last = V.tensor_scalar(XL[:, t, 0:C], XN[:, t, 0:C], RS[:, t:t + 1], None, ALU.mult)
                if t % TG == TG - 1:
                    last.then_inc(xl_last, 1)
            dve.wait_ge(rl_ready, 1)
            st(V.tensor_tensor(BLT[:, :], bank[1][:, 0:E], ro["router_b"], ALU.add))
            st.wait()
            st(V.tensor_tensor(LE[:, :, :], bank[0][:, 0:NT * E].rearrange("p (t e) -> p t e", t=NT),
                               BLT[:, :].unsqueeze(1).broadcast_to([P, NT, E]), ALU.add))
            st.wait()
            for t in range(NT):
                st(V.max(V8[:, t, :], LE[:, t, :]))
            st.wait()
            for t in range(NT):
                st(V.max_index(I8[:, t, :], V8[:, t, :], LE[:, t, :]))
            st.wait()
            V.tensor_tensor(LE[:, :, :], LE[:, :, :], V8[:, :, 0:1].broadcast_to([P, NT, E]),
                            ALU.subtract).then_inc(gates_ready, 1)
            dve.wait_ge(gates_ready, 1)
            st(V.tensor_copy(V8[:, :, 0:2], I8[:, :, 0:2]))
            st.wait()
            iota = ro["iota8"].unsqueeze(1).broadcast_to([P, NT, E])
            st(V.tensor_copy(XL[:, :, C + 1:C + 2], V8[:, :, 0:1]))
            for j in range(TOP):
                st(V.tensor_tensor(OH[j][:, :, :], iota, V8[:, :, j:j + 1].broadcast_to([P, NT, E]), ALU.is_equal))
            st(V.memset(ONE[:, :], 1.0))
            st.wait()
            V.tensor_tensor(POS[:, :, :], OH[0][:, :, :], OH[1][:, :, :], ALU.add).then_inc(m_ready, 1)
            dve.wait_ge(m_ready, 1)
            dve.wait_ge(gates_ready, 2)
            st(V.tensor_tensor(GT[:, :, :], POS[:, :, :], LE[:, :, :], ALU.mult))
            st.wait()
            st(V.tensor_reduce(rden_t[:, :], GT[:, :, :], AX_X, ALU.add))
            st.wait()
            st(V.reciprocal(rden_t[:, :], rden_t[:, :]))
            st.wait()
            st(V.tensor_tensor(GT[:, :, :], GT[:, :, :], rden_t[:, :].unsqueeze(2).broadcast_to([P, NT, E]), ALU.mult))
            st.wait()
            V.memset(cst[:, 10:11], 0.0).then_inc(gt_ready, 1)
            for j in range(TOP):
                st(V.tensor_tensor(G2[:, :, :], GT[:, :, :], OH[j][:, :, :], ALU.mult))
                st.wait()
                st(V.tensor_reduce(G12[:, j, :], G2[:, :, :], AX_X, ALU.add))
                st.wait()
            dve.wait_ge(count_mm, 1)
            total = bank[0][:, 0:NT * E].rearrange("p (t e) -> p t e", t=NT)
            before = bank[1][:, 0:NT * E].rearrange("p (t e) -> p t e", t=NT)
            for e in range(E):
                st(V.tensor_tensor_scan(CUM[:, e, :], ONE[:, :], total[:, :, e], 0.0, ALU.mult, ALU.add))
            st.wait()
            nw = NTOK // BW
            st(V.tensor_tensor(CMP[:, :, :], CUM[:, :, NT - 1:NT].broadcast_to([P, E, nw]),
                               ro["iota_blk"].unsqueeze(1).broadcast_to([P, E, nw]), ALU.is_gt))
            st(V.tensor_tensor(POS[:, :, :], CUM[:, :, :].rearrange("p e t -> p t e"), total, ALU.subtract))
            st.wait()
            st(V.tensor_reduce(NBL[:, :], CMP[:, :, :], AX_X, ALU.add))
            st(V.tensor_tensor(POS[:, :, :], POS[:, :, :], before, ALU.add))
            st.wait()
            st(V.tensor_scalar(NBL[:, :], NBL[:, :], 1.0, None, ALU.max))
            st.wait()
            st(V.tensor_tensor_scan(BI[:, :], ONE[:, 0:E], NBL[:, :], 0.0, ALU.mult, ALU.add))
            st.wait()
            st(V.tensor_tensor(BS[:, :], BI[:, :], NBL[:, :], ALU.subtract))
            V.tensor_copy(BII[:, :], BI[:, :]).then_inc(ends_ready, 1)
            st.wait()
            st(V.tensor_scalar(BS[:, :], BS[:, :], float(BW), None, ALU.mult))
            st.wait()
            st(V.tensor_tensor(POS[:, :, :], POS[:, :, :], BS[:, :].unsqueeze(1).broadcast_to([P, NT, E]), ALU.add))
            st.wait()
            for j in range(TOP):
                st(V.tensor_tensor(OH[j][:, :, :], OH[j][:, :, :], POS[:, :, :], ALU.mult))
                st.wait()
                st(V.tensor_reduce(PJ[:, :, j], OH[j][:, :, :], AX_X, ALU.add))
            st.wait()
            V.tensor_copy(PJI[:, :, :], PJ[:, :, :]).then_inc(pos_ready, 1)
            for g in range(NG + 2):
                if g < NG:
                    dve.wait_ge(gate_ready, g + 1)
                    if g >= 2:
                        dve.wait_ge(hT_ready, g - 1)
                    r = g % 2
                    st(V.scalar_tensor_tensor(out=tv_t[r], in0=tg_t[r], scalar=1.0, in1=tv_t[r], op0=ALU.add, op1=ALU.mult))
                    st(V.tensor_scalar(ta_t[r], ta_t[r], 0.499, 0.5, ALU.mult, ALU.add))
                    if g >= 1:
                        dve.wait_ge(scan_ready, g)
                    st.wait()
                    init = 0.0 if g % GB == 0 else hh_t[(g - 1) % 2][:, GW - 1:GW]
                    V.tensor_tensor_scan(hh_t[r], ta_t[r], tv_t[r], init, ALU.mult, ALU.add).then_inc(scan_ready, 1)
                if 1 <= g <= NG:
                    i = g - 1
                    sl = slice(i * TG, (i + 1) * TG)
                    dve.wait_ge(hT_ready, i + 1)
                    V.scalar_tensor_tensor(out=XN[:, sl, 0:C], in0=bank4[6], scalar=0.5, in1=XN[:, sl, 0:C],
                                           op0=ALU.mult, op1=ALU.add).then_inc(hT_used, 1)
                    if g * TG % QT == 0:
                        dve.wait_ge(hT_used, g)
                        statistics("x2", g * TG // QT - 1, XN, None, RMS_EPS)
                if g >= 2:
                    i = g - 2
                    sl = slice(i * TG, (i + 1) * TG)
                    dve.wait_ge(gb_ready, i + 1)
                    V.tensor_tensor(ACC[:, sl, :], ACC[:, sl, :], bank4[i % 2], ALU.add).then_inc(gb_used, 1)
            dve.wait_ge(gb_used, NG)
            V.memset(cst[:, 9:10], 0.0).then_inc(phase_done, 1)
            for g in range(NG):
                o = 1 + 3 * (g % 2)
                for (hi, src, scale, parts, r, split) in ((q_hi, bank[o], DH ** -0.5, part[g % 2], rest[0], q_split),
                                                          (k_hi, bank[o + 1], 1.0, part2[g % 2], rest[1], k_split)):
                    dve.wait_ge(hi, g + 1)
                    if g >= 1:
                        dve.wait_ge(split, g)
                    st(V.scalar_tensor_tensor(out=r, in0=src, scalar=scale, in1=parts[0], op0=ALU.mult, op1=ALU.subtract))
                    st.wait()
                    st(V.tensor_copy(parts[1], r))
                    st.wait()
                    V.tensor_tensor(parts[2], r, parts[1], ALU.subtract).then_inc(split, 1)
            dve.wait_ge(v_copied, NG)
            dve.wait_ge(q_split, NG)
            dve.wait_ge(k_split, NG)
            V.memset(cst[:, 9:10], 0.0).then_inc(phase_done, 1)
            maskp = m2["maskprev"].bitcast(U32).unsqueeze(1).broadcast_to([P, HQ, P])
            def softmax_input(i):
                c, r = i // NQ, i % 2
                first = c % (NT // B) == 0
                dve.wait_ge(s_ready, i + 1)
                if i >= 2:
                    dve.wait_ge(p_ready, i - 1)
                prev, cur = PSQ[r][:, :, 0:P], PSQ[r][:, :, P:2 * P]
                st(V.copy_predicated(cur, maskp, NGT if first else prev))
                st.wait()
                V.tensor_reduce(NM[:, r, :], cur, AX_X, ALU.max, negate=True).then_inc(d_ready, 1)

            def v_difference(c):
                if c >= 2:
                    dve.wait_ge(pv_ready, NQ * (c - 1))
                n = max(c, 1)
                V.tensor_tensor(VD[:, c % 2, :, :], VN[:, n, :, :], VN[:, n - 1, :, :], ALU.subtract).then_inc(vd_ready, 1)

            def heads_out(c):
                dve.wait_ge(o_turned, c + 1)
                if c >= 2:
                    dve.wait_ge(aoT_ready, c - 1)
                if c >= 1:
                    dve.wait_ge(ao_ready, c)
                o3 = bank[7].rearrange("p (h d) -> p h d", h=NH)
                st(V.reciprocal(RC[:, :], o3[:, :, DH]))
                st.wait()
                V.tensor_tensor(AO[c % 2].rearrange("p (h d) -> p h d", h=NH), o3[:, :, 0:DH],
                                RC[:, :].unsqueeze(2).broadcast_to([P, NH, DH]), ALU.mult).then_inc(ao_ready, 1)

            def residual(c):
                dve.wait_ge(at_ready, c + 1)
                cols = bias_columns(c)
                if cols:
                    a, b = cols[0], cols[-1] + 1
                    st(V.tensor_tensor(B1C[:, a:b], bank[7][:, P:P + b - a], co["b1"][:, a:b], ALU.add))
                V.tensor_tensor(XN[:, c, 0:C], XN[:, c, 0:C], bank[7][:, 0:P], ALU.add).then_inc(x3_done, 1)

            def x3_statistics(c):
                dve.wait_ge(x3_done, c + 1)
                st(V.bn_stats(ST[:, c, :], XN[:, c, 0:C]))
                st.wait()
                st(V.bn_aggr(MV[:, c, :], ST[:, c, :]))
                if c % QT == QT - 1:
                    st.wait()
                    q = c // QT
                    root_input("x3", q, quarter(q), None, RMS_EPS)

            V.memset(bank[6][:, :], 0.0).then_inc(zero_bank, 1)
            for i in range(N + LAG):
                if i < N:
                    softmax_input(i)
                if i % NQ == 2 and i < N:
                    v_difference(i // NQ)
                if ends_chunk(i - LAG_SUMS):
                    heads_out((i - LAG_SUMS) // NQ)
                if ends_chunk(i - LAG_PROJ - 1):
                    residual((i - LAG_PROJ - 1) // NQ)
                if ends_chunk(i - LAG_PROJ - 2):
                    x3_statistics((i - LAG_PROJ - 2) // NQ)
            dve.wait_ge(x3_done, NT)
            V.memset(cst[:, 9:10], 0.0).then_inc(phase_done, 1)
            ends = [0] + [dve.value_load(BII[0:1, e:e + 1], min_val=e + 1, max_val=NBLK) for e in range(E)]
            def ff_add(i):
                sl = slice(i * TG, (i + 1) * TG)
                dve.wait_ge(ff_ready, i + 1)
                dve.wait_ge(x3_added, i + 1)
                V.scalar_tensor_tensor(out=ACC[:, sl, :], in0=bank4[5 + i % 2], scalar=0.5, in1=ACC[:, sl, :],
                                       op0=ALU.mult, op1=ALU.add).then_inc(ff_used, 1)

            for g in range(NG + 1):
                if g < NG:
                    for f in range(NF):
                        n = g * NF + f
                        dve.wait_ge(th_ready, n + 1)
                        if f == 0 and g >= 2:
                            dve.wait_ge(ff_ready, g - 1)
                        if n >= 2:
                            dve.wait_ge(gu_used, n - 1)
                        st(V.scalar_tensor_tensor(out=t1_t[n % 2], in0=th_t[n % 2], scalar=1.0, in1=bank[1 + 2 * (n % 2)],
                                                  op0=ALU.add, op1=ALU.mult))
                        st.wait()
                        V.tensor_tensor(hf_t[g % 2][:, f * GW:(f + 1) * GW], t1_t[n % 2], bank[2 + 2 * (n % 2)],
                                        ALU.mult).then_inc(gu_used, 1)
                if g >= 1:
                    ff_add(g - 1)
                if g < E:
                    V.tensor_scalar(MW1[:, g, :], MW1[:, g, :], co["els"][:, g:g + 1], None, ALU.mult).then_inc(w1_scaled, 1)
            dve.wait_ge(ff_used, NG)
            dve.sem_inc(y_copied, 1)
            dve.sem_inc(idx_ready, 1)
            dve.wait_ge(x_turned, 1)
            V.tensor_copy(XTS, bank[4][:, 0:BW]).then_inc(xT_ready, 1)
            V.tensor_copy(IDT[:, :, :], XI[:, :, C:XW]).then_inc(xi_used, 1)
            for e in range(E):
                with dve.Fori(ends[e], ends[e + 1]) as k:
                    dve.wait_ge(x_turned, k + 2)
                    dve.wait_ge(idx_ready, k * (3 + BT) + 1)
                    V.tensor_copy(IDN[:, :, :], XI[:, :, C:XW]).then_inc(xi_used, 1)
                    dve.wait_ge(xi_used, k + 2)
                    dve.wait_ge(up_ready, k * NF + NF)
                    V.tensor_copy(XTS, bank[4][:, 0:BW]).then_inc(xT_ready, 1)
                    V.tensor_scalar(DST[:, :, 0], IDT[:, :, 1], float(e), float(NTOK), ALU.not_equal, ALU.mult).then_inc(idx_ready, 1)
                    dve.wait_ge(idx_ready, k * (3 + BT) + 2)
                    V.tensor_tensor(DST[:, :, 1], DST[:, :, 0], IDT[:, :, 0], ALU.add).then_inc(idx_ready, 1)
                    dve.wait_ge(idx_ready, k * (3 + BT) + 3)
                    V.tensor_copy(IDT[:, :, :], IDN[:, :, :]).then_inc(idx_ready, 1)
                    for t in range(BT):
                        dve.wait_ge(y_sent[t], k * 16 + 16)
                        V.tensor_copy(DSTI[:, t:t + 1], DST[:, t:t + 1, 1]).then_inc(idx_ready, 1)
                        dve.wait_ge(dn_ready, k * BT + (t + 2))
                        V.tensor_copy(YB[t], bank[5 + t][:, 0:P]).then_inc(y_copied, 1)
            for g in range(NG):
                dve.wait_ge(y_in[g], 16 * TOP)
                for j in range(TOP):
                    for t in range(TG):
                        n = g * TG + t
                        last = V.scalar_tensor_tensor(out=ACC[:, n, :], in0=YR[g][j][:, t, :], scalar=G12[:, j, n:n + 1],
                                                      in1=ACC[:, n, :], op0=ALU.mult, op1=ALU.add)
                        if j == 0 or t < TG - 1:
                            st(last)
                    if j == 0:
                        st.wait()
                last.then_inc(out_ready, 1)


def kernel(**inp):
    import numpy as np
    import concourse.bacc as bacc
    from concourse import mybir as mb
    from concourse.bass_utils import run_bass_kernel_spmd

    def arr(name):
        return np.asarray(inp[name])

    def pack(spec, have):
        return np.ascontiguousarray(np.concatenate([have[n].reshape(have[n].shape[0], -1) for n, _ in spec], axis=1))

    a, f, t, m = "L0_attn_", "L0_ffn_", "L1_attn_", "L1_ffn_"
    slot = arr(f + "slot_init")
    w1 = arr(f + "w1")
    k, q = np.arange(P)[:, None], np.arange(P)[None, :]
    fp = np.float32
    mat0 = pack(MAT0, {"Wk": arr(a + "Wk").T, "Wv": arr(a + "Wv").T, "Wr": arr(a + "Wr").T, "Wo": arr(a + "Wo").T,
                       "w1a": w1[:C], "w1b": w1[C:], "slotT": slot.T, "slotT2": np.tile(slot.T, (1, B)),
                       "slot2": np.tile(slot, (B, 1)), "ident": np.eye(P, dtype=fp)})
    mat1 = pack(MAT1, {"Wih": arr(f + "Wih").T, "Whh": arr(f + "Whh").T, "wq": arr(f + "wq"), "wk": arr(f + "wk"),
                       "wv": arr(f + "wv"), "wvp": arr(f + "wvp"), "wo": arr(f + "wo"),
                       "blockneg": np.where(k // SLOTS == q // SLOTS, fp(0), fp(NEG))})
    wout = arr(t + "Wout").reshape(C, NF, P).transpose(2, 1, 0)
    mat2 = pack(MAT2, {"Wg": arr(t + "Wg").T, "Wv": arr(t + "Wv").T, "Wd": arr(t + "Wd").T, "Wqkv": arr(t + "Wqkv").T,
                       "Wo": arr(t + "Wo").T, "Wgate": arr(t + "Wgate").T, "Wup": arr(t + "Wup").T, "Wout": wout,
                       "maskprev": (q > k).astype(fp), "maskcur": (k <= q).astype(fp), "router": arr(m + "router_w").T,
                       "tri": (k < q).astype(fp), "ones": np.ones((P, P), fp)})
    cols = pack(COLS, {"mk": arr(a + "time_mix_k")[:, None], "mv": arr(a + "time_mix_v")[:, None],
                       "mr": arr(a + "time_mix_r")[:, None], "decay": arr(a + "time_decay")[:, None],
                       "first": arr(a + "time_first")[:, None], "ln_w": arr(a + "ln_w")[:, None],
                       "ln_b": arr(a + "ln_b")[:, None], "bvp": arr(f + "bvp")[:, None],
                       "w_mix": arr(t + "w_rms_mix")[:, None], "bg": arr(t + "bg")[:, None], "bv": arr(t + "bv")[:, None],
                       "bd": arr(t + "bd")[:, None], "w_attn": arr(t + "w_rms_attn")[:, None],
                       "w_ffn": arr(t + "w_rms_ffn")[:, None], "rln_s": arr(m + "router_ln_scale")[:, None],
                       "rln_b": arr(m + "router_ln_bias")[:, None], "els": arr(m + "expert_ln_scale").T,
                       "elb": arr(m + "expert_ln_bias").T,
                       "b1": arr(m + "b1").reshape(E, NF, P).transpose(2, 0, 1)})
    rows = np.concatenate([arr(f + "b2"), arr(f + "tau"), arr(f + "bih"), arr(f + "bhh"), arr(f + "bv"), arr(f + "ln_g"),
                           arr(f + "ln_b"), arr(f + "bo"), arr(m + "router_b"), np.arange(E, dtype=fp),
                           np.arange(NTOK // BW, dtype=fp) * fp(BW)])
    host = {
        "x": arr("L0_attn_x").reshape(NTOK, C), "mat0": mat0, "mat1": mat1, "mat2": mat2, "cols": cols, "rows": rows,
        "w2s": arr(f + "w2"), "bqk": np.stack([arr(f + "bq"), arr(f + "bk")], axis=1), "b1s": arr(f + "b1")[:, None],
        "moe_w1": arr(m + "w1").transpose(2, 0, 1), "moe_w2": arr(m + "w2").reshape(E, C, NF, P).transpose(3, 0, 2, 1),
        "moe_b2": arr(m + "b2"),
        "ids": (PAD_ID + np.arange(XTILES)[None, :] * P + np.arange(P)[:, None]).astype(fp),
    }
    nc = bacc.Bacc("TRN2", target_bir_lowering=False, num_devices=1)
    arrays, args = {}, []
    for name, v in host.items():
        v = np.ascontiguousarray(v)
        arrays[f"in_{name}"] = v
        args.append(nc.dram_tensor(f"in_{name}", v.shape, mb.dt.from_np(v.dtype), kind="ExternalInput").ap())
    out = nc.dram_tensor("out_x", (NTOK, C), F32, kind="ExternalOutput").ap()
    build(nc, *args, out)
    r = run_bass_kernel_spmd(nc, [arrays], core_ids=[0])
    return r.results[0]["out_x"].reshape(B, T, C)
```
